# Optimizing a Trainium2 kernel written in Bass

```python
import numpy as np
import jax
import jax.numpy as jnp

def _softmax(x, axis=-1):
    return jax.nn.softmax(x, axis=axis)

def _gelu(x):
    return jax.nn.gelu(x, approximate=True)

def _silu(x):
    return jax.nn.silu(x)

def _sigmoid(x):
    return jax.nn.sigmoid(x)

def _layernorm(x, axis=-1, eps=1e-05):
    m = jnp.mean(x, axis=axis, keepdims=True)
    v = jnp.var(x, axis=axis, keepdims=True)
    return (x - m) / jnp.sqrt(v + eps)

def _scatter_add(tgt, idx, src, axis=0):
    return tgt.at[idx].add(src)

def _segment_sum(src, seg, n):
    return jax.ops.segment_sum(src, seg, n)
kernel_name = 'mk_gnn_preln_d2_gnn_r8_703ef8'

def setup_inputs(seed: int=0):
    np.random.seed(seed)
    _w = jnp.asarray

    def _rec_inputs():
        import jax
        import jax.numpy as jnp
        _gk = jax.random.key(seed)
        x = -0.000124 + 1 * jax.random.normal(jax.random.fold_in(_gk, 1), (6250, 256), jnp.float32)
        _s = jax.random.randint(jax.random.fold_in(_gk, 2), (50000,), 0, 6250, jnp.int32)
        _d = jax.random.randint(jax.random.fold_in(_gk, 3), (50000,), 0, 6250, jnp.int32)
        _loop = jnp.arange(6250, dtype=jnp.int32)
        src = jnp.concatenate([_s, _d, _loop])
        dst = jnp.concatenate([_d, _s, _loop])
        _o = jnp.argsort(dst, stable=True)
        src = src[_o]
        dst = dst[_o]
        edge_weight = jax.random.uniform(jax.random.fold_in(_gk, 12), (106250,), jnp.float32, 0.0, 0.999999)
        return (x, src, dst, edge_weight)
    x, src, dst, edge_weight = _rec_inputs()

    def _L0_gnn_setup():
        import jax, jax.numpy as jnp
        import numpy as np
        N_NODES = 18870
        N_EDGES = 150000
        DIM = 256
        EPS = 1e-05

        def _layer_norm(x, g, b):
            mu = jnp.mean(x, axis=-1, keepdims=True)
            var = jnp.mean(jnp.square(x - mu), axis=-1, keepdims=True)
            return (x - mu) * jax.lax.rsqrt(var + EPS) * g + b

        def _gcn_conv(x, edge_index, edge_weight, W, b):
            n = x.shape[0]
            row, col = (edge_index[0], edge_index[1])
            loop = jnp.arange(n, dtype=row.dtype)
            row = jnp.concatenate([row, loop])
            col = jnp.concatenate([col, loop])
            ew = jnp.concatenate([edge_weight, jnp.ones((n,), dtype=x.dtype)])
            deg = jax.ops.segment_sum(ew, col, num_segments=n)
            dis = jnp.where(deg > 0, jax.lax.rsqrt(jnp.where(deg > 0, deg, 1.0)), 0.0)
            norm = dis[row] * ew * dis[col]
            h = x @ W.T
            msg = h[row] * norm[:, None]
            out = jax.ops.segment_sum(msg, col, num_segments=n)
            return out + b

        def _block(x, edge_index, edge_weight, g, bln, W, b):
            h = _layer_norm(x, g, bln)
            h = _gcn_conv(h, edge_index, edge_weight, W, b)
            h = jax.nn.relu(h)
            return x + h
        key = jax.random.key(seed)
        ks = jax.random.split(key, 8)
        s = 0.05
        return {'x': jax.random.normal(ks[0], (N_NODES, DIM), dtype=jnp.float32), 'edge_index': jax.random.randint(ks[1], (2, N_EDGES), 0, N_NODES, dtype=jnp.int64) if jax.config.jax_enable_x64 else jax.random.randint(ks[1], (2, N_EDGES), 0, N_NODES).astype(jnp.int32), 'edge_weight': jax.random.uniform(ks[2], (N_EDGES,), dtype=jnp.float32), 'ln6_g': jnp.ones((DIM,), jnp.float32), 'ln6_b': jnp.zeros((DIM,), jnp.float32), 'W6': jax.random.normal(ks[3], (DIM, DIM), jnp.float32) * s, 'b6': jnp.zeros((DIM,), jnp.float32), 'ln7_g': jnp.ones((DIM,), jnp.float32), 'ln7_b': jnp.zeros((DIM,), jnp.float32), 'W7': jax.random.normal(ks[4], (DIM, DIM), jnp.float32) * s, 'b7': jnp.zeros((DIM,), jnp.float32), 'Wp': jax.random.normal(ks[5], (DIM, DIM), jnp.float32) * s, 'bp': jnp.zeros((DIM,), jnp.float32)}
    _L0_gnn_all = _L0_gnn_setup()
    _L0_gnn_in = {k: v for k, v in _L0_gnn_all.items() if k in ('ln6_g', 'ln6_b', 'W6', 'b6', 'ln7_g', 'ln7_b', 'W7', 'b7', 'Wp', 'bp')}
    del _L0_gnn_all

    def _L1_gnn_setup():
        import jax, jax.numpy as jnp
        import numpy as np
        N = 1250
        E = 40000
        IN = 256
        H = 4
        C1 = 64
        C2 = 256

        def _segment_softmax(logits, seg, n):
            m = jax.lax.stop_gradient(jax.ops.segment_max(logits, seg, num_segments=n))
            e = jnp.exp(logits - m[seg])
            s = jax.ops.segment_sum(e, seg, num_segments=n)
            return e / (s[seg] + 1e-16)

        def _prelu(x, a):
            return jnp.where(x > 0, x, a * x)
        key = jax.random.key(seed)
        ks = jax.random.split(key, 12)
        g = lambda k, shp: jax.random.normal(k, shp, jnp.float32) * 0.05
        return {'x': jax.random.normal(ks[0], (N, IN), jnp.float32), 'edge_index': jax.random.randint(ks[1], (2, E), 0, N), 'gat_W': g(ks[2], (IN, H * C1)), 'att_src': g(ks[3], (H, C1)), 'att_dst': g(ks[4], (H, C1)), 'gat_bias': jnp.zeros((H * C1,), jnp.float32), 'prelu1_a': jnp.full((H * C1,), 0.25, jnp.float32), 'Wq': g(ks[5], (H * C1, C2)), 'bq': jnp.zeros((C2,), jnp.float32), 'Wk': g(ks[6], (H * C1, C2)), 'bk': jnp.zeros((C2,), jnp.float32), 'Wv': g(ks[7], (H * C1, C2)), 'bv': jnp.zeros((C2,), jnp.float32), 'Wskip': g(ks[8], (H * C1, C2)), 'bskip': jnp.zeros((C2,), jnp.float32), 'prelu2_a': jnp.full((C2,), 0.25, jnp.float32)}
    _L1_gnn_all = _L1_gnn_setup()
    _L1_gnn_in = {k: v for k, v in _L1_gnn_all.items() if k in ('gat_W', 'att_src', 'att_dst', 'gat_bias', 'prelu1_a', 'Wq', 'bq', 'Wk', 'bk', 'Wv', 'bv', 'Wskip', 'bskip', 'prelu2_a')}
    del _L1_gnn_all
    return {'x': x, 'src': src, 'dst': dst, 'edge_weight': edge_weight, 'L0_gnn_ln6_g': _L0_gnn_in['ln6_g'], 'L0_gnn_ln6_b': _L0_gnn_in['ln6_b'], 'L0_gnn_W6': _L0_gnn_in['W6'], 'L0_gnn_b6': _L0_gnn_in['b6'], 'L0_gnn_ln7_g': _L0_gnn_in['ln7_g'], 'L0_gnn_ln7_b': _L0_gnn_in['ln7_b'], 'L0_gnn_W7': _L0_gnn_in['W7'], 'L0_gnn_b7': _L0_gnn_in['b7'], 'L0_gnn_Wp': _L0_gnn_in['Wp'], 'L0_gnn_bp': _L0_gnn_in['bp'], 'L1_gnn_gat_W': _L1_gnn_in['gat_W'], 'L1_gnn_att_src': _L1_gnn_in['att_src'], 'L1_gnn_att_dst': _L1_gnn_in['att_dst'], 'L1_gnn_gat_bias': _L1_gnn_in['gat_bias'], 'L1_gnn_prelu1_a': _L1_gnn_in['prelu1_a'], 'L1_gnn_Wq': _L1_gnn_in['Wq'], 'L1_gnn_bq': _L1_gnn_in['bq'], 'L1_gnn_Wk': _L1_gnn_in['Wk'], 'L1_gnn_bk': _L1_gnn_in['bk'], 'L1_gnn_Wv': _L1_gnn_in['Wv'], 'L1_gnn_bv': _L1_gnn_in['bv'], 'L1_gnn_Wskip': _L1_gnn_in['Wskip'], 'L1_gnn_bskip': _L1_gnn_in['bskip'], 'L1_gnn_prelu2_a': _L1_gnn_in['prelu2_a']}

def reference(x, src, dst, edge_weight, L0_gnn_ln6_g, L0_gnn_ln6_b, L0_gnn_W6, L0_gnn_b6, L0_gnn_ln7_g, L0_gnn_ln7_b, L0_gnn_W7, L0_gnn_b7, L0_gnn_Wp, L0_gnn_bp, L1_gnn_gat_W, L1_gnn_att_src, L1_gnn_att_dst, L1_gnn_gat_bias, L1_gnn_prelu1_a, L1_gnn_Wq, L1_gnn_bq, L1_gnn_Wk, L1_gnn_bk, L1_gnn_Wv, L1_gnn_bv, L1_gnn_Wskip, L1_gnn_bskip, L1_gnn_prelu2_a):
    import jax
    import jax.numpy as jnp

    def _L0_gnn_ref(x, edge_index, edge_weight, ln6_g, ln6_b, W6, b6, ln7_g, ln7_b, W7, b7, Wp, bp):
        import jax, jax.numpy as jnp
        import numpy as np
        N_NODES = 18870
        N_EDGES = 150000
        DIM = 256
        EPS = 1e-05

        def _layer_norm(x, g, b):
            mu = jnp.mean(x, axis=-1, keepdims=True)
            var = jnp.mean(jnp.square(x - mu), axis=-1, keepdims=True)
            return (x - mu) * jax.lax.rsqrt(var + EPS) * g + b

        def _gcn_conv(x, edge_index, edge_weight, W, b):
            n = x.shape[0]
            row, col = (edge_index[0], edge_index[1])
            loop = jnp.arange(n, dtype=row.dtype)
            row = jnp.concatenate([row, loop])
            col = jnp.concatenate([col, loop])
            ew = jnp.concatenate([edge_weight, jnp.ones((n,), dtype=x.dtype)])
            deg = jax.ops.segment_sum(ew, col, num_segments=n)
            dis = jnp.where(deg > 0, jax.lax.rsqrt(jnp.where(deg > 0, deg, 1.0)), 0.0)
            norm = dis[row] * ew * dis[col]
            h = x @ W.T
            msg = h[row] * norm[:, None]
            out = jax.ops.segment_sum(msg, col, num_segments=n)
            return out + b

        def _block(x, edge_index, edge_weight, g, bln, W, b):
            h = _layer_norm(x, g, bln)
            h = _gcn_conv(h, edge_index, edge_weight, W, b)
            h = jax.nn.relu(h)
            return x + h
        x = _block(x, edge_index, edge_weight, ln6_g, ln6_b, W6, b6)
        x = _block(x, edge_index, edge_weight, ln7_g, ln7_b, W7, b7)
        return x @ Wp.T + bp

    def _L1_gnn_ref(x, edge_index, gat_W, att_src, att_dst, gat_bias, prelu1_a, Wq, bq, Wk, bk, Wv, bv, Wskip, bskip, prelu2_a):
        import jax, jax.numpy as jnp
        import numpy as np
        N = 1250
        E = 40000
        IN = 256
        H = 4
        C1 = 64
        C2 = 256

        def _segment_softmax(logits, seg, n):
            m = jax.lax.stop_gradient(jax.ops.segment_max(logits, seg, num_segments=n))
            e = jnp.exp(logits - m[seg])
            s = jax.ops.segment_sum(e, seg, num_segments=n)
            return e / (s[seg] + 1e-16)

        def _prelu(x, a):
            return jnp.where(x > 0, x, a * x)
        n = x.shape[0]
        loops = jnp.arange(n)
        src = jnp.concatenate([edge_index[0], loops])
        dst = jnp.concatenate([edge_index[1], loops])
        h = (x @ gat_W).reshape(n, H, C1)
        a_src = jnp.einsum('nhc,hc->nh', h, att_src)
        a_dst = jnp.einsum('nhc,hc->nh', h, att_dst)
        logits = jax.nn.leaky_relu(a_src[src] + a_dst[dst], negative_slope=0.2)
        alpha = _segment_softmax(logits, dst, n)
        msg = h[src] * alpha[:, :, None]
        x1 = jax.ops.segment_sum(msg, dst, num_segments=n).reshape(n, H * C1) + gat_bias
        x1 = _prelu(x1, prelu1_a)
        q = x1 @ Wq + bq
        k = x1 @ Wk + bk
        v = x1 @ Wv + bv
        s2, d2 = (edge_index[0], edge_index[1])
        scale = 1.0 / jnp.sqrt(jnp.float32(C2))
        logits2 = jnp.einsum('ec,ec->e', q[d2], k[s2]) * scale
        alpha2 = _segment_softmax(logits2, d2, n)
        out = jax.ops.segment_sum(v[s2] * alpha2[:, None], d2, num_segments=n)
        out = out + x1 @ Wskip + bskip
        return _prelu(out, prelu2_a)
    edge_index = jnp.stack([src, dst])
    h = jnp.maximum(_layernorm(x, axis=-1), 0.0)
    x = x + _L0_gnn_ref(h, edge_index, edge_weight, L0_gnn_ln6_g, L0_gnn_ln6_b, L0_gnn_W6, L0_gnn_b6, L0_gnn_ln7_g, L0_gnn_ln7_b, L0_gnn_W7, L0_gnn_b7, L0_gnn_Wp, L0_gnn_bp)
    h = jnp.maximum(_layernorm(x, axis=-1), 0.0)
    x = x + _L1_gnn_ref(h, edge_index, L1_gnn_gat_W, L1_gnn_att_src, L1_gnn_att_dst, L1_gnn_gat_bias, L1_gnn_prelu1_a, L1_gnn_Wq, L1_gnn_bq, L1_gnn_Wk, L1_gnn_bk, L1_gnn_Wv, L1_gnn_bv, L1_gnn_Wskip, L1_gnn_bskip, L1_gnn_prelu2_a)
    return x

_drawn_inputs = setup_inputs


def setup_inputs(seed=0):
    import zlib

    import numpy as np

    out = dict(_drawn_inputs(seed))
    spreads = {'L0_gnn_ln6_g': (1.0, 0.6),
     'L0_gnn_ln6_b': (0.0, 0.1),
     'L0_gnn_b6': (0.0, 0.1),
     'L0_gnn_ln7_g': (1.0, 0.6),
     'L0_gnn_ln7_b': (0.0, 0.1),
     'L0_gnn_b7': (0.0, 0.1),
     'L0_gnn_bp': (0.0, 0.1),
     'L1_gnn_gat_bias': (0.0, 0.1),
     'L1_gnn_prelu1_a': (0.25, 0.6),
     'L1_gnn_bq': (0.0, 2.0),
     'L1_gnn_bk': (0.0, 2.0),
     'L1_gnn_bv': (0.0, 0.1),
     'L1_gnn_bskip': (0.0, 0.1),
     'L1_gnn_prelu2_a': (0.25, 0.6)}
    factors = {'L1_gnn_att_src': 8.0, 'L1_gnn_att_dst': 29.269, 'L1_gnn_Wq': 21.854, 'L1_gnn_Wk': 8.0}
    for name, (base, spread) in spreads.items():
        noise = np.random.default_rng([zlib.crc32(name.encode()), seed]).standard_normal(out[name].shape)
        drawn = base * np.exp(spread * noise) if base else spread * noise
        out[name] = jnp.asarray(drawn.astype(out[name].dtype))
    for name, factor in factors.items():
        out[name] = (out[name] * factor).astype(out[name].dtype)
    return out
```

```python
from contextlib import ExitStack

import concourse.bass as bass
from concourse import mybir

F32 = mybir.dt.float32
I32 = mybir.dt.int32
ALU = mybir.AluOpType
ACT = mybir.ActivationFunctionType
P = 128
N = 6250
E = 106250
D = 256
H = 4
HC = D // H
U = 8
GE = U * P
NG = -(-E // GE)
NC = NG * U
NT = -(-N // P)
NP = NT * P
NW = NP + P
NB = 4
ROW = 260
AGW = 264
LN_EPS = 1e-5
BIG = 1.0e30
LEAD = 2
IOA = bass.IndirectOffsetOnAxis
WINDOW_FITS = "a group's windows end less than P nodes after the next group's first node"


class Shared:
    pass


class Tally:

    def __init__(self, eng, sem):
        self.eng, self.sem, self.base, self.k = eng, sem, 0, 0

    def at(self, base):
        self.base, self.k = base, 0

    def chain(self, ins):
        self.k += 1
        ins.then_inc(self.sem, 1)
        self.eng.wait_ge(self.sem, self.base + self.k)
        return ins


def semaphores(nc, c, tag):
    sems = []

    def release():
        nc.clear_and_free_semaphores(sems)
        nc.all_engine_barrier()

    def sem(name):
        sems.append(nc.alloc_semaphore(tag + name))
        return sems[-1]

    c.callback(release)
    return sem


def hold(m, eng):
    eng.sem_inc(m.held[str(eng.engine)], 1)


def load_group(nc, m, eng, g):
    return [eng.value_load(m.ctl[0:1, bass.ds(g * 3 + k, 1)], min_val=lo, max_val=hi)
            for k, lo, hi in ((0, 0, N - 1), (1, 1, NT), (2, 0, NG + NT))]


def window_start(nc, d0, i):
    return nc.s_assert_within(d0 + i * P, 0, NP - 1, skip_runtime_bounds_check_because=WINDOW_FITS)


def load_all(nc, m, a):
    with ExitStack() as c:
        sb = lambda n, s, d=F32: c.enter_context(nc.sbuf_tensor("in_" + n, s, d))
        sem = semaphores(nc, c, "in_")
        pt = c.enter_context(nc.psum_tensor("in_ps", [P, 4, 512], F32))
        dstR, nxtR = sb("dstR", [P, NC], I32), sb("nxtR", [P, NC], I32)
        hiI = sb("hiI", [P, NC], I32)
        rowsI = sb("rowsI", [NG, 3, GE], I32)
        rowsF = sb("rowsF", [NG, 3, GE])
        mks = sb("mks", [NG, 2, GE])
        d0i = sb("d0i", [1, NG + 1], I32)
        d0f = sb("d0f", [1, NG + 1])
        spn = sb("spn", [1, NG], I32)
        rem = sb("rem", [1, NG + 1], I32)
        remf = sb("remf", [1, NG + 1])
        nwf, zero, incl, bas = (sb(n, [1, NG]) for n in ("nwf", "zero", "incl", "bas"))
        gw = sb("gw", [P, 2, D])
        zrow = sb("zrow", [P, D + 1])
        gwT, att, wqT, wkb, bqc = (sb("gwT", [P, 2, D]), sb("att", [P, 2, 2 * H]), sb("wqT", [P, 2, D]),
                                   sb("wkb", [P, 2, D + 1]), sb("bqc", [P, 2]))
        s_set, s_ld, s_w, s_v, s_cast, s_pe, s_st, s_seg, s_rd = (
            sem(n) for n in ("set", "ld", "w", "v", "cast", "pe", "st", "seg", "rd"))
        block = c.enter_context(nc.Block())

        @block.gpsimd
        def _(pool):
            nc.gpsimd.memset(m.ident[:], 0.0).then_inc(s_set, 1)
            nc.gpsimd.memset(m.ones[:], 1.0)
            nc.gpsimd.memset(zrow[:], 0.0)
            nc.gpsimd.memset(m.eps[:], LN_EPS)
            nc.gpsimd.iota(m.iota[:], [[1, P]], base=0, channel_multiplier=0,
                           allow_small_or_imprecise_dtypes=True)
            nc.gpsimd.iota(m.iotap[:], [[1, 1]], base=0, channel_multiplier=1,
                           allow_small_or_imprecise_dtypes=True).then_inc(s_set, 1)
            pool.wait_ge(s_set, 2)
            nc.gpsimd.affine_select(out=m.ident[:], in_=m.ident[:], compare_op=ALU.not_equal, fill=1.0,
                                    base=0, pattern=[[-1, P]], channel_multiplier=1).then_inc(s_set, 1)

        @block.sync
        def _(sp):
            sp.dma_start(dstR[:], a["dst_cols"]).then_inc(s_ld, 16)
            sp.dma_start(nxtR[:], a["next_cols"]).then_inc(s_ld, 16)
            for k in range(3):
                sp.dma_start(rowsI[:, k, :], a["dst_flat"][k:k + NC * P].rearrange("(g e) -> g e", e=GE)).then_inc(s_ld, 16)
            with nc.allow_non_contiguous_dma(reason="first destination of each group"):
                sp.dma_start(d0i[0:1, 0:NG], a["dst_flat"][1:1 + NC * P].rearrange("(a g e) -> a g e", a=1, e=GE)[:, :, 0]).then_inc(s_ld, 16)
            sp.dma_start(m.srcI[:], a["src_cols"]).then_inc(s_w, 16)
            sp.dma_start(m.wF[:], a["w_cols"]).then_inc(s_w, 16)
            for t_, n in ((m.w6, "W6T"), (m.w7, "W7T"), (m.wp, "WpT"), (gw, "gat_W"), (gwT, "gat_WT"), (att, "att"),
                          (wqT, "WqT"), (wkb, "WkTb"), (m.wv, "Wv"), (m.wsk, "Wskip")):
                sp.dma_start(t_[:], a[n].rearrange("(k p) n -> p k n", p=P)).then_inc(s_w, 16)
            with nc.allow_non_contiguous_dma(reason="a column of biases"):
                sp.dma_start(bqc[:], a["bq"].rearrange("(k p) -> p k", p=P)).then_inc(s_w, 16)
            for k, n in enumerate(m.ROWS):
                sp.dma_start(m.rows[:, k, :], a[n].partition_broadcast(P)).then_inc(s_w, 16)
            for t_, n in ((m.bv, "bv"), (m.bsk, "bskip")):
                sp.dma_start(t_[:], a[n].rearrange("(a n) -> a n", a=1)).then_inc(s_w, 16)
            sp.wait_ge(s_set, 3)
            sp.dma_start(m.ad[NP:NW, :], zrow[:, 0:H]).then_inc(s_st, 16)
            sp.dma_start(m.qk[NP:NW, :], zrow[:]).then_inc(s_st, 16)
            sp.wait_ge(s_seg, 1)
            sp.dma_start(m.masks.rearrange("k (g e) -> g k e", e=GE), mks[:]).then_inc(s_st, 16)
            sp.dma_start(m.dstf.rearrange("(g e) -> g e", e=GE), rowsF[:, 1, :]).then_inc(s_st, 16)
            sp.wait_ge(s_st, 64)
        NWL = 2 + 10 + 1 + len(m.ROWS) + 2

        @block.vector
        def _(dve):
            y = Tally(dve, s_v)
            dve.wait_ge(s_ld, 16 * 6)
            y.chain(nc.vector.tensor_copy(m.dstF[:], dstR[:]))
            nc.vector.tensor_copy(rowsF[:], rowsI[:])
            y.chain(nc.vector.tensor_tensor(m.lastE[:], dstR[:], nxtR[:], ALU.not_equal))
            y.chain(nc.vector.tensor_scalar(hiI[:], dstR[:], 7, None, ALU.arith_shift_right))
            y.chain(nc.vector.tensor_copy(m.hiF[:], hiI[:]))
            y.chain(nc.vector.scalar_tensor_tensor(m.loF[:], m.hiF[:], -float(P), m.dstF[:], ALU.mult, ALU.add))
            for k in (0, 1):
                y.chain(nc.vector.tensor_tensor(mks[:, k, :], rowsF[:, 1, :], rowsF[:, 2 * k, :], ALU.not_equal))
            y.chain(nc.vector.tensor_scalar(mks[:], mks[:], -BIG, None, ALU.mult))
            nc.vector.memset(m.ctl[0:1, 0:1], 0).then_inc(s_seg, 1)
            y.chain(nc.vector.memset(d0i[0:1, 0:1], 0))
            y.chain(nc.vector.memset(d0i[0:1, NG:NG + 1], NP - 1))
            y.chain(nc.vector.tensor_tensor(spn[:], d0i[0:1, 1:NG + 1], d0i[0:1, 0:NG], ALU.subtract))
            y.chain(nc.vector.tensor_scalar(rem[0:1, 1:NG + 1], spn[:], P - 1, None, ALU.bitwise_and))
            y.chain(nc.vector.memset(rem[0:1, 0:1], -1))
            y.chain(nc.vector.tensor_copy(remf[:], rem[:]))
            y.chain(nc.vector.tensor_scalar(spn[:], spn[:], 7, None, ALU.arith_shift_right))
            y.chain(nc.vector.tensor_scalar(nwf[:], spn[:], 1.0, None, ALU.add))
            y.chain(nc.vector.memset(zero[:], 0.0))
            y.chain(nc.vector.tensor_tensor_scan(incl[:], nwf[:], zero[:], 0.0, ALU.add, ALU.add))
            y.chain(nc.vector.tensor_tensor(bas[:], incl[:], nwf[:], ALU.subtract))
            y.chain(nc.vector.tensor_copy(d0f[:], d0i[:]))
            cv = m.ctl[0:1, :].rearrange("a (g k) -> a g k", k=3)
            y.chain(nc.vector.tensor_copy(cv[:, :, 0], d0i[0:1, 0:NG]))
            y.chain(nc.vector.tensor_copy(cv[:, :, 1], nwf[:]))
            y.chain(nc.vector.tensor_copy(cv[:, :, 2], bas[:]))
            nc.vector.memset(m.t4one[:], 1.0).then_inc(s_cast, 1)
            dve.wait_ge(s_pe, 1)
            nc.vector.tensor_copy(m.d0rep[:], pt[:, 0, 0:NG])
            nc.vector.tensor_scalar(m.rcol[:], pt[:, 1, 0:NG], m.iotap[:, 0:1], None, ALU.is_equal).then_inc(s_rd, 1)
            dve.wait_ge(s_w, 16 * NWL)
            dve.wait_ge(s_pe, 2)
            gv = m.gw[:, :, 0:H * (HC + 1)].rearrange("p k (h c) -> p k h c", h=H)
            for k in range(2):
                nc.vector.tensor_copy(gv[:, k, :, 0:HC], gw[:, k, :].rearrange("p (h c) -> p h c", h=H))
                nc.vector.tensor_copy(gv[:, k, :, HC], pt[:, 0, 16 * k:16 * k + H])
                nc.vector.tensor_copy(m.gw[:, k, H * (HC + 1):AGW], pt[:, 0, 16 * k + H:16 * k + 2 * H])
            dve.wait_ge(s_pe, 3)
            for k in range(2):
                nc.vector.tensor_scalar(m.wqk[:, k, :], pt[:, 2 + k, 0:D + 1], float(D) ** -0.5, None, ALU.mult)
            dve.wait_ge(s_pe, 4)
            y.chain(nc.vector.tensor_scalar(m.bqk[:], pt[0:1, 1, 0:D + 1], float(D) ** -0.5, None, ALU.mult))

        @block.tensor
        def _(pe):
            pe.wait_ge(s_set, 3)
            pe.wait_ge(s_cast, 1)
            nc.tensor.matmul(pt[:, 0, 0:NG], m.ones[0:1, :], d0f[0:1, 0:NG], start=True, stop=True)
            nc.tensor.matmul(pt[:, 1, 0:NG], m.ones[0:1, :], remf[0:1, 0:NG], start=True, stop=True).then_inc(s_pe, 1)
            pe.wait_ge(s_w, 16 * NWL)
            pe.wait_ge(s_rd, 1)
            for k in range(2):
                for j in range(2):
                    last = nc.tensor.matmul(pt[:, 0, 16 * k:16 * k + 2 * H], gwT[:, j, k * P:k * P + P], att[:, j, :],
                                            start=(j == 0), stop=(j == 1))
            last.then_inc(s_pe, 1)
            for k in range(2):
                for j in range(2):
                    last = nc.tensor.matmul(pt[:, 2 + k, 0:D + 1], wqT[:, j, k * P:k * P + P], wkb[:, j, :],
                                            start=(j == 0), stop=(j == 1))
            last.then_inc(s_pe, 1)
            for j in range(2):
                last = nc.tensor.matmul(pt[0:1, 1, 0:D + 1], bqc[:, j:j + 1], wkb[:, j, :], start=(j == 0), stop=(j == 1))
            last.then_inc(s_pe, 1)


def degrees(nc, m):
    with ExitStack() as c:
        sb = lambda n, s, d=F32: c.enter_context(nc.sbuf_tensor("dg_" + n, s, d))
        sem = semaphores(nc, c, "dg_")
        lo, hi = sb("lo", [P, U, P]), sb("hi", [P, U, NT])
        deg, sd, pos = sb("deg", [P, NT]), sb("sd", [P, NT]), sb("pos", [P, NT])
        zero = sb("zero", [P, P])
        ps = c.enter_context(nc.psum_tensor("dg_ps", [P, 512], F32))
        s_z, s_oh, s_mm, s_v, s_sd = (sem(n) for n in ("z", "oh", "mm", "v", "sd"))
        block = c.enter_context(nc.Block())

        @block.gpsimd
        def _(pool):
            nc.gpsimd.memset(zero[:], 0.0).then_inc(s_z, 1)

        @block.vector
        def _(dve):
            y = Tally(dve, s_v)
            with dve.Fori(0, NG) as g:
                for u in range(U):
                    dve.wait_ge(s_mm, g * U + u + 1)
                    nc.vector.tensor_scalar(lo[:, u, :], m.iota[:], m.loF[:, bass.ds(g * U + u, 1)], None, ALU.is_equal)
                    nc.vector.tensor_scalar(hi[:, u, :], m.iota[:, 0:NT], m.hiF[:, bass.ds(g * U + u, 1)],
                                            m.wF[:, bass.ds(g * U + u, 1)], ALU.is_equal, ALU.mult).then_inc(s_oh, 1)
            dve.wait_ge(s_mm, NC + U + 1)
            y.chain(nc.vector.tensor_scalar(deg[:], ps[:, 0:NT], 1.0, None, ALU.add))
            y.chain(nc.vector.tensor_scalar(pos[:], deg[:], 0.0, None, ALU.is_gt))
            y.chain(nc.vector.tensor_scalar(deg[:], deg[:], 1e-30, None, ALU.max))
            dve.wait_ge(s_sd, 1)
            y.chain(nc.vector.reciprocal(sd[:], sd[:]))
            y.chain(nc.vector.tensor_tensor(m.dis[:], sd[:], pos[:], ALU.mult))

        @block.scalar
        def _(act):
            act.wait_ge(s_v, 3)
            nc.scalar.activation(sd[:], deg[:], ACT.Sqrt).then_inc(s_sd, 1)

        @block.tensor
        def _(pe):
            pe.wait_ge(s_z, 1)
            pe.sem_inc(s_mm, U)
            nc.tensor.matmul(ps[:, 0:NT], zero[:], zero[:, 0:NT], start=True, stop=False)
            with pe.Fori(0, NG) as g:
                for u in range(U):
                    pe.wait_ge(s_oh, g * U + u + 1)
                    nc.tensor.matmul(ps[:, 0:NT], lo[:, u, :], hi[:, u, :], start=False, stop=False).then_inc(s_mm, 1)
            nc.tensor.matmul(ps[:, 0:NT], zero[:], zero[:, 0:NT], start=False, stop=True).then_inc(s_mm, 1)


def first_rows(nc, m, x):
    B = 7
    assert NT % B == 0
    with ExitStack() as c:
        sb = lambda n, s, d=F32: c.enter_context(nc.sbuf_tensor("fr_" + n, s, d))
        sem = semaphores(nc, c, "fr_")
        xb, hb, nb = sb("x", [P, B, D]), sb("h", [P, B, D]), sb("n", [P, B, D])
        st, mv, sd, r = sb("st", [P, B, 6]), sb("mv", [P, B, 2]), sb("sd", [P, B]), sb("r", [P, B])
        s_ld, s_v, s_a, s_st, s_go = (sem(n) for n in ("ld", "v", "a", "st", "go"))
        block = c.enter_context(nc.Block())
        rows = lambda t_: t_[0:NP, 0:D].rearrange("(t p) n -> p t n", p=P)
        K = 11

        @block.sync
        def _(sp):
            with sp.Fori(0, NT // B) as t:
                sp.dma_start(xb[:], rows(x)[:, bass.ds(t * B, B), :]).then_inc(s_ld, 16)
                sp.wait_ge(s_v, t * K + K)
                sp.dma_start(rows(m.h0)[:, bass.ds(t * B, B), :], hb[:]).then_inc(s_st, 16)
                sp.dma_start(rows(m.t1)[:, bass.ds(t * B, B), :], nb[:]).then_inc(s_st, 16)
                sp.wait_ge(s_st, t * 32 + 32)
                hold(m, sp)

        @block.scalar
        def _(act):
            with act.Fori(0, NT // B) as t:
                act.wait_ge(s_v, t * K + 2)
                nc.scalar.activation(sd[:], mv[:, :, 1], ACT.Sqrt, bias=m.eps[:, 0:1]).then_inc(s_a, 1)
                act.wait_ge(s_v, t * K + 4)
                nc.scalar.activation(hb[:], hb[:], ACT.Relu).then_inc(s_a, 1)
                act.wait_ge(s_v, t * K + 6)
                nc.scalar.activation(sd[:], mv[:, :, 1], ACT.Sqrt, bias=m.eps[:, 0:1]).then_inc(s_a, 1)

        @block.vector
        def _(dve):
            y = Tally(dve, s_v)
            with dve.Fori(0, NT // B) as t:
                y.at(t * K)
                dve.wait_ge(s_ld, t * 16 + 16)
                for part in (0, 1):
                    src = (xb, hb)[part]
                    for j in range(B):
                        last = nc.vector.bn_stats(st[:, j, :], src[:, j, :])
                    y.chain(last)
                    hold(m, dve)
                    for j in range(B):
                        last = nc.vector.bn_aggr(mv[:, j, :], st[:, j, :])
                    y.chain(last)
                    dve.wait_ge(s_a, t * 3 + (1, 3)[part])
                    y.chain(nc.vector.reciprocal(r[:], sd[:]))
                    if part == 1:
                        y.chain(nc.vector.tensor_tensor(r[:], r[:], m.dis[:, bass.ds(t * B, B)], ALU.mult))
                    for j in range(B):
                        last = nc.vector.tensor_scalar((hb, nb)[part][:, j, :], src[:, j, :], mv[:, j, 0:1], r[:, j:j + 1],
                                                       ALU.subtract, ALU.mult)
                    y.chain(last)
                    if part == 0:
                        dve.wait_ge(s_a, t * 3 + 2)
                y.chain(nc.vector.tensor_tensor(nb[:], nb[:], m.row("g6").unsqueeze(1).broadcast_to([P, B, D]), ALU.mult))
                for j in range(B):
                    last = nc.vector.scalar_tensor_tensor(nb[:, j, :], m.row("c6"), m.dis[:, bass.ds(t * B + j, 1)], nb[:, j, :],
                                                          ALU.mult, ALU.add)
                y.k += 1
                assert y.k == K, y.k
                last.then_inc(s_v, 1)
                dve.wait_ge(s_v, t * K + K)
                dve.wait_ge(s_st, t * 32 + 32)


def feed_indices(nc, m, sp, g, b, cur, s_cur, s_done):
    sp.wait_ge(s_done, g + 1)
    sp.dma_start(cur[:, b, :], m.srcI[:, bass.ds(g * U, U)]).then_inc(s_cur[b], 16)


def gather_rows(nc, pool, cur, G, width, table, s_cur, s_g, s_gate):
    with pool.Fori(0, NG // NB) as t:
        for b in range(NB):
            pool.wait_ge(s_cur[b], 16 * t + 16)
            pool.sem_inc(s_gate, 1)
            for u in range(U):
                pool.indirect_dma_start(G[:, b, u, 0:width], None, table,
                                        IOA(ap=cur[:, b, u:u + 1], axis=0)).then_inc(s_g[b], 16)


def store_windows(nc, m, act, d0, nwin, base, width, ps, stage, s_ohu, s_st, s_ev, s_gate):
    with act.Fori(0, nwin) as i:
        act.wait_ge(s_ohu, (base + i + 2) * U)
        act.wait_ge(s_st, (base + i) * 16 + 16)
        nc.scalar.activation(stage[:, 0:width], ps[:, 0:width], ACT.Copy).then_inc(s_ev, 1)
        act.wait_ge(s_ev, base + i + 2)
        act.dma_start(m.agg[bass.ds(window_start(nc, d0, i), P), 0:width], stage[:, 0:width]).then_inc(s_st, 16)


def gcn_pass(nc, m, tag, table):
    with ExitStack() as c:
        sb = lambda n, s, d=F32: c.enter_context(nc.sbuf_tensor(tag + n, s, d))
        sem = semaphores(nc, c, tag)
        G, cur = sb("G", [P, NB, U, D]), sb("cur", [P, NB, U], I32)
        rel, oh = sb("rel", [P, U]), sb("oh", [P, U, P])
        S, scol, stage = sb("S", [P, P]), sb("scol", [P, 1]), sb("stage", [P, D])
        ps = c.enter_context(nc.psum_tensor(tag + "ps", [P, 512], F32))
        s_cur = [sem(f"cur{b}") for b in range(NB)]
        s_g = [sem(f"gath{b}") for b in range(NB)]
        s_zero, s_rel, s_oh, s_ohu, s_S, s_y, s_ev, s_st, s_done, s_gate, s_pgate, s_agate = (
            sem(n) for n in ("zero", "rel", "oh", "ohu", "S", "y", "ev", "st", "done", "gate", "pgate", "agate"))
        block = c.enter_context(nc.Block())

        @block.sync
        def _(sp):
            with sp.Fori(0, NG // NB) as t:
                for b in range(NB):
                    feed_indices(nc, m, sp, t * NB + b, b, cur, s_cur, s_done)

        @block.gpsimd
        def _(pool):
            nc.gpsimd.memset(S[:], 0.0)
            nc.gpsimd.memset(stage[:], 0.0).then_inc(s_zero, 1)
            gather_rows(nc, pool, cur, G, D, table, s_cur, s_g, s_gate)

        @block.vector
        def _(dve):
            dve.wait_ge(s_zero, 1)
            dve.sem_inc(s_rel, 1)
            dve.sem_inc(s_y, 1)
            with dve.Fori(0, NG) as g:
                _, nwin, base = load_group(nc, m, dve, g)
                dve.wait_ge(s_rel, g + base + 1)
                nc.vector.tensor_scalar(rel[:], m.dstF[:, bass.ds(g * U, U)], m.d0rep[:, bass.ds(g, 1)],
                                        None, ALU.subtract).then_inc(s_rel, 1)
                dve.wait_ge(s_y, g + base + 1)
                nc.vector.tensor_copy(scol[:], m.rcol[:, bass.ds(g, 1)]).then_inc(s_y, 1)
                hold(m, dve)
                with dve.Fori(0, nwin) as i:
                    dve.wait_ge(s_rel, g + base + i + 2)
                    for u in range(U):
                        dve.wait_ge(s_ohu, (base + i) * U + u + 1)
                        nc.vector.tensor_scalar(oh[:, u, :], m.iota[:], rel[:, u:u + 1],
                                                m.wF[:, bass.ds(g * U + u, 1)],
                                                ALU.is_equal, ALU.mult).then_inc(s_oh, 1)
                    dve.wait_ge(s_ohu, (base + i + 1) * U)
                    dve.wait_ge(s_y, g + base + i + 2)
                    nc.vector.tensor_copy(S[:, 0:1], scol[:]).then_inc(s_S, 1)
                    dve.wait_ge(s_S, base + i + 1)
                    nc.vector.memset(scol[:], 0.0).then_inc(s_y, 1)
                    dve.wait_ge(s_oh, (base + i + 1) * U)
                    nc.vector.tensor_scalar(rel[:], rel[:], float(P), None, ALU.subtract).then_inc(s_rel, 1)

        @block.tensor
        def _(pe):
            pe.sem_inc(s_ohu, U)
            with pe.Fori(0, NG // NB) as t:
                for b in range(NB):
                    _, nwin, base = load_group(nc, m, pe, t * NB + b)
                    pe.wait_ge(s_g[b], 16 * U * t + 16 * U)
                    pe.sem_inc(s_pgate, 1)
                    with pe.Fori(0, nwin) as i:
                        pe.wait_ge(s_ev, base + i + 1)
                        for u in range(U):
                            if u == U - 1:
                                pe.wait_ge(s_S, base + i + 1)
                                nc.tensor.matmul(ps[:, 0:D], S[:], stage[:], start=False, stop=False)
                            pe.wait_ge(s_oh, (base + i) * U + u + 1)
                            nc.tensor.matmul(ps[:, 0:D], oh[:, u, :], G[:, b, u, :],
                                             start=(u == 0), stop=(u == U - 1)).then_inc(s_ohu, 1)

        @block.scalar
        def _(act):
            act.sem_inc(s_ev, 1)
            act.sem_inc(s_done, NB)
            act.sem_inc(s_st, 16)
            with act.Fori(0, NG) as g:
                d0, nwin, base = load_group(nc, m, act, g)
                store_windows(nc, m, act, d0, nwin, base, D, ps, stage, s_ohu, s_st, s_ev, s_agate)
                act.wait_ge(s_ohu, (base + nwin + 1) * U)
                act.sem_inc(s_done, 1)
            _, nwin, base = load_group(nc, m, act, NG - 1)
            act.wait_ge(s_st, (base + nwin) * 16 + 16)
            act.sem_inc(s_agate, 1)


def softmax_pass(nc, m, tag, table, win_table, gat):
    HH = H if gat else 1
    WW = H if gat else D + 1
    AW = AGW if gat else D + 1
    SW = HC + 1 if gat else D + 1
    MA = 1 if gat else U
    KA, KW = (9 if gat else 8), 3
    KC, KX = (5 if gat else 3), 3
    with ExitStack() as c:
        sb = lambda n, s, d=F32: c.enter_context(nc.sbuf_tensor(tag + n, s, d))
        sem = semaphores(nc, c, tag)
        psb = lambda n, s: c.enter_context(nc.psum_tensor(tag + n, s, F32))
        G, cur = sb("G", [P, NB, U, ROW]), sb("cur", [P, NB, U], I32)
        Gp = sb("Gp", [P, U, AGW])
        dB, ohT = sb("dB", [P, GE]), sb("ohT", [P, GE])
        win = sb("win", [P, WW])
        wpos = sb("wpos", [P, 1])
        mk = sb("mk", [HH, 2, GE])
        L, Lp, p, z = (sb(n, [P, U, HH]) for n in ("L", "Lp", "p", "z"))
        F, M = sb("F", [HH, GE]), sb("M", [HH, GE])
        carry, dif, fac, dg = sb("carry", [HH, 1]), sb("dif", [HH, 1]), sb("fac", [HH, 1]), sb("dg", [HH, HH])
        junk = sb("junk", [P, D + 1])
        rel, oh = sb("rel", [P, U]), sb("oh", [P, U, P])
        S, scol, stage = sb("S", [P, HH, P]), sb("scol", [P, HH]), sb("stage", [P, AW])
        psA, psL = psb("psA", [P, 2, 512]), psb("psL", [HH, GE])
        psM, psF, ps = psb("psM", [P, 512]), psb("psF", [P, 512]), psb("ps", [P, 512])
        s_cur = [sem(f"cur{b}") for b in range(NB)]
        s_g = [sem(f"gath{b}") for b in range(NB)]
        (s_zero, s_db, s_mk, s_win, s_free, s_ya, s_yc, s_oht, s_pa, s_pu, s_L, s_lt, s_M, s_mb, s_z, s_p, s_fac, s_dg, s_f,
         s_gp, s_oh, s_ohu, s_S, s_ev, s_st, s_done, s_gate, s_pgate, s_agate) = (sem(n) for n in (
             "zero", "db", "mk", "win", "free", "ya", "yc", "oht", "pa", "pu", "L", "lt", "M", "mb", "z", "p", "fac", "dg",
             "f", "gp", "oh", "ohu", "S", "ev", "st", "done", "gate", "pgate", "agate"))
        block = c.enter_context(nc.Block())
        heads = lambda t_: t_.rearrange("p u (h c) -> p u h c", h=H)

        @block.sync
        def _(sp):
            for b in range(LEAD):
                feed_indices(nc, m, sp, b, b, cur, s_cur, s_done)
            with sp.Fori(0, NG // NB) as t:
                for b in range(NB):
                    g = t * NB + b
                    feed_indices(nc, m, sp, g + LEAD, (b + LEAD) % NB, cur, s_cur, s_done)
                    d0, nwin, base = load_group(nc, m, sp, g)
                    sp.wait_ge(s_free, g + 1)
                    sp.dma_start(dB[:], m.dstf[bass.ds(g * GE, GE)].partition_broadcast(P)).then_inc(s_db, 16)
                    sp.dma_start(mk[:], m.masks[:, bass.ds(g * GE, GE)].partition_broadcast(HH)).then_inc(s_mk, 16)
                    with sp.Fori(0, nwin) as i:
                        sp.wait_ge(s_pa, (base + i) * MA + 1)
                        hold(m, sp)
                        sp.dma_start(win[:], win_table[bass.ds(window_start(nc, d0, i), P), 0:WW]).then_inc(s_win, 16)
            for b in range(LEAD):
                sp.wait_ge(s_cur[b], 16 * (NG // NB + 1))

        @block.gpsimd
        def _(pool):
            nc.gpsimd.memset(carry[:], -BIG)
            nc.gpsimd.memset(S[:], 0.0)
            nc.gpsimd.memset(stage[:], 0.0).then_inc(s_zero, 1)
            gather_rows(nc, pool, cur, G, ROW, table, s_cur, s_g, s_gate)

        @block.vector
        def _(dve):
            ya, yc = Tally(dve, s_ya), Tally(dve, s_yc)
            dve.wait_ge(s_zero, 1)
            dve.sem_inc(s_free, 1)
            dve.sem_inc(s_pu, 2)
            with dve.Fori(0, NG // NB) as t:
                for b in range(NB):
                    g = t * NB + b
                    _, nwin, base = load_group(nc, m, dve, g)
                    dve.wait_ge(s_g[b], 16 * U * t + 16 * U)
                    ya.at(g * KA + base * KW)
                    if gat:
                        ya.chain(nc.vector.tensor_copy(L[:], heads(G[:, b, :, :])[:, :, :, HC]))
                    else:
                        ya.chain(nc.vector.memset(L[:], 0.0))
                    ya.chain(nc.vector.tensor_tensor(wpos[:], m.iotap[:], m.d0rep[:, bass.ds(g, 1)], ALU.add))
                    dve.wait_ge(s_db, g * 16 + 16)
                    hold(m, dve)
                    with dve.Fori(0, nwin) as i:
                        ya.at(g * KA + 2 + (base + i) * KW)
                        dve.wait_ge(s_pa, (base + i) * MA + 1)
                        ya.chain(nc.vector.tensor_scalar(ohT[:], dB[:], wpos[:, 0:1], None, ALU.is_equal))
                        dve.sem_inc(s_oht, 1)
                        ya.chain(nc.vector.tensor_scalar(wpos[:], wpos[:], float(P), None, ALU.add))
                        if gat:
                            dve.wait_ge(s_pa, base + i + 2)
                            ya.chain(nc.vector.tensor_tensor(L[:], L[:], psA[:, 0, 0:U * H].rearrange("p (u h) -> p u h", h=H), ALU.add))
                        else:
                            for u in range(U):
                                dve.wait_ge(s_pa, (base + i) * U + u + 2)
                                if u:
                                    dve.wait_ge(s_pu, (base + i) * U + u + 2)
                                nc.vector.tensor_tensor_reduce(out=junk[:], in0=G[:, b, u, 0:D + 1], in1=psA[:, u % 2, 0:D + 1],
                                                               scale=1.0, scalar=0.0, op0=ALU.mult, op1=ALU.add,
                                                               accum_out=Lp[:, u, :]).then_inc(s_pu, 1)
                            dve.wait_ge(s_pu, (base + i + 1) * U + 2)
                            ya.chain(nc.vector.tensor_tensor(L[:], L[:], Lp[:], ALU.add))
                    ya.at(g * KA + 2 + (base + nwin) * KW)
                    if gat:
                        ya.chain(nc.vector.scalar_tensor_tensor(L[:], L[:], 0.2, L[:], ALU.mult, ALU.max))
                    ya.chain(nc.vector.tensor_copy(z[:], L[:]))
                    dve.sem_inc(s_L, 1)
                    dve.wait_ge(s_lt, g + 1)
                    dve.wait_ge(s_mk, g * 16 + 16)
                    ya.chain(nc.vector.tensor_tensor_scan(F[:], mk[:, 0, :], psL[:], carry[:, 0:1], ALU.add, ALU.max))
                    ya.chain(nc.vector.tensor_tensor_scan(M[:, ::-1], mk[:, 1, ::-1], F[:, ::-1], -BIG, ALU.add, ALU.max))
                    ya.chain(nc.vector.tensor_scalar(dif[:], carry[:], M[:, 0:1], 0.0, ALU.subtract, ALU.min))
                    dve.sem_inc(s_M, 1)
                    ya.chain(nc.vector.tensor_copy(carry[:], M[:, GE - 1:GE]))
                    dve.wait_ge(s_mb, g + 1)
                    mxs = psM[:, 0:U * HH].rearrange("p (u h) -> p u h", h=HH)
                    ya.chain(nc.vector.tensor_tensor(z[:], z[:], mxs, ALU.subtract))
                    dve.sem_inc(s_z, 1)
                    dve.sem_inc(s_free, 1)
                    assert ya.k == KA - 2, ya.k
                    yc.at(g * KC + base * KX)
                    dve.wait_ge(s_ohu, (base + 1) * U)
                    if gat:
                        yc.chain(nc.vector.tensor_tensor(Gp[:, :, H * SW:AW], mxs,
                                                         m.lastE[:, bass.ds(g * U, U)].unsqueeze(2).broadcast_to([P, U, H]), ALU.mult))
                        dve.wait_ge(s_p, g + 1)
                        pw = heads(Gp[:, :, 0:H * SW])
                        nc.vector.tensor_copy(pw[:, :, :, HC], p[:])
                        yc.chain(nc.vector.tensor_tensor(pw[:, :, :, 0:HC], heads(G[:, b, :, :])[:, :, :, 0:HC],
                                                         p[:].unsqueeze(3).broadcast_to([P, U, H, HC]), ALU.mult))
                        dve.sem_inc(s_gp, 1)
                    dve.wait_ge(s_fac, g + 1)
                    yc.chain(nc.vector.tensor_scalar(dg[:], m.ident[0:HH, 0:HH], fac[:, 0:1], None, ALU.mult))
                    dve.sem_inc(s_dg, 1)
                    dve.wait_ge(s_f, g + 1)
                    yc.chain(nc.vector.tensor_scalar(scol[:], psF[:, 0:HH], m.rcol[:, bass.ds(g, 1)], None, ALU.mult))
                    yc.chain(nc.vector.tensor_scalar(rel[:], m.dstF[:, bass.ds(g * U, U)], m.d0rep[:, bass.ds(g, 1)],
                                                     None, ALU.subtract))
                    k0 = yc.k
                    assert k0 == KC, k0
                    if not gat:
                        dve.wait_ge(s_p, g + 1)
                    hold(m, dve)
                    with dve.Fori(0, nwin) as i:
                        yc.at(g * KC + k0 + (base + i) * KX)
                        for u in range(U):
                            dve.wait_ge(s_ohu, (base + i) * U + u + 1)
                            if gat:
                                nc.vector.tensor_scalar(oh[:, u, :], m.iota[:], rel[:, u:u + 1], None, ALU.is_equal).then_inc(s_oh, 1)
                            else:
                                nc.vector.tensor_scalar(oh[:, u, :], m.iota[:], rel[:, u:u + 1], p[:, u, 0:1],
                                                        ALU.is_equal, ALU.mult).then_inc(s_oh, 1)
                        dve.wait_ge(s_ohu, (base + i + 1) * U)
                        yc.chain(nc.vector.tensor_copy(S[:, :, 0], scol[:]))
                        dve.sem_inc(s_S, 1)
                        yc.chain(nc.vector.memset(scol[:], 0.0))
                        dve.wait_ge(s_oh, (base + i + 1) * U)
                        yc.chain(nc.vector.tensor_scalar(rel[:], rel[:], float(P), None, ALU.subtract))
                        assert yc.k == KX

        @block.tensor
        def _(pe):
            pe.sem_inc(s_pa, 1)
            pe.sem_inc(s_ohu, U)
            with pe.Fori(0, NG // NB) as t:
                for b in range(NB):
                    g = t * NB + b
                    _, nwin, base = load_group(nc, m, pe, g)
                    with pe.Fori(0, nwin) as i:
                        pe.wait_ge(s_win, (base + i) * 16 + 16)
                        pe.wait_ge(s_oht, base + i + 1)
                        for u in range(U):
                            if gat:
                                last = nc.tensor.matmul(psA[:, 0, u * H:u * H + H], ohT[:, u * P:u * P + P], win[:], start=True, stop=True)
                            else:
                                pe.wait_ge(s_pu, (base + i) * U + u + 1)
                                nc.tensor.matmul(psA[:, u % 2, 0:WW], ohT[:, u * P:u * P + P], win[:],
                                                 start=True, stop=True).then_inc(s_pa, 1)
                        if gat:
                            last.then_inc(s_pa, 1)
                    pe.wait_ge(s_L, g + 1)
                    for u in range(U):
                        last = nc.tensor.transpose(psL[:, u * P:u * P + P], L[:, u, :], m.ident[:])
                    last.then_inc(s_lt, 1)
                    pe.wait_ge(s_M, g + 1)
                    hold(m, pe)
                    for u in range(U):
                        last = nc.tensor.transpose(psM[:, u * HH:u * HH + HH], M[:, u * P:u * P + P], m.ident[0:HH, 0:HH])
                    last.then_inc(s_mb, 1)
                    pe.wait_ge(s_dg, g + 1)
                    nc.tensor.matmul(psF[:, 0:HH], m.ones[0:HH, :], dg[:], start=True, stop=True).then_inc(s_f, 1)
                    if gat:
                        pe.wait_ge(s_gp, g + 1)
                    else:
                        pe.wait_ge(s_g[b], 16 * U * t + 16 * U)
                    pe.sem_inc(s_pgate, 1)
                    with pe.Fori(0, nwin) as i:
                        pe.wait_ge(s_ev, base + i + 1)
                        for u in range(U):
                            if u == U - 1:
                                pe.wait_ge(s_S, base + i + 1)
                                for h in range(HH):
                                    nc.tensor.matmul(ps[:, h * SW:h * SW + SW], S[:, h, :], stage[:, h * SW:h * SW + SW],
                                                     start=False, stop=False)
                            pe.wait_ge(s_oh, (base + i) * U + u + 1)
                            rhs = Gp[:, u, :] if gat else G[:, b, u, 0:AW]
                            nc.tensor.matmul(ps[:, 0:AW], oh[:, u, :], rhs, start=(u == 0), stop=(u == U - 1)).then_inc(s_ohu, 1)

        @block.scalar
        def _(act):
            act.sem_inc(s_ev, 1)
            act.sem_inc(s_done, NB)
            act.sem_inc(s_st, 16)
            with act.Fori(0, NG) as g:
                d0, nwin, base = load_group(nc, m, act, g)
                act.wait_ge(s_M, g + 1)
                nc.scalar.activation(fac[:], dif[:], ACT.Exp).then_inc(s_fac, 1)
                act.wait_ge(s_z, g + 1)
                nc.scalar.activation(p[:], z[:], ACT.Exp).then_inc(s_p, 1)
                store_windows(nc, m, act, d0, nwin, base, AW, ps, stage, s_ohu, s_st, s_ev, s_agate)
                act.wait_ge(s_ohu, (base + nwin + 1) * U)
                act.sem_inc(s_done, 1)
            _, nwin, base = load_group(nc, m, act, NG - 1)
            act.wait_ge(s_st, (base + nwin) * 16 + 16)
            act.sem_inc(s_agate, 1)


def node_phase(nc, m, tag, body):
    with ExitStack() as c:
        sb = lambda n, s, d=F32: c.enter_context(nc.sbuf_tensor(tag + n, s, d))
        sem = semaphores(nc, c, tag)
        psb = lambda n, s: c.enter_context(nc.psum_tensor(tag + n, s, F32))
        parts = body(nc, m, sb, sem, psb)
        block = c.enter_context(nc.Block())

        @block.sync
        def _(sp):
            with sp.Fori(0, NT) as t:
                parts["sp"](sp, t)

        @block.scalar
        def _(act):
            with act.Fori(0, NT) as t:
                parts["act"](act, t)

        @block.vector
        def _(dve):
            with dve.Fori(0, NT) as t:
                parts["dve"](dve, t)

        @block.tensor
        def _(pe):
            with pe.Fori(0, NT) as t:
                parts["pe"](pe, t)


def tile(table, t, width=D, at=0):
    return table[bass.ds(t * P, P), at:at + width]


def two_transposes(nc, m, psT, src):
    for k in range(2):
        last = nc.tensor.transpose(psT[:, k * P:k * P + P], src[:, k * P:k * P + P], m.ident[:])
    return last


def products(nc, m, pe, act, t, s, psT, psO, lt, rounds):
    R = len(rounds)
    for j, (src, rhs, n) in enumerate(rounds):
        if pe is not None:
            pe.wait_ge(s.ready, t * R + j + 1)
            for k in range(2):
                last = nc.tensor.transpose(psT[:, k * P:k * P + P], src[:, k * P:k * P + P], m.ident[:])
            last.then_inc(s.turned, 1)
            pe.wait_ge(s.copied, t * R + j + 1)
            for k in range(2):
                last = nc.tensor.matmul(psO[:, 0:n], lt[:, k * P:k * P + P], rhs[:, k, 0:n], start=(k == 0), stop=(k == 1))
            last.then_inc(s.product, 1)
        else:
            act.wait_ge(s.turned, t * R + j + 1)
            nc.scalar.activation(lt[:], psT[:, 0:D], ACT.Copy).then_inc(s.copied, 1)


def gcn_nodes(layer):
    def body(nc, m, sb, sem, psb):
        ag, tt_, res, o1, o2 = (sb(n, [P, D]) for n in ("ag", "tt", "res", "o1", "o2"))
        xin, hb, nb, lt = (sb(n, [P, D]) for n in ("xin", "hb", "nb", "lt"))
        t3 = sb("t3", [P, AGW])
        st, mv, sd, r = sb("st", [P, 6]), sb("mv", [P, 2]), sb("sd", [P, 1]), sb("r", [P, 1])
        psT, psO = psb("psT", [P, 512]), psb("psO", [P, 512])
        s = Shared()
        s.loaded, s.stored, s.chained, s.ready, s.turned = (sem(n) for n in ("loaded", "stored", "chained", "ready", "turned"))
        s.copied, s.product, s.variance, s.deviation, s.result = (
            sem(n) for n in ("copied", "product", "variance", "deviation", "result"))
        w = m.w6 if layer == 1 else m.w7
        table, resid = (m.t1, m.h0) if layer == 1 else (m.t2, m.x1)
        bias = m.row("b6" if layer == 1 else "b7")
        rounds = [(ag, w, D)] if layer == 1 else [(ag, w, D), (o1, m.wp, D), (hb, m.gw, AGW)]
        R = len(rounds)
        KV = 10

        def sp_part(sp, t):
            loads = [(ag, m.agg), (tt_, table), (res, resid)] + ([(xin, m.x)] if layer == 2 else [])
            for to, fr in loads:
                sp.dma_start(to[:], tile(fr, t)).then_inc(s.loaded, 16)
            sp.wait_ge(s.result, t + 1)
            if layer == 1:
                sp.dma_start(tile(m.x1, t), o1[:]).then_inc(s.stored, 16)
                sp.dma_start(tile(m.t2, t), o2[:]).then_inc(s.stored, 16)
                sp.wait_ge(s.stored, t * 32 + 32)
                hold(m, sp)
            else:
                sp.dma_start(tile(m.xa, t), o2[:]).then_inc(s.stored, 16)
                sp.dma_start(tile(m.t3, t, ROW), t3[:, 0:ROW]).then_inc(s.stored, 16)
                sp.dma_start(tile(m.ad, t, H), t3[:, ROW:AGW]).then_inc(s.stored, 16)
                sp.wait_ge(s.stored, t * 48 + 48)
                hold(m, sp)

        def dve_part(dve, t):
            y = Tally(dve, s.chained)
            y.at(t * KV)
            dve.wait_ge(s.loaded, t * (48 if layer == 1 else 64) + (48 if layer == 1 else 64))
            y.chain(nc.vector.tensor_tensor(ag[:], ag[:], tt_[:], ALU.add))
            dve.sem_inc(s.ready, 1)
            dve.wait_ge(s.product, t * R + 1)
            y.chain(nc.vector.scalar_tensor_tensor(o1[:], psO[:, 0:D], m.dis[:, bass.ds(t, 1)], bias, ALU.mult, ALU.add))
            y.chain(nc.vector.scalar_tensor_tensor(o1[:], o1[:], 0.0, res[:], ALU.max, ALU.add))
            if layer == 2:
                dve.sem_inc(s.ready, 1)
            src = o1
            if layer == 2:
                dve.wait_ge(s.product, t * R + 2)
                y.chain(nc.vector.tensor_tensor(o2[:], psO[:, 0:D], m.row("bp"), ALU.add))
                y.chain(nc.vector.tensor_tensor(o2[:], o2[:], xin[:], ALU.add))
                src = o2
            y.chain(nc.vector.bn_stats(st[:], src[:]))
            hold(m, dve)
            y.chain(nc.vector.bn_aggr(mv[:], st[:]))
            dve.sem_inc(s.variance, 1)
            dve.wait_ge(s.deviation, t + 1)
            y.chain(nc.vector.reciprocal(r[:], sd[:]))
            if layer == 1:
                y.chain(nc.vector.tensor_tensor(r[:], r[:], m.dis[:, bass.ds(t, 1)], ALU.mult))
                y.chain(nc.vector.tensor_scalar(nb[:], o1[:], mv[:, 0:1], r[:, 0:1], ALU.subtract, ALU.mult))
                y.chain(nc.vector.tensor_tensor(nb[:], nb[:], m.row("g7"), ALU.mult))
                y.chain(nc.vector.scalar_tensor_tensor(o2[:], m.row("c7"), m.dis[:, bass.ds(t, 1)], nb[:],
                                                       ALU.mult, ALU.add))
                dve.sem_inc(s.result, 1)
            else:
                y.chain(nc.vector.tensor_scalar(nb[:], o2[:], mv[:, 0:1], r[:, 0:1], ALU.subtract, ALU.mult))
                y.chain(nc.vector.tensor_scalar(hb[:], nb[:], 0.0, None, ALU.max))
                dve.sem_inc(s.ready, 1)
            assert y.k == KV, y.k

        def pe_part(pe, t):
            products(nc, m, pe, None, t, s, psT, psO, lt, rounds)

        def act_part(act, t):
            for j in range(R):
                act.wait_ge(s.turned, t * R + j + 1)
                nc.scalar.activation(lt[:], psT[:, 0:D], ACT.Copy).then_inc(s.copied, 1)
                if j == min(1, R - 1):
                    act.wait_ge(s.variance, t + 1)
                    nc.scalar.activation(sd[:], mv[:, 1:2], ACT.Sqrt, bias=m.eps[:, 0:1]).then_inc(s.deviation, 1)
            if layer == 2:
                act.wait_ge(s.product, t * R + R)
                nc.scalar.activation(t3[:], psO[:, 0:AGW], ACT.Copy).then_inc(s.result, 1)

        return dict(sp=sp_part, dve=dve_part, pe=pe_part, act=act_part)
    return body


def gat_nodes(nc, m, sb, sem, psb):
    ag, own, ad = sb("ag", [P, AGW]), sb("own", [P, ROW]), sb("ad", [P, H])
    v, v2 = sb("v", [P, D]), sb("v2", [P, D])
    t4, lt, q = sb("t4", [P, ROW]), sb("lt", [P, D]), sb("q", [P, D + 1])
    mx, ls, m2, ab, sm, rs = (sb(n, [P, H]) for n in ("mx", "ls", "m2", "ab", "sm", "rs"))
    e = sb("e", [P, 2, H])
    psT, psO = psb("psT", [P, 512]), psb("psO", [P, 512])
    s_set, s_loaded, s_stored, s_chained, s_exps, s_exp, s_ready, s_turned, s_copied, s_product, s_q = (
        sem(n) for n in ("set", "loaded", "stored", "chained", "exps", "exp", "ready", "turned", "copied", "product", "q"))
    KV = 20
    hv = lambda t_: t_[:, 0:H * (HC + 1)].rearrange("p (h c) -> p h c", h=H)
    wide = lambda t_: t_[:].rearrange("p (h c) -> p h c", h=H)
    each = lambda t_: t_.unsqueeze(2).broadcast_to([P, H, HC])

    def sp_part(sp, t):
        for to, fr, n in ((ag, m.agg, AGW), (own, m.t3, ROW), (ad, m.ad, H)):
            sp.dma_start(to[:], tile(fr, t, n)).then_inc(s_loaded, 16)
        sp.wait_ge(s_q, t + 1)
        sp.dma_start(tile(m.t4, t, ROW), t4[:]).then_inc(s_stored, 16)
        sp.dma_start(tile(m.qk, t, D + 1), q[:]).then_inc(s_stored, 16)
        sp.wait_ge(s_stored, t * 32 + 32)
        hold(m, sp)

    def dve_part(dve, t):
        y = Tally(dve, s_chained)
        y.at(t * KV)
        dve.wait_ge(s_loaded, t * 48 + 48)
        sums = hv(ag)[:, :, HC]
        y.chain(nc.vector.tensor_scalar(mx[:], sums, 0.0, -BIG, ALU.is_equal, ALU.mult))
        y.chain(nc.vector.tensor_tensor(mx[:], mx[:], ag[:, H * (HC + 1):AGW], ALU.add))
        y.chain(nc.vector.tensor_tensor(ls[:], hv(own)[:, :, HC], ad[:], ALU.add))
        y.chain(nc.vector.scalar_tensor_tensor(ls[:], ls[:], 0.2, ls[:], ALU.mult, ALU.max))
        y.chain(nc.vector.tensor_tensor(m2[:], mx[:], ls[:], ALU.max))
        y.chain(nc.vector.tensor_tensor(e[:, 0, :], mx[:], m2[:], ALU.subtract))
        y.chain(nc.vector.tensor_tensor(e[:, 1, :], ls[:], m2[:], ALU.subtract))
        dve.sem_inc(s_exps, 1)
        dve.wait_ge(s_exp, t + 1)
        y.chain(nc.vector.tensor_tensor(ab[:], sums, e[:, 0, :], ALU.mult))
        y.chain(nc.vector.tensor_tensor(sm[:], ab[:], e[:, 1, :], ALU.add))
        y.chain(nc.vector.tensor_scalar(sm[:], sm[:], 1e-16, None, ALU.add))
        y.chain(nc.vector.reciprocal(rs[:], sm[:]))
        y.chain(nc.vector.tensor_tensor(e[:], e[:], rs[:].unsqueeze(1).broadcast_to([P, 2, H]), ALU.mult))
        y.chain(nc.vector.tensor_tensor(wide(v), hv(ag)[:, :, 0:HC], each(e[:, 0, :]), ALU.mult))
        y.chain(nc.vector.tensor_tensor(wide(v2), hv(own)[:, :, 0:HC], each(e[:, 1, :]), ALU.mult))
        y.chain(nc.vector.tensor_tensor(v[:], v[:], v2[:], ALU.add))
        y.chain(nc.vector.tensor_tensor(v[:], v[:], m.row("gat_bias"), ALU.add))
        y.chain(nc.vector.scalar_tensor_tensor(v2[:], v[:], 0.0, m.row("prelu1"), ALU.min, ALU.mult))
        y.chain(nc.vector.scalar_tensor_tensor(t4[:, 0:D], v[:], 0.0, v2[:], ALU.max, ALU.add))
        y.chain(nc.vector.memset(t4[:, D:ROW], 1.0))
        dve.sem_inc(s_ready, 1)
        y.chain(nc.vector.memset(mx[:], 0.0))
        assert y.k == KV, y.k

    def pe_part(pe, t):
        pe.wait_ge(s_ready, t + 1)
        for k in range(2):
            last = nc.tensor.transpose(psT[:, k * P:k * P + P], t4[:, k * P:k * P + P], m.ident[:])
        last.then_inc(s_turned, 1)
        pe.wait_ge(s_copied, t + 1)
        for k in range(2):
            nc.tensor.matmul(psO[:, 0:D + 1], lt[:, k * P:k * P + P], m.wqk[:, k, :], start=(k == 0), stop=False)
        nc.tensor.matmul(psO[:, 0:D + 1], m.ones[0:1, :], m.bqk[:], start=False, stop=True).then_inc(s_product, 1)

    def act_part(act, t):
        act.wait_ge(s_exps, t + 1)
        nc.scalar.activation(e[:], e[:], ACT.Exp).then_inc(s_exp, 1)
        act.wait_ge(s_turned, t + 1)
        nc.scalar.activation(lt[:], psT[:, 0:D], ACT.Copy).then_inc(s_copied, 1)
        act.wait_ge(s_product, t + 1)
        nc.scalar.activation(q[:], psO[:, 0:D + 1], ACT.Copy).then_inc(s_q, 1)

    return dict(sp=sp_part, dve=dve_part, pe=pe_part, act=act_part)


def out_nodes(nc, m, sb, sem, psb):
    ag, t4, xa = sb("ag", [P, D + 1]), sb("t4", [P, ROW]), sb("xa", [P, D])
    an, lt, sa, v, o = sb("an", [P, D + 1]), sb("lt", [P, 4, P]), sb("sa", [1, P]), sb("v", [P, D]), sb("o", [P, D])
    rs = sb("rs", [P, 1])
    psT, psS, psO = psb("psT", [P, 4, P]), psb("psS", [P, 512]), psb("psO", [P, 512])
    s_loaded, s_stored, s_chained, s_ready, s_turned, s_copied, s_product, s_out = (
        sem(n) for n in ("loaded", "stored", "chained", "ready", "turned", "copied", "product", "out"))
    KV = 6

    def sp_part(sp, t):
        for to, fr, n in ((ag, m.agg, D + 1), (t4, m.t4, ROW), (xa, m.xa, D)):
            sp.dma_start(to[:], tile(fr, t, n)).then_inc(s_loaded, 16)
        sp.wait_ge(s_out, t + 1)
        sp.dma_start(tile(m.out, t), o[:]).then_inc(s_stored, 16)
        sp.wait_ge(s_stored, t * 16 + 16)
        hold(m, sp)

    def dve_part(dve, t):
        y = Tally(dve, s_chained)
        y.at(t * KV)
        dve.wait_ge(s_loaded, t * 48 + 48)
        y.chain(nc.vector.tensor_scalar(rs[:], ag[:, D:D + 1], 1e-16, None, ALU.add))
        y.chain(nc.vector.reciprocal(rs[:], rs[:]))
        y.chain(nc.vector.tensor_scalar(an[:], ag[:], rs[:, 0:1], None, ALU.mult))
        dve.sem_inc(s_ready, 1)
        dve.wait_ge(s_product, t + 1)
        y.chain(nc.vector.scalar_tensor_tensor(v[:], psO[:, 0:D], 0.0, m.row("prelu2"), ALU.min, ALU.mult))
        y.chain(nc.vector.scalar_tensor_tensor(o[:], psO[:, 0:D], 0.0, v[:], ALU.max, ALU.add))
        y.chain(nc.vector.tensor_tensor(o[:], o[:], xa[:], ALU.add))
        dve.sem_inc(s_out, 1)
        assert y.k == KV

    def pe_part(pe, t):
        pe.wait_ge(s_ready, t + 1)
        for j, src in enumerate((an, an, t4, t4)):
            nc.tensor.transpose(psT[:, j, :], src[:, (j % 2) * P:(j % 2) * P + P], m.ident[:])
        nc.tensor.transpose(psS[0:1, 0:P], an[:, D:D + 1], m.ident[:]).then_inc(s_turned, 1)
        pe.wait_ge(s_copied, t * 2 + 2)
        for j in range(4):
            nc.tensor.matmul(psO[:, 0:D], lt[:, j, :], (m.wv, m.wsk)[j // 2][:, j % 2, :], start=(j == 0), stop=False)
        nc.tensor.matmul(psO[:, 0:D], sa[:], m.bv[:], start=False, stop=False)
        nc.tensor.matmul(psO[:, 0:D], m.ones[0:1, :], m.bsk[:], start=False, stop=True).then_inc(s_product, 1)

    def act_part(act, t):
        act.wait_ge(s_turned, t + 1)
        nc.scalar.activation(lt[:], psT[:], ACT.Copy).then_inc(s_copied, 1)
        nc.scalar.activation(sa[:], psS[0:1, 0:P], ACT.Copy).then_inc(s_copied, 1)

    return dict(sp=sp_part, dve=dve_part, pe=pe_part, act=act_part)


def build(nc, a, out):
    with ExitStack() as c:
        sb = lambda n, s, d=F32: c.enter_context(nc.sbuf_tensor(n, s, d))
        m = Shared()
        m.ROWS = ("g6", "c6", "b6", "g7", "c7", "b7", "bp", "gat_bias", "prelu1", "prelu2")
        m.ident, m.ones, m.iota = sb("ident", [P, P]), sb("ones", [P, P]), sb("iota", [P, P])
        m.iotap, m.eps, m.t4one = sb("iotap", [P, 1]), sb("eps", [P, 1]), sb("t4one", [1, 1])
        m.srcI = sb("srcI", [P, NC + LEAD * U], I32)
        m.dstF, m.wF, m.lastE, m.hiF, m.loF = (sb(n, [P, NC]) for n in ("dstF", "wF", "lastE", "hiF", "loF"))
        m.d0rep, m.rcol = sb("d0rep", [P, NG]), sb("rcol", [P, NG])
        m.ctl = sb("ctl", [1, NG * 3], I32)
        m.dis = sb("dis", [P, NT])
        m.w6, m.w7, m.wp, m.wv, m.wsk = (sb(n, [P, 2, D]) for n in ("w6", "w7", "wp", "wv", "wsk"))
        m.gw, m.wqk = sb("gw", [P, 2, AGW]), sb("wqk", [P, 2, D + 1])
        m.bqk, m.bv, m.bsk = sb("bqk", [1, D + 1]), sb("bvr", [1, D]), sb("bskr", [1, D])
        m.rows = sb("rows", [P, len(m.ROWS), D])
        m.row = lambda n: m.rows[:, m.ROWS.index(n), :]
        dram = lambda n, s: nc.dram_tensor(n, s, F32, kind="Internal").ap()
        m.x, m.out = a["x"], out
        m.h0, m.x1, m.xa, m.t1, m.t2 = (dram(n, (NP, D)) for n in ("h0", "x1", "xa", "t1", "t2"))
        m.t3, m.t4 = dram("t3", (NP, ROW)), dram("t4", (NP, ROW))
        m.ad, m.qk = dram("ad", (NW, H)), dram("qk", (NW, D + 1))
        m.agg = dram("agg", (NW, AGW))
        m.masks, m.dstf = dram("masks", (2, NC * P)), dram("dstf", (NC * P,))
        m.held = {str(e.engine): c.enter_context(nc.semaphore(f"held{k}"))
                  for k, e in enumerate((nc.sync, nc.scalar, nc.vector, nc.tensor, nc.gpsimd))}
        load_all(nc, m, a)
        degrees(nc, m)
        first_rows(nc, m, a["x"])
        gcn_pass(nc, m, "g1_", m.t1)
        node_phase(nc, m, "n1_", gcn_nodes(1))
        gcn_pass(nc, m, "g2_", m.t2)
        node_phase(nc, m, "n2_", gcn_nodes(2))
        softmax_pass(nc, m, "g3_", m.t3, m.ad, True)
        node_phase(nc, m, "n3_", gat_nodes)
        softmax_pass(nc, m, "g4_", m.t4, m.qk, False)
        node_phase(nc, m, "n4_", out_nodes)


def kernel(**inputs):
    import numpy as np
    import concourse.bacc as bacc
    from concourse.bass_utils import run_bass_kernel_spmd as run
    i = {k: np.asarray(v) for k, v in inputs.items()}
    L0 = lambda n: i["L0_gnn_" + n]
    L1 = lambda n: i["L1_gnn_" + n]
    pad = NC * P - E
    dst = np.concatenate([np.full(1, -2, np.int32), i["dst"], np.full(pad + 1, -1, np.int32)])
    src = np.concatenate([i["src"], np.zeros(pad + LEAD * GE, np.int32)])
    w = np.concatenate([i["edge_weight"], np.zeros(pad, np.float32)])
    nxt = dst[2:].copy().reshape(NG, GE)
    nxt[:, -1] = -3
    cols = lambda v: np.ascontiguousarray(v.reshape(-1, P).T)
    att = np.zeros((D, 2 * H), np.float32)
    for h in range(H):
        att[h * HC:(h + 1) * HC, h] = L1("att_src")[h]
        att[h * HC:(h + 1) * HC, H + h] = L1("att_dst")[h]
    arrays = {
        "x": np.concatenate([i["x"], np.zeros((NP - N, D), np.float32)]),
        "dst_flat": dst, "src_cols": cols(src), "dst_cols": cols(dst[1:1 + NC * P]), "next_cols": cols(nxt), "w_cols": cols(w),
        "W6T": L0("W6").T, "W7T": L0("W7").T, "WpT": L0("Wp").T,
        "gat_W": L1("gat_W"), "gat_WT": L1("gat_W").T, "att": att, "WqT": L1("Wq").T,
        "WkTb": np.concatenate([L1("Wk").T, L1("bk")[:, None]], axis=1), "Wv": L1("Wv"), "Wskip": L1("Wskip"),
        "bq": L1("bq"), "bv": L1("bv"), "bskip": L1("bskip"),
        "g6": L0("ln6_g"), "c6": L0("ln6_b"), "b6": L0("b6"), "g7": L0("ln7_g"), "c7": L0("ln7_b"), "b7": L0("b7"),
        "bp": L0("bp"), "gat_bias": L1("gat_bias"), "prelu1": L1("prelu1_a"), "prelu2": L1("prelu2_a"),
    }
    nc = bacc.Bacc("TRN2", target_bir_lowering=False, num_devices=1)
    ins = {k + "_in": np.ascontiguousarray(v) for k, v in arrays.items()}
    aps = {k[:-3]: nc.dram_tensor(k, v.shape, mybir.dt.from_np(v.dtype), kind="ExternalInput").ap() for k, v in ins.items()}
    out = nc.dram_tensor("out", (NP, D), F32, kind="ExternalOutput").ap()
    build(nc, aps, out)
    return run(nc, [ins], core_ids=[0]).results[0]["out"][:N]
```

```python
from contextlib import ExitStack

import concourse.bass as bass
from concourse import mybir

F32 = mybir.dt.float32
I32 = mybir.dt.int32
ALU = mybir.AluOpType
ACT = mybir.ActivationFunctionType
P = 128
N = 6250
E = 106250
D = 256
H = 4
HC = D // H
U = 8
GE = U * P
NG = -(-E // GE)
NC = NG * U
NT = -(-N // P)
NP = NT * P
NW = NP + P
NB = 8
NBG = 4
ROW = 260
AGW = 264
LN_EPS = 1e-5
BIG = 1.0e30
LEAD = 4
IOA = bass.IndirectOffsetOnAxis
WINDOW_FITS = "a group's windows end less than P nodes after the next group's first node"


class Shared:
    pass


class Tally:

    def __init__(self, eng, sem):
        self.eng, self.sem, self.base, self.k = eng, sem, 0, 0

    def at(self, base):
        self.base, self.k = base, 0

    def chain(self, ins):
        self.k += 1
        ins.then_inc(self.sem, 1)
        self.eng.wait_ge(self.sem, self.base + self.k)
        return ins


def semaphores(nc, c, tag):
    sems = []

    def release():
        nc.clear_and_free_semaphores(sems)
        nc.all_engine_barrier()

    def sem(name):
        sems.append(nc.alloc_semaphore(tag + name))
        return sems[-1]

    c.callback(release)
    return sem


def hold(m, eng):
    eng.sem_inc(m.held[str(eng.engine)], 1)


def load_group(nc, m, eng, g, first=False):
    return [eng.value_load(m.ctl[0:1, bass.ds(g * 3 + k, 1)], min_val=lo, max_val=hi)
            for k, lo, hi in ((0, 0, N - 1), (1, 1, NT), (2, 0, NG + NT))[not first:]]


def window_start(nc, d0, i):
    return nc.s_assert_within(d0 + i * P, 0, NP - 1, skip_runtime_bounds_check_because=WINDOW_FITS)


def load_all(nc, m, a):
    with ExitStack() as c:
        sb = lambda n, s, d=F32: c.enter_context(nc.sbuf_tensor("in_" + n, s, d))
        sem = semaphores(nc, c, "in_")
        pt = c.enter_context(nc.psum_tensor("in_ps", [P, 4, 512], F32))
        dstR, nxtR = sb("dstR", [P, NC], I32), sb("nxtR", [P, NC], I32)
        hiI = sb("hiI", [P, NC], I32)
        rowsI = sb("rowsI", [NG, 3, GE], I32)
        rowsF = sb("rowsF", [NG, 3, GE])
        mks = sb("mks", [NG, 4, GE])
        endI, endF = sb("endI", [1, 2, NC + 1], I32), sb("endF", [1, 2, NC + 1])
        con, sgl, rf = sb("con", [1, NC + 1]), sb("sgl", [1, NC]), sb("rf", [1, NC])
        d0i = sb("d0i", [1, NG + 1], I32)
        d0f = sb("d0f", [1, NG + 1])
        spn = sb("spn", [1, NG], I32)
        rem = sb("rem", [1, NG + 1], I32)
        remf = sb("remf", [1, NG + 1])
        nwf, zero, incl, bas = (sb(n, [1, NG]) for n in ("nwf", "zero", "incl", "bas"))
        gw = sb("gw", [P, 2, D])
        zrow = sb("zrow", [P, D + 1])
        gwT, att, wqT, wkb, bqc = (sb("gwT", [P, 2, D]), sb("att", [P, 2, 2 * H]), sb("wqT", [P, 2, D]),
                                   sb("wkb", [P, 2, D + 1]), sb("bqc", [P, 2]))
        s_set, s_ld, s_w, s_v, s_cast, s_pe, s_st, s_seg, s_rd = (
            sem(n) for n in ("set", "ld", "w", "v", "cast", "pe", "st", "seg", "rd"))
        block = c.enter_context(nc.Block())

        @block.gpsimd
        def _(pool):
            nc.gpsimd.memset(m.ident[:], 0.0).then_inc(s_set, 1)
            nc.gpsimd.memset(m.ones[:], 1.0)
            nc.gpsimd.memset(zrow[:], 0.0)
            nc.gpsimd.memset(m.eps[:], LN_EPS)
            nc.gpsimd.iota(m.iota[:], [[1, P]], base=0, channel_multiplier=0,
                           allow_small_or_imprecise_dtypes=True)
            nc.gpsimd.iota(m.iotap[:], [[1, 1]], base=0, channel_multiplier=1,
                           allow_small_or_imprecise_dtypes=True).then_inc(s_set, 1)
            pool.wait_ge(s_set, 2)
            nc.gpsimd.affine_select(out=m.ident[:], in_=m.ident[:], compare_op=ALU.not_equal, fill=1.0,
                                    base=0, pattern=[[-1, P]], channel_multiplier=1).then_inc(s_set, 1)

        @block.sync
        def _(sp):
            sp.dma_start(dstR[:], a["dst_cols"]).then_inc(s_ld, 16)
            sp.dma_start(nxtR[:], a["next_cols"]).then_inc(s_ld, 16)
            for k in range(3):
                sp.dma_start(rowsI[:, k, :], a["dst_flat"][k:k + NC * P].rearrange("(g e) -> g e", e=GE)).then_inc(s_ld, 16)
            with nc.allow_non_contiguous_dma(reason="first destination of each group"):
                sp.dma_start(d0i[0:1, 0:NG], a["dst_flat"][1:1 + NC * P].rearrange("(a g e) -> a g e", a=1, e=GE)[:, :, 0]).then_inc(s_ld, 16)
                sp.dma_start(endI[0:1, 0, 0:NC], a["dst_flat"][1:1 + NC * P].rearrange("(a c e) -> a c e", a=1, e=P)[:, :, 0]).then_inc(s_ld, 16)
                sp.dma_start(endI[0:1, 0, NC:NC + 1], a["dst_flat"][0:1].rearrange("(a c) -> a c", a=1)).then_inc(s_ld, 16)
                sp.dma_start(endI[0:1, 1, 0:NC], a["dst_flat"][0:NC * P].rearrange("(a c e) -> a c e", a=1, e=P)[:, :, 0]).then_inc(s_ld, 16)
                sp.dma_start(endI[0:1, 1, NC:NC + 1], a["dst_flat"][NC * P:NC * P + 1].rearrange("(a c) -> a c", a=1)).then_inc(s_ld, 16)
            sp.dma_start(m.srcI[:], a["src_cols"]).then_inc(s_w, 16)
            sp.dma_start(m.wF[:], a["w_cols"]).then_inc(s_w, 16)
            for t_, n in ((m.w6, "W6T"), (m.w7, "W7T"), (m.wp, "WpT"), (gw, "gat_W"), (gwT, "gat_WT"), (att, "att"),
                          (wqT, "WqT"), (wkb, "WkTb"), (m.wv, "Wv"), (m.wsk, "Wskip")):
                sp.dma_start(t_[:], a[n].rearrange("(k p) n -> p k n", p=P)).then_inc(s_w, 16)
            with nc.allow_non_contiguous_dma(reason="a column of biases"):
                sp.dma_start(bqc[:], a["bq"].rearrange("(k p) -> p k", p=P)).then_inc(s_w, 16)
            for k, n in enumerate(m.ROWS):
                sp.dma_start(m.rows[:, k, :], a[n].partition_broadcast(P)).then_inc(s_w, 16)
            for t_, n in ((m.bv, "bv"), (m.bsk, "bskip")):
                sp.dma_start(t_[:], a[n].rearrange("(a n) -> a n", a=1)).then_inc(s_w, 16)
            sp.wait_ge(s_set, 3)
            sp.dma_start(m.ad[NP:NW, :], zrow[:, 0:H]).then_inc(s_st, 16)
            sp.dma_start(m.qk[NP:NW, :], zrow[:]).then_inc(s_st, 16)
            sp.wait_ge(s_seg, 1)
            sp.dma_start(m.masks.rearrange("k (g e) -> g k e", e=GE), mks[:]).then_inc(s_st, 16)
            sp.dma_start(m.dstf.rearrange("(g e) -> g e", e=GE), rowsF[:, 1, :]).then_inc(s_st, 16)
            sp.wait_ge(s_st, 64)
        NWL = 2 + 10 + 1 + len(m.ROWS) + 2

        @block.vector
        def _(dve):
            y = Tally(dve, s_v)
            dve.wait_ge(s_ld, 16 * 10)
            y.chain(nc.vector.tensor_copy(m.dstF[:], dstR[:]))
            nc.vector.tensor_copy(rowsF[:], rowsI[:])
            y.chain(nc.vector.tensor_tensor(m.lastE[:], dstR[:], nxtR[:], ALU.not_equal))
            y.chain(nc.vector.tensor_scalar(hiI[:], dstR[:], 7, None, ALU.arith_shift_right))
            y.chain(nc.vector.tensor_copy(m.hiF[:], hiI[:]))
            y.chain(nc.vector.scalar_tensor_tensor(m.loF[:], m.hiF[:], -float(P), m.dstF[:], ALU.mult, ALU.add))
            for k in (0, 1):
                y.chain(nc.vector.tensor_tensor(mks[:, k, :], rowsF[:, 1, :], rowsF[:, 2 * k, :], ALU.not_equal))
            rows = rowsF[:, 1, :].rearrange("g (u e) -> g u e", e=P)
            for k, e in ((2, 0), (3, P - 1)):
                y.chain(nc.vector.tensor_tensor(mks[:, k, :].rearrange("g (u e) -> g u e", e=P), rows,
                                                rows[:, :, e:e + 1].broadcast_to([NG, U, P]), ALU.not_equal))
            y.chain(nc.vector.tensor_scalar(mks[:], mks[:], -BIG, None, ALU.mult))
            nc.vector.memset(m.ctl[0:1, 0:1], 0).then_inc(s_seg, 1)
            y.chain(nc.vector.memset(d0i[0:1, 0:1], 0))
            y.chain(nc.vector.memset(d0i[0:1, NG:NG + 1], NP - 1))
            y.chain(nc.vector.tensor_tensor(spn[:], d0i[0:1, 1:NG + 1], d0i[0:1, 0:NG], ALU.subtract))
            y.chain(nc.vector.tensor_scalar(rem[0:1, 1:NG + 1], spn[:], P - 1, None, ALU.bitwise_and))
            y.chain(nc.vector.memset(rem[0:1, 0:1], -1))
            y.chain(nc.vector.tensor_copy(remf[:], rem[:]))
            y.chain(nc.vector.tensor_scalar(spn[:], spn[:], 7, None, ALU.arith_shift_right))
            y.chain(nc.vector.tensor_scalar(nwf[:], spn[:], 1.0, None, ALU.add))
            y.chain(nc.vector.memset(zero[:], 0.0))
            y.chain(nc.vector.tensor_tensor_scan(incl[:], nwf[:], zero[:], 0.0, ALU.add, ALU.add))
            y.chain(nc.vector.tensor_tensor(bas[:], incl[:], nwf[:], ALU.subtract))
            y.chain(nc.vector.tensor_copy(d0f[:], d0i[:]))
            y.chain(nc.vector.tensor_copy(endF[:], endI[:]))
            y.chain(nc.vector.memset(con[:], 0.0))
            y.chain(nc.vector.tensor_tensor(con[0:1, 0:NC], endF[0:1, 0, 0:NC], endF[0:1, 1, 0:NC], ALU.is_equal))
            y.chain(nc.vector.tensor_tensor(sgl[:], endF[0:1, 0, 0:NC], endF[0:1, 1, 1:NC + 1], ALU.is_equal))
            y.chain(nc.vector.tensor_scalar(m.cont[:], con[0:1, 0:NC], -1.0, BIG, ALU.add, ALU.mult))
            y.chain(nc.vector.memset(m.runf[:], -BIG))
            y.chain(nc.vector.memset(m.runb[:], -BIG))
            of = lambda t_: t_[0:1, 0:NC].rearrange("a (g u) -> a g u", u=U)
            fv = m.runf[:].rearrange("a (g h v) -> a g h v", h=H, v=U + 1)
            bv = m.runb[:].rearrange("a (g h u) -> a g h u", h=H, u=U)
            y.chain(nc.vector.tensor_tensor(rf[:], con[0:1, 0:NC], sgl[:], ALU.mult))
            y.chain(nc.vector.tensor_scalar(rf[:], rf[:], -1.0, BIG, ALU.add, ALU.mult))
            for h in range(H):
                y.chain(nc.vector.tensor_copy(fv[:, :, h, 1:U + 1], of(rf)))
            y.chain(nc.vector.tensor_tensor(rf[:], con[0:1, 1:NC + 1], sgl[:], ALU.mult))
            y.chain(nc.vector.tensor_scalar(rf[:], rf[:], -1.0, BIG, ALU.add, ALU.mult))
            for h in range(H):
                y.chain(nc.vector.tensor_copy(bv[:, :, h, 1:U], of(rf)[:, :, 0:U - 1][:, :, ::-1]))
            cv = m.ctl[0:1, :].rearrange("a (g k) -> a g k", k=3)
            y.chain(nc.vector.tensor_copy(cv[:, :, 0], d0i[0:1, 0:NG]))
            y.chain(nc.vector.tensor_copy(cv[:, :, 1], nwf[:]))
            y.chain(nc.vector.tensor_copy(cv[:, :, 2], bas[:]))
            nc.vector.memset(m.t4one[:], 1.0).then_inc(s_cast, 1)
            dve.wait_ge(s_pe, 1)
            nc.vector.tensor_copy(m.d0rep[:], pt[:, 0, 0:NG])
            nc.vector.tensor_scalar(m.rcol[:], pt[:, 1, 0:NG], m.iotap[:, 0:1], None, ALU.is_equal).then_inc(s_rd, 1)
            dve.wait_ge(s_w, 16 * NWL)
            dve.wait_ge(s_pe, 2)
            gv = m.gw[:, :, 0:H * (HC + 1)].rearrange("p k (h c) -> p k h c", h=H)
            for k in range(2):
                nc.vector.tensor_copy(gv[:, k, :, 0:HC], gw[:, k, :].rearrange("p (h c) -> p h c", h=H))
                nc.vector.tensor_copy(gv[:, k, :, HC], pt[:, 0, 16 * k:16 * k + H])
                nc.vector.tensor_copy(m.gw[:, k, H * (HC + 1):AGW], pt[:, 0, 16 * k + H:16 * k + 2 * H])
            dve.wait_ge(s_pe, 3)
            for k in range(2):
                nc.vector.tensor_scalar(m.wqk[:, k, :], pt[:, 2 + k, 0:D + 1], float(D) ** -0.5, None, ALU.mult)
            dve.wait_ge(s_pe, 4)
            y.chain(nc.vector.tensor_scalar(m.bqk[:], pt[0:1, 1, 0:D + 1], float(D) ** -0.5, None, ALU.mult))

        @block.tensor
        def _(pe):
            pe.wait_ge(s_set, 3)
            pe.wait_ge(s_cast, 1)
            nc.tensor.matmul(pt[:, 0, 0:NG], m.ones[0:1, :], d0f[0:1, 0:NG], start=True, stop=True)
            nc.tensor.matmul(pt[:, 1, 0:NG], m.ones[0:1, :], remf[0:1, 0:NG], start=True, stop=True).then_inc(s_pe, 1)
            pe.wait_ge(s_w, 16 * NWL)
            pe.wait_ge(s_rd, 1)
            for k in range(2):
                for j in range(2):
                    last = nc.tensor.matmul(pt[:, 0, 16 * k:16 * k + 2 * H], gwT[:, j, k * P:k * P + P], att[:, j, :],
                                            start=(j == 0), stop=(j == 1))
            last.then_inc(s_pe, 1)
            for k in range(2):
                for j in range(2):
                    last = nc.tensor.matmul(pt[:, 2 + k, 0:D + 1], wqT[:, j, k * P:k * P + P], wkb[:, j, :],
                                            start=(j == 0), stop=(j == 1))
            last.then_inc(s_pe, 1)
            for j in range(2):
                last = nc.tensor.matmul(pt[0:1, 1, 0:D + 1], bqc[:, j:j + 1], wkb[:, j, :], start=(j == 0), stop=(j == 1))
            last.then_inc(s_pe, 1)


def degrees(nc, m):
    with ExitStack() as c:
        sb = lambda n, s, d=F32: c.enter_context(nc.sbuf_tensor("dg_" + n, s, d))
        sem = semaphores(nc, c, "dg_")
        lo, hi = sb("lo", [P, U, P]), sb("hi", [P, U, NT])
        deg, sd, pos = sb("deg", [P, NT]), sb("sd", [P, NT]), sb("pos", [P, NT])
        zero = sb("zero", [P, P])
        ps = c.enter_context(nc.psum_tensor("dg_ps", [P, 512], F32))
        s_z, s_oh, s_mm, s_v, s_sd = (sem(n) for n in ("z", "oh", "mm", "v", "sd"))
        block = c.enter_context(nc.Block())

        @block.gpsimd
        def _(pool):
            nc.gpsimd.memset(zero[:], 0.0).then_inc(s_z, 1)

        @block.vector
        def _(dve):
            y = Tally(dve, s_v)
            with dve.Fori(0, NG) as g:
                for u in range(U):
                    dve.wait_ge(s_mm, g * U + u + 1)
                    nc.vector.tensor_scalar(lo[:, u, :], m.iota[:], m.loF[:, bass.ds(g * U + u, 1)], None, ALU.is_equal)
                    nc.vector.tensor_scalar(hi[:, u, :], m.iota[:, 0:NT], m.hiF[:, bass.ds(g * U + u, 1)],
                                            m.wF[:, bass.ds(g * U + u, 1)], ALU.is_equal, ALU.mult).then_inc(s_oh, 1)
            dve.wait_ge(s_mm, NC + U + 1)
            y.chain(nc.vector.tensor_scalar(deg[:], ps[:, 0:NT], 1.0, None, ALU.add))
            y.chain(nc.vector.tensor_scalar(pos[:], deg[:], 0.0, None, ALU.is_gt))
            y.chain(nc.vector.tensor_scalar(deg[:], deg[:], 1e-30, None, ALU.max))
            dve.wait_ge(s_sd, 1)
            y.chain(nc.vector.reciprocal(sd[:], sd[:]))
            y.chain(nc.vector.tensor_tensor(m.dis[:], sd[:], pos[:], ALU.mult))

        @block.scalar
        def _(act):
            act.wait_ge(s_v, 3)
            nc.scalar.activation(sd[:], deg[:], ACT.Sqrt).then_inc(s_sd, 1)

        @block.tensor
        def _(pe):
            pe.wait_ge(s_z, 1)
            pe.sem_inc(s_mm, U)
            nc.tensor.matmul(ps[:, 0:NT], zero[:], zero[:, 0:NT], start=True, stop=False)
            with pe.Fori(0, NG) as g:
                for u in range(U):
                    pe.wait_ge(s_oh, g * U + u + 1)
                    nc.tensor.matmul(ps[:, 0:NT], lo[:, u, :], hi[:, u, :], start=False, stop=False).then_inc(s_mm, 1)
            nc.tensor.matmul(ps[:, 0:NT], zero[:], zero[:, 0:NT], start=False, stop=True).then_inc(s_mm, 1)


def first_rows(nc, m, x):
    B = 7
    assert NT % B == 0
    with ExitStack() as c:
        sb = lambda n, s, d=F32: c.enter_context(nc.sbuf_tensor("fr_" + n, s, d))
        sem = semaphores(nc, c, "fr_")
        xb, hb, nb = sb("x", [P, B, D]), sb("h", [P, B, D]), sb("n", [P, B, D])
        st, mv, sd, r = sb("st", [P, B, 6]), sb("mv", [P, B, 2]), sb("sd", [P, B]), sb("r", [P, B])
        s_ld, s_v, s_a, s_st, s_go = (sem(n) for n in ("ld", "v", "a", "st", "go"))
        block = c.enter_context(nc.Block())
        rows = lambda t_: t_[0:NP, 0:D].rearrange("(t p) n -> p t n", p=P)
        K = 11

        @block.sync
        def _(sp):
            with sp.Fori(0, NT // B) as t:
                sp.dma_start(xb[:], rows(x)[:, bass.ds(t * B, B), :]).then_inc(s_ld, 16)
                sp.wait_ge(s_v, t * K + K)
                sp.dma_start(rows(m.h0)[:, bass.ds(t * B, B), :], hb[:]).then_inc(s_st, 16)
                sp.dma_start(rows(m.t1)[:, bass.ds(t * B, B), :], nb[:]).then_inc(s_st, 16)
                sp.wait_ge(s_st, t * 32 + 32)
                hold(m, sp)

        @block.scalar
        def _(act):
            with act.Fori(0, NT // B) as t:
                act.wait_ge(s_v, t * K + 2)
                nc.scalar.activation(sd[:], mv[:, :, 1], ACT.Sqrt, bias=m.eps[:, 0:1]).then_inc(s_a, 1)
                act.wait_ge(s_v, t * K + 4)
                nc.scalar.activation(hb[:], hb[:], ACT.Relu).then_inc(s_a, 1)
                act.wait_ge(s_v, t * K + 6)
                nc.scalar.activation(sd[:], mv[:, :, 1], ACT.Sqrt, bias=m.eps[:, 0:1]).then_inc(s_a, 1)

        @block.vector
        def _(dve):
            y = Tally(dve, s_v)
            with dve.Fori(0, NT // B) as t:
                y.at(t * K)
                dve.wait_ge(s_ld, t * 16 + 16)
                for part in (0, 1):
                    src = (xb, hb)[part]
                    for j in range(B):
                        last = nc.vector.bn_stats(st[:, j, :], src[:, j, :])
                    y.chain(last)
                    hold(m, dve)
                    for j in range(B):
                        last = nc.vector.bn_aggr(mv[:, j, :], st[:, j, :])
                    y.chain(last)
                    dve.wait_ge(s_a, t * 3 + (1, 3)[part])
                    y.chain(nc.vector.reciprocal(r[:], sd[:]))
                    if part == 1:
                        y.chain(nc.vector.tensor_tensor(r[:], r[:], m.dis[:, bass.ds(t * B, B)], ALU.mult))
                    for j in range(B):
                        last = nc.vector.tensor_scalar((hb, nb)[part][:, j, :], src[:, j, :], mv[:, j, 0:1], r[:, j:j + 1],
                                                       ALU.subtract, ALU.mult)
                    y.chain(last)
                    if part == 0:
                        dve.wait_ge(s_a, t * 3 + 2)
                y.chain(nc.vector.tensor_tensor(nb[:], nb[:], m.row("g6").unsqueeze(1).broadcast_to([P, B, D]), ALU.mult))
                for j in range(B):
                    last = nc.vector.scalar_tensor_tensor(nb[:, j, :], m.row("c6"), m.dis[:, bass.ds(t * B + j, 1)], nb[:, j, :],
                                                          ALU.mult, ALU.add)
                y.k += 1
                assert y.k == K, y.k
                last.then_inc(s_v, 1)
                dve.wait_ge(s_v, t * K + K)
                dve.wait_ge(s_st, t * 32 + 32)


def feed_indices(nc, m, sp, g, b, cur, s_cur, s_done):
    sp.wait_ge(s_done, g + 1)
    sp.dma_start(cur[:, b, :], m.srcI[:, bass.ds(g * U, U)]).then_inc(s_cur[b], 16)


def gather_rows(nc, m, pool, cur, G, width, table, s_cur, s_g, nb):
    with pool.Fori(0, NG // nb) as t:
        for b in range(nb):
            pool.wait_ge(s_cur[b], 16 * t + 16)
            hold(m, pool)
            for u in range(U):
                pool.indirect_dma_start(G[:, b, u, 0:width], None, table,
                                        IOA(ap=cur[:, b, u:u + 1], axis=0)).then_inc(s_g[b], 16)


def store_windows(nc, m, act, d0, nwin, base, width, ps, stage, s_ohu, s_st, s_ev):
    with act.Fori(0, nwin) as i:
        act.wait_ge(s_ohu, (base + i + 2) * U)
        act.wait_ge(s_st, (base + i) * 16 + 16)
        nc.scalar.activation(stage[:, 0:width], ps[:, 0:width], ACT.Copy).then_inc(s_ev, 1)
        act.wait_ge(s_ev, base + i + 2)
        act.dma_start(m.agg[bass.ds(window_start(nc, d0, i), P), 0:width], stage[:, 0:width]).then_inc(s_st, 16)


def gcn_pass(nc, m, tag, table):
    with ExitStack() as c:
        sb = lambda n, s, d=F32: c.enter_context(nc.sbuf_tensor(tag + n, s, d))
        sem = semaphores(nc, c, tag)
        G, cur = sb("G", [P, NBG, U, D]), sb("cur", [P, NBG, U], I32)
        rel, oh = sb("rel", [P, U]), sb("oh", [P, U, P])
        S, scol, stage = sb("S", [P, P]), sb("scol", [P, 1]), sb("stage", [P, D])
        ps = c.enter_context(nc.psum_tensor(tag + "ps", [P, 512], F32))
        s_cur = [sem(f"cur{b}") for b in range(NBG)]
        s_g = [sem(f"gath{b}") for b in range(NBG)]
        s_zero, s_rel, s_oh, s_ohu, s_S, s_y, s_ev, s_st, s_done = (
            sem(n) for n in ("zero", "rel", "oh", "ohu", "S", "y", "ev", "st", "done"))
        block = c.enter_context(nc.Block())

        @block.sync
        def _(sp):
            with sp.Fori(0, NG // NBG) as t:
                for b in range(NBG):
                    feed_indices(nc, m, sp, t * NBG + b, b, cur, s_cur, s_done)

        @block.gpsimd
        def _(pool):
            nc.gpsimd.memset(S[:], 0.0)
            nc.gpsimd.memset(stage[:], 0.0).then_inc(s_zero, 1)
            gather_rows(nc, m, pool, cur, G, D, table, s_cur, s_g, NBG)

        @block.vector
        def _(dve):
            dve.wait_ge(s_zero, 1)
            dve.sem_inc(s_rel, 1)
            dve.sem_inc(s_y, 1)
            with dve.Fori(0, NG) as g:
                nwin, base = load_group(nc, m, dve, g)
                dve.wait_ge(s_rel, g + base + 1)
                nc.vector.tensor_scalar(rel[:], m.dstF[:, bass.ds(g * U, U)], m.d0rep[:, bass.ds(g, 1)],
                                        None, ALU.subtract).then_inc(s_rel, 1)
                dve.wait_ge(s_y, g + base + 1)
                nc.vector.tensor_copy(scol[:], m.rcol[:, bass.ds(g, 1)]).then_inc(s_y, 1)
                hold(m, dve)
                with dve.Fori(0, nwin) as i:
                    dve.wait_ge(s_rel, g + base + i + 2)
                    for u in range(U):
                        dve.wait_ge(s_ohu, (base + i) * U + u + 1)
                        nc.vector.tensor_scalar(oh[:, u, :], m.iota[:], rel[:, u:u + 1],
                                                m.wF[:, bass.ds(g * U + u, 1)],
                                                ALU.is_equal, ALU.mult).then_inc(s_oh, 1)
                    dve.wait_ge(s_ohu, (base + i + 1) * U)
                    dve.wait_ge(s_y, g + base + i + 2)
                    nc.vector.tensor_copy(S[:, 0:1], scol[:]).then_inc(s_S, 1)
                    dve.wait_ge(s_S, base + i + 1)
                    nc.vector.memset(scol[:], 0.0).then_inc(s_y, 1)
                    dve.wait_ge(s_oh, (base + i + 1) * U)
                    nc.vector.tensor_scalar(rel[:], rel[:], float(P), None, ALU.subtract).then_inc(s_rel, 1)

        @block.tensor
        def _(pe):
            pe.sem_inc(s_ohu, U)
            with pe.Fori(0, NG // NBG) as t:
                for b in range(NBG):
                    nwin, base = load_group(nc, m, pe, t * NBG + b)
                    pe.wait_ge(s_g[b], 16 * U * t + 16 * U)
                    hold(m, pe)
                    with pe.Fori(0, nwin) as i:
                        pe.wait_ge(s_ev, base + i + 1)
                        for u in range(U):
                            if u == U - 1:
                                pe.wait_ge(s_S, base + i + 1)
                                nc.tensor.matmul(ps[:, 0:D], S[:], stage[:], start=False, stop=False)
                            pe.wait_ge(s_oh, (base + i) * U + u + 1)
                            nc.tensor.matmul(ps[:, 0:D], oh[:, u, :], G[:, b, u, :],
                                             start=(u == 0), stop=(u == U - 1)).then_inc(s_ohu, 1)

        @block.scalar
        def _(act):
            act.sem_inc(s_ev, 1)
            act.sem_inc(s_done, NBG)
            act.sem_inc(s_st, 16)
            with act.Fori(0, NG) as g:
                d0, nwin, base = load_group(nc, m, act, g, True)
                store_windows(nc, m, act, d0, nwin, base, D, ps, stage, s_ohu, s_st, s_ev)
                act.wait_ge(s_ohu, (base + nwin + 1) * U)
                act.sem_inc(s_done, 1)
            nwin, base = load_group(nc, m, act, NG - 1)
            act.wait_ge(s_st, (base + nwin) * 16 + 16)
            hold(m, act)


def skewed(eng, body):
    for k in range(NB):
        body(k, k)
    with eng.Fori(1, NG // NB) as t:
        for b in range(NB):
            body(t * NB + b, b)
    for k in (NG, NG + 1):
        body(k, k % NB)


def softmax_pass(nc, m, tag, table, win_table, gat):
    HH = H if gat else 1
    HU = HH * U
    WW = H if gat else D + 1
    AW = AGW if gat else D + 1
    SW = HC + 1 if gat else D + 1
    MA = 1 if gat else U
    NA = 1 if gat else 2
    KA, KW = (3 if gat else 2), 3
    KC, KX = (4 if gat else 2), 3
    K1, K2, K3 = 2, 10, 2
    with ExitStack() as c:
        sb = lambda n, s, d=F32: c.enter_context(nc.sbuf_tensor(tag + n, s, d))
        sem = semaphores(nc, c, tag)
        psb = lambda n, s: c.enter_context(nc.psum_tensor(tag + n, s, F32))
        G, cur = sb("G", [P, NB, U, ROW]), sb("cur", [P, NB, U], I32)
        Gp = sb("Gp", [P, U, AGW])
        dB, ohT = sb("dB", [P, 2, GE]), sb("ohT", [P, GE])
        win = sb("win", [P, WW])
        wpos = sb("wpos", [P, 1])
        mk = sb("mk", [HU, 2, 4, P])
        L = sb("L", [P, NB, HH, U])
        Lp, p, z = (sb(n, [P, HH, U]) for n in ("Lp", "p", "z"))
        F, M = sb("F", [HU, P]), sb("M", [HU, 2, P])
        ends = sb("ends", [1, HH, U + 1])
        run = sb("run", [1, HH, U + 1])
        nf, Tf, Tl, Tm = (sb(n, [1, HH, U]) for n in ("nf", "Tf", "Tl", "Tm"))
        dif, fac = sb("dif", [1, HH]), sb("fac", [1, HH])
        junk = sb("junk", [P, D + 1])
        rel, oh = sb("rel", [P, U]), sb("oh", [P, U, P])
        S, scol, stage = sb("S", [P, HH, P]), sb("scol", [P, HH]), sb("stage", [P, AW])
        psA = psb("psA", [P, NA, 512])
        psL, psE, psM, ps = psb("psL", [HU, 512]), psb("psE", [P, 512]), psb("psM", [P, 2, 512]), psb("ps", [P, 512])
        psX = psE[0:1, 0:2 * HU]
        psY = psE[0:HU, 128:130]
        psF = lambda g: psM[:, g % 2, HU:HU + HH]
        s_cur = [sem(f"cur{b}") for b in range(NB)]
        s_g = [sem(f"gath{b}") for b in range(NB)]
        s_mk = [sem(f"mk{b}") for b in range(2)]
        s_db = [sem(f"db{b}") for b in range(2)]
        (s_zero, s_win, s_free, s_ya, s_y1, s_y2, s_y3, s_yc, s_oht, s_pa, s_pu, s_L, s_lt, s_s1, s_fl, s_s2, s_tt,
         s_s3, s_mb, s_z, s_p, s_fac, s_gp, s_oh, s_ohu, s_S, s_ev, s_st, s_done) = (sem(n) for n in (
             "zero", "win", "free", "ya", "y1", "y2", "y3", "yc", "oht", "pa", "pu", "L", "lt", "s1", "fl", "s2",
             "tt", "s3", "mb", "z", "p", "fac", "gp", "oh", "ohu", "S", "ev", "st", "done"))
        block = c.enter_context(nc.Block())
        heads = lambda t_: t_.rearrange("p u (h c) -> p u h c", h=H)
        flat = lambda t_: t_.rearrange("a h u -> a (h u)")
        uh = lambda t_: t_.rearrange("p h u -> p u h")
        mxs = lambda g: psM[:, g % 2, 0:HU].rearrange("p (h u) -> p h u", h=HH)

        @block.sync
        def _(sp):
            for b in range(LEAD):
                feed_indices(nc, m, sp, b, b, cur, s_cur, s_done)
            with sp.Fori(0, NG // NB) as t:
                for b in range(NB):
                    g = t * NB + b
                    feed_indices(nc, m, sp, g + LEAD, (b + LEAD) % NB, cur, s_cur, s_done)
                    d0, nwin, base = load_group(nc, m, sp, g, True)
                    sp.wait_ge(s_free, g + 1)
                    sp.dma_start(dB[:, b % 2, :], m.dstf[bass.ds(g * GE, GE)].partition_broadcast(P)).then_inc(s_db[b % 2], 16)
                    with sp.Fori(0, nwin) as i:
                        sp.wait_ge(s_pa, (base + i) * MA + 1)
                        hold(m, sp)
                        sp.dma_start(win[:], win_table[bass.ds(window_start(nc, d0, i), P), 0:WW]).then_inc(s_win, 16)
                    sp.wait_ge(s_s3, g + 1)
                    for h in range(HH):
                        sp.dma_start(mk[h * U:h * U + U, b % 2, :, :],
                                     m.masks[:, bass.ds(g * GE, GE)].rearrange("k (u e) -> u k e", e=P)).then_inc(s_mk[b % 2], 16)
            for b in range(LEAD):
                sp.wait_ge(s_cur[b], 16 * (NG // NB + 1))

        @block.gpsimd
        def _(pool):
            nc.gpsimd.memset(ends[:], -BIG)
            nc.gpsimd.memset(Tl[:], -BIG)
            nc.gpsimd.memset(S[:], 0.0)
            nc.gpsimd.memset(stage[:], 0.0).then_inc(s_zero, 1)
            gather_rows(nc, m, pool, cur, G, ROW, table, s_cur, s_g, NB)

        @block.vector
        def _(dve):
            ya, y1, y2, y3, yc = (Tally(dve, s_) for s_ in (s_ya, s_y1, s_y2, s_y3, s_yc))
            dve.wait_ge(s_zero, 1)
            dve.sem_inc(s_free, 2)
            dve.sem_inc(s_pu, NA)
            dve.sem_inc(s_s3, 2)

            kept = {}

            def spread(g, n, b):
                ya.at(g * KA + 2 + n * KW)
                dve.wait_ge(s_pa, n * MA + 1)
                ya.chain(nc.vector.tensor_scalar(ohT[:], dB[:, b % 2, :], wpos[:, 0:1], None, ALU.is_equal))
                dve.sem_inc(s_oht, 1)
                ya.chain(nc.vector.tensor_scalar(wpos[:], wpos[:], float(P), None, ALU.add))

            def logits(g, n, b):
                ya.at(g * KA + 4 + n * KW)
                if gat:
                    dve.wait_ge(s_pa, n + 2)
                    ya.chain(nc.vector.tensor_tensor(uh(L[:, b]), uh(L[:, b]), psA[:, 0, 0:HU].rearrange("p (u h) -> p u h", h=H), ALU.add))
                else:
                    for u in range(U):
                        dve.wait_ge(s_pa, n * U + u + 2)
                        if u:
                            dve.wait_ge(s_pu, n * U + u + NA)
                        nc.vector.tensor_tensor_reduce(out=junk[:], in0=G[:, b, u, 0:D + 1], in1=psA[:, u % NA, 0:D + 1],
                                                       scale=1.0, scalar=0.0, op0=ALU.mult, op1=ALU.add,
                                                       accum_out=Lp[:, 0, u:u + 1]).then_inc(s_pu, 1)
                    dve.wait_ge(s_pu, n * U + U + NA)
                    ya.chain(nc.vector.tensor_tensor(L[:, b], L[:, b], Lp[:], ALU.add))

            def body(k, b):
                fixed = isinstance(k, int)
                if not fixed or k < NG:
                    nwin, base = kept[b] = load_group(nc, m, dve, k)
                    dve.wait_ge(s_g[b], (k - b) * (16 * U // NB) + 16 * U)
                    ya.at(k * KA + base * KW)
                    if gat:
                        ya.chain(nc.vector.tensor_copy(uh(L[:, b]), heads(G[:, b, :, :])[:, :, :, HC]))
                    else:
                        ya.chain(nc.vector.memset(L[:, b], 0.0))
                    ya.chain(nc.vector.tensor_tensor(wpos[:], m.iotap[:], m.d0rep[:, bass.ds(k, 1)], ALU.add))
                    dve.wait_ge(s_db[b % 2], (k - b % 2) * 8 + 16)
                    spread(k, base, b)
                if not fixed or k >= 2:
                    dve.wait_ge(s_mb, k - 1)
                    nc.vector.tensor_tensor(z[:], L[:, (b - 2) % NB], mxs(b), ALU.subtract).then_inc(s_z, 1)
                if not fixed or 1 <= k <= NG:
                    g = k - 1
                    y2.at(g * K2)
                    dve.wait_ge(s_fl, g + 1)
                    dve.wait_ge(s_fac, g + 1)
                    first, last = (psX[:, j * HU:j * HU + HU].rearrange("a (h u) -> a h u", h=HH) for j in (0, 1))
                    cont = m.cont[0:1, bass.ds(g * U, U)].unsqueeze(1).broadcast_to([1, HH, U])
                    y2.chain(nc.vector.tensor_copy(ends[:, :, 1:U + 1], last))
                    y2.chain(nc.vector.tensor_tensor_scan(flat(run[:]), m.runf[0:1, bass.ds(g * H * (U + 1), HH * (U + 1))],
                                                          flat(ends[:]), -BIG, ALU.add, ALU.max))
                    y2.chain(nc.vector.tensor_tensor(nf[:], run[:, :, 0:U], cont, ALU.add))
                    y2.chain(nc.vector.tensor_tensor(nf[:], nf[:], first, ALU.max))
                    back = m.runb[0:1, bass.ds(g * H * U, HH * U)]
                    y2.chain(nc.vector.tensor_tensor_scan(flat(Tf[:])[:, ::-1], back, flat(nf[:])[:, ::-1], -BIG, ALU.add, ALU.max))
                    y2.chain(nc.vector.tensor_tensor(Tl[:, :, 0:U - 1], Tf[:, :, 1:U], cont[:, :, 1:U], ALU.add))
                    y2.chain(nc.vector.tensor_tensor(Tm[:], Tl[:], run[:, :, 1:U + 1], ALU.max))
                    y2.chain(nc.vector.tensor_tensor(dif[:], ends[:, :, 0], Tf[:, :, 0], ALU.subtract))
                    y2.chain(nc.vector.tensor_scalar(dif[:], dif[:], 0.0, None, ALU.min))
                    y2.chain(nc.vector.tensor_copy(ends[:, :, 0], run[:, :, U]))
                    dve.sem_inc(s_s2, 1)
                    assert y2.k == K2
                if not fixed or k < NG:
                    logits(k, base, b)
                    hold(m, dve)
                    with dve.If(nwin > 1):
                        with dve.Fori(1, nwin) as i:
                            spread(k, base + i, b)
                            logits(k, base + i, b)
                    ya.at(k * KA + 2 + (base + nwin) * KW)
                    if gat:
                        ya.chain(nc.vector.scalar_tensor_tensor(L[:, b], L[:, b], 0.2, L[:, b], ALU.mult, ALU.max))
                    dve.sem_inc(s_L, 1)
                    dve.sem_inc(s_free, 1)
                if not fixed or 1 <= k <= NG:
                    g, q = k - 1, (b - 1) % 2
                    y3.at(g * K3)
                    dve.wait_ge(s_tt, g + 1)
                    for j in (0, 1):
                        y3.chain(nc.vector.scalar_tensor_tensor(M[:, q, :], mk[:, q, 2 + j, :], psY[:, j:j + 1], M[:, q, :], ALU.add, ALU.max))
                    dve.sem_inc(s_s3, 1)
                if not fixed or k < NG:
                    y1.at(k * K1)
                    dve.wait_ge(s_lt, k + 1)
                    dve.wait_ge(s_mk[b % 2], (k - b % 2) * (8 * HH) + 16 * HH)
                    y1.chain(nc.vector.tensor_tensor_scan(F[:], mk[:, b % 2, 0, :], psL[:, 0:P], -BIG, ALU.add, ALU.max))
                    y1.chain(nc.vector.tensor_tensor_scan(M[:, b % 2, ::-1], mk[:, b % 2, 1, ::-1], F[:, ::-1], -BIG, ALU.add, ALU.max))
                    dve.sem_inc(s_s1, 1)
                if not fixed or k >= 2:
                    weigh(k - 2, (b - 2) % NB)

            def weigh(g, b):
                nwin, base = kept[b] if b < NB - 2 else load_group(nc, m, dve, g)
                yc.at(g * KC + base * KX)
                dve.wait_ge(s_ohu, (base + 1) * U)
                if gat:
                    yc.chain(nc.vector.tensor_tensor(Gp[:, :, H * SW:AW], uh(mxs(b)),
                                                     m.lastE[:, bass.ds(g * U, U)].unsqueeze(2).broadcast_to([P, U, H]), ALU.mult))
                    dve.wait_ge(s_p, g + 1)
                    pw = heads(Gp[:, :, 0:H * SW])
                    nc.vector.tensor_copy(pw[:, :, :, HC], uh(p[:]))
                    yc.chain(nc.vector.tensor_tensor(pw[:, :, :, 0:HC], heads(G[:, b, :, :])[:, :, :, 0:HC],
                                                     uh(p[:]).unsqueeze(3).broadcast_to([P, U, H, HC]), ALU.mult))
                    dve.sem_inc(s_gp, 1)
                yc.chain(nc.vector.tensor_scalar(scol[:], psF(b), m.rcol[:, bass.ds(g, 1)], None, ALU.mult))
                yc.chain(nc.vector.tensor_scalar(rel[:], m.dstF[:, bass.ds(g * U, U)], m.d0rep[:, bass.ds(g, 1)],
                                                 None, ALU.subtract))
                k0 = yc.k
                assert k0 == KC, k0
                if not gat:
                    dve.wait_ge(s_p, g + 1)
                hold(m, dve)
                with dve.Fori(0, nwin) as i:
                    yc.at(g * KC + k0 + (base + i) * KX)
                    for u in range(U):
                        dve.wait_ge(s_ohu, (base + i) * U + u + 1)
                        if gat:
                            nc.vector.tensor_scalar(oh[:, u, :], m.iota[:], rel[:, u:u + 1], None, ALU.is_equal).then_inc(s_oh, 1)
                        else:
                            nc.vector.tensor_scalar(oh[:, u, :], m.iota[:], rel[:, u:u + 1], p[:, 0, u:u + 1],
                                                    ALU.is_equal, ALU.mult).then_inc(s_oh, 1)
                        if u == U - 2:
                            yc.chain(nc.vector.tensor_copy(S[:, :, 0], scol[:]))
                            dve.sem_inc(s_S, 1)
                    yc.chain(nc.vector.memset(scol[:], 0.0))
                    dve.wait_ge(s_oh, (base + i + 1) * U)
                    yc.chain(nc.vector.tensor_scalar(rel[:], rel[:], float(P), None, ALU.subtract))
                    assert yc.k == KX

            skewed(dve, body)

        @block.tensor
        def _(pe):
            pe.sem_inc(s_pa, 1)
            pe.sem_inc(s_ohu, U)

            kept = {}

            def body(k, b):
                fixed = isinstance(k, int)
                if not fixed or k < NG:
                    nwin, base = kept[b] = load_group(nc, m, pe, k)
                    with pe.Fori(0, nwin) as i:
                        pe.wait_ge(s_win, (base + i) * 16 + 16)
                        pe.wait_ge(s_oht, base + i + 1)
                        for u in range(U):
                            if gat:
                                last = nc.tensor.matmul(psA[:, 0, u * H:u * H + H], ohT[:, u * P:u * P + P], win[:], start=True, stop=True)
                            else:
                                pe.wait_ge(s_pu, (base + i) * U + u + 1)
                                nc.tensor.matmul(psA[:, u % NA, 0:WW], ohT[:, u * P:u * P + P], win[:],
                                                 start=True, stop=True).then_inc(s_pa, 1)
                        if gat:
                            last.then_inc(s_pa, 1)
                if not fixed or 1 <= k <= NG:
                    pe.wait_ge(s_s2, k)
                    hold(m, pe)
                    nc.tensor.matmul(psY[:, 0:1], flat(Tf[:]), m.ones[0:1, 0:1], start=True, stop=True)
                    nc.tensor.matmul(psY[:, 1:2], flat(Tm[:]), m.ones[0:1, 0:1], start=True, stop=True).then_inc(s_tt, 1)
                if not fixed or k < NG:
                    pe.wait_ge(s_L, k + 1)
                    hold(m, pe)
                    nc.tensor.transpose(psL[:, 0:P], L[:, b].rearrange("p h u -> p (h u)"), m.ident[:]).then_inc(s_lt, 1)
                if not fixed or 1 <= k <= NG:
                    pe.wait_ge(s_fac, k + 1)
                    nc.tensor.matmul(psF(b - 1), m.ones[0:1, :], fac[:], start=True, stop=True)
                    pe.wait_ge(s_s3, k + 2)
                    hold(m, pe)
                    q = (b - 1) % 2
                    nc.tensor.transpose(psM[:, q, 0:HU], M[:, q, :], m.ident[0:HU, 0:HU]).then_inc(s_mb, 1)
                if not fixed or k < NG:
                    pe.wait_ge(s_s1, k + 1)
                    hold(m, pe)
                    nc.tensor.matmul(psX[:, 0:HU], M[:, b % 2, 0:1], m.ident[0:HU, 0:HU], start=True, stop=True)
                    nc.tensor.matmul(psX[:, HU:2 * HU], M[:, b % 2, P - 1:P], m.ident[0:HU, 0:HU], start=True, stop=True).then_inc(s_fl, 1)
                if not fixed or k >= 2:
                    g, bc = k - 2, (b - 2) % NB
                    nwin2, base2 = kept[bc] if bc < NB - 2 else load_group(nc, m, pe, g)
                    if gat:
                        pe.wait_ge(s_gp, g + 1)
                    hold(m, pe)
                    with pe.Fori(0, nwin2) as i:
                        pe.wait_ge(s_ev, base2 + i + 1)
                        for u in range(U):
                            if u == U - 1:
                                pe.wait_ge(s_S, base2 + i + 1)
                                for h in range(HH):
                                    nc.tensor.matmul(ps[:, h * SW:h * SW + SW], S[:, h, :], stage[:, h * SW:h * SW + SW],
                                                     start=False, stop=False)
                            pe.wait_ge(s_oh, (base2 + i) * U + u + 1)
                            rhs = Gp[:, u, :] if gat else G[:, bc, u, 0:AW]
                            nc.tensor.matmul(ps[:, 0:AW], oh[:, u, :], rhs, start=(u == 0), stop=(u == U - 1)).then_inc(s_ohu, 1)

            skewed(pe, body)

        @block.scalar
        def _(act):
            act.sem_inc(s_ev, 1)
            act.sem_inc(s_done, NB)
            act.sem_inc(s_st, 16)
            act.sem_inc(s_fac, 1)

            def body(k, factors=True, sums=True):
                if factors:
                    act.wait_ge(s_s2, k)
                    nc.scalar.activation(fac[:], dif[:], ACT.Exp).then_inc(s_fac, 1)
                if sums:
                    d0, nwin, base = load_group(nc, m, act, k - 2, True)
                    act.wait_ge(s_z, k - 1)
                    nc.scalar.activation(p[:], z[:], ACT.Exp).then_inc(s_p, 1)
                    store_windows(nc, m, act, d0, nwin, base, AW, ps, stage, s_ohu, s_st, s_ev)
                    act.wait_ge(s_ohu, (base + nwin + 1) * U)
                    act.sem_inc(s_done, 1)

            body(1, sums=False)
            with act.Fori(2, NG + 1) as k:
                body(k)
            body(NG + 1, factors=False)
            nwin, base = load_group(nc, m, act, NG - 1)
            act.wait_ge(s_st, (base + nwin) * 16 + 16)
            hold(m, act)


def node_phase(nc, m, tag, body):
    with ExitStack() as c:
        sb = lambda n, s, d=F32: c.enter_context(nc.sbuf_tensor(tag + n, s, d))
        sem = semaphores(nc, c, tag)
        psb = lambda n, s: c.enter_context(nc.psum_tensor(tag + n, s, F32))
        parts = body(nc, m, sb, sem, psb)
        block = c.enter_context(nc.Block())

        @block.sync
        def _(sp):
            with sp.Fori(0, NT) as t:
                parts["sp"](sp, t)

        @block.scalar
        def _(act):
            with act.Fori(0, NT) as t:
                parts["act"](act, t)

        @block.vector
        def _(dve):
            with dve.Fori(0, NT) as t:
                parts["dve"](dve, t)

        @block.tensor
        def _(pe):
            with pe.Fori(0, NT) as t:
                parts["pe"](pe, t)


def tile(table, t, width=D, at=0):
    return table[bass.ds(t * P, P), at:at + width]


def two_transposes(nc, m, psT, src):
    for k in range(2):
        last = nc.tensor.transpose(psT[:, k * P:k * P + P], src[:, k * P:k * P + P], m.ident[:])
    return last


def products(nc, m, pe, act, t, s, psT, psO, lt, rounds):
    R = len(rounds)
    for j, (src, rhs, n) in enumerate(rounds):
        if pe is not None:
            pe.wait_ge(s.ready, t * R + j + 1)
            for k in range(2):
                last = nc.tensor.transpose(psT[:, k * P:k * P + P], src[:, k * P:k * P + P], m.ident[:])
            last.then_inc(s.turned, 1)
            pe.wait_ge(s.copied, t * R + j + 1)
            for k in range(2):
                last = nc.tensor.matmul(psO[:, 0:n], lt[:, k * P:k * P + P], rhs[:, k, 0:n], start=(k == 0), stop=(k == 1))
            last.then_inc(s.product, 1)
        else:
            act.wait_ge(s.turned, t * R + j + 1)
            nc.scalar.activation(lt[:], psT[:, 0:D], ACT.Copy).then_inc(s.copied, 1)


def gcn_nodes(layer):
    def body(nc, m, sb, sem, psb):
        ag, tt_, res, o1, o2 = (sb(n, [P, D]) for n in ("ag", "tt", "res", "o1", "o2"))
        xin, hb, nb, lt = (sb(n, [P, D]) for n in ("xin", "hb", "nb", "lt"))
        t3 = sb("t3", [P, AGW])
        st, mv, sd, r = sb("st", [P, 6]), sb("mv", [P, 2]), sb("sd", [P, 1]), sb("r", [P, 1])
        psT, psO = psb("psT", [P, 512]), psb("psO", [P, 512])
        s = Shared()
        s.loaded, s.stored, s.chained, s.ready, s.turned = (sem(n) for n in ("loaded", "stored", "chained", "ready", "turned"))
        s.copied, s.product, s.variance, s.deviation, s.result = (
            sem(n) for n in ("copied", "product", "variance", "deviation", "result"))
        w = m.w6 if layer == 1 else m.w7
        table, resid = (m.t1, m.h0) if layer == 1 else (m.t2, m.x1)
        bias = m.row("b6" if layer == 1 else "b7")
        rounds = [(ag, w, D)] if layer == 1 else [(ag, w, D), (o1, m.wp, D), (hb, m.gw, AGW)]
        R = len(rounds)
        KV = 10

        def sp_part(sp, t):
            loads = [(ag, m.agg), (tt_, table), (res, resid)] + ([(xin, m.x)] if layer == 2 else [])
            for to, fr in loads:
                sp.dma_start(to[:], tile(fr, t)).then_inc(s.loaded, 16)
            sp.wait_ge(s.result, t + 1)
            if layer == 1:
                sp.dma_start(tile(m.x1, t), o1[:]).then_inc(s.stored, 16)
                sp.dma_start(tile(m.t2, t), o2[:]).then_inc(s.stored, 16)
                sp.wait_ge(s.stored, t * 32 + 32)
                hold(m, sp)
            else:
                sp.dma_start(tile(m.xa, t), o2[:]).then_inc(s.stored, 16)
                sp.dma_start(tile(m.t3, t, ROW), t3[:, 0:ROW]).then_inc(s.stored, 16)
                sp.dma_start(tile(m.ad, t, H), t3[:, ROW:AGW]).then_inc(s.stored, 16)
                sp.wait_ge(s.stored, t * 48 + 48)
                hold(m, sp)

        def dve_part(dve, t):
            y = Tally(dve, s.chained)
            y.at(t * KV)
            dve.wait_ge(s.loaded, t * (48 if layer == 1 else 64) + (48 if layer == 1 else 64))
            y.chain(nc.vector.tensor_tensor(ag[:], ag[:], tt_[:], ALU.add))
            dve.sem_inc(s.ready, 1)
            dve.wait_ge(s.product, t * R + 1)
            y.chain(nc.vector.scalar_tensor_tensor(o1[:], psO[:, 0:D], m.dis[:, bass.ds(t, 1)], bias, ALU.mult, ALU.add))
            y.chain(nc.vector.scalar_tensor_tensor(o1[:], o1[:], 0.0, res[:], ALU.max, ALU.add))
            if layer == 2:
                dve.sem_inc(s.ready, 1)
            src = o1
            if layer == 2:
                dve.wait_ge(s.product, t * R + 2)
                y.chain(nc.vector.tensor_tensor(o2[:], psO[:, 0:D], m.row("bp"), ALU.add))
                y.chain(nc.vector.tensor_tensor(o2[:], o2[:], xin[:], ALU.add))
                src = o2
            y.chain(nc.vector.bn_stats(st[:], src[:]))
            hold(m, dve)
            y.chain(nc.vector.bn_aggr(mv[:], st[:]))
            dve.sem_inc(s.variance, 1)
            dve.wait_ge(s.deviation, t + 1)
            y.chain(nc.vector.reciprocal(r[:], sd[:]))
            if layer == 1:
                y.chain(nc.vector.tensor_tensor(r[:], r[:], m.dis[:, bass.ds(t, 1)], ALU.mult))
                y.chain(nc.vector.tensor_scalar(nb[:], o1[:], mv[:, 0:1], r[:, 0:1], ALU.subtract, ALU.mult))
                y.chain(nc.vector.tensor_tensor(nb[:], nb[:], m.row("g7"), ALU.mult))
                y.chain(nc.vector.scalar_tensor_tensor(o2[:], m.row("c7"), m.dis[:, bass.ds(t, 1)], nb[:],
                                                       ALU.mult, ALU.add))
                dve.sem_inc(s.result, 1)
            else:
                y.chain(nc.vector.tensor_scalar(nb[:], o2[:], mv[:, 0:1], r[:, 0:1], ALU.subtract, ALU.mult))
                y.chain(nc.vector.tensor_scalar(hb[:], nb[:], 0.0, None, ALU.max))
                dve.sem_inc(s.ready, 1)
            assert y.k == KV, y.k

        def pe_part(pe, t):
            products(nc, m, pe, None, t, s, psT, psO, lt, rounds)

        def act_part(act, t):
            for j in range(R):
                act.wait_ge(s.turned, t * R + j + 1)
                nc.scalar.activation(lt[:], psT[:, 0:D], ACT.Copy).then_inc(s.copied, 1)
                if j == min(1, R - 1):
                    act.wait_ge(s.variance, t + 1)
                    nc.scalar.activation(sd[:], mv[:, 1:2], ACT.Sqrt, bias=m.eps[:, 0:1]).then_inc(s.deviation, 1)
            if layer == 2:
                act.wait_ge(s.product, t * R + R)
                nc.scalar.activation(t3[:], psO[:, 0:AGW], ACT.Copy).then_inc(s.result, 1)

        return dict(sp=sp_part, dve=dve_part, pe=pe_part, act=act_part)
    return body


def gat_nodes(nc, m, sb, sem, psb):
    ag, own, ad = sb("ag", [P, AGW]), sb("own", [P, ROW]), sb("ad", [P, H])
    v, v2 = sb("v", [P, D]), sb("v2", [P, D])
    t4, lt, q = sb("t4", [P, ROW]), sb("lt", [P, D]), sb("q", [P, D + 1])
    mx, ls, m2, ab, sm, rs = (sb(n, [P, H]) for n in ("mx", "ls", "m2", "ab", "sm", "rs"))
    e = sb("e", [P, 2, H])
    psT, psO = psb("psT", [P, 512]), psb("psO", [P, 512])
    s_set, s_loaded, s_stored, s_chained, s_exps, s_exp, s_ready, s_turned, s_copied, s_product, s_q = (
        sem(n) for n in ("set", "loaded", "stored", "chained", "exps", "exp", "ready", "turned", "copied", "product", "q"))
    KV = 20
    hv = lambda t_: t_[:, 0:H * (HC + 1)].rearrange("p (h c) -> p h c", h=H)
    wide = lambda t_: t_[:].rearrange("p (h c) -> p h c", h=H)
    each = lambda t_: t_.unsqueeze(2).broadcast_to([P, H, HC])

    def sp_part(sp, t):
        for to, fr, n in ((ag, m.agg, AGW), (own, m.t3, ROW), (ad, m.ad, H)):
            sp.dma_start(to[:], tile(fr, t, n)).then_inc(s_loaded, 16)
        sp.wait_ge(s_q, t + 1)
        sp.dma_start(tile(m.t4, t, ROW), t4[:]).then_inc(s_stored, 16)
        sp.dma_start(tile(m.qk, t, D + 1), q[:]).then_inc(s_stored, 16)
        sp.wait_ge(s_stored, t * 32 + 32)
        hold(m, sp)

    def dve_part(dve, t):
        y = Tally(dve, s_chained)
        y.at(t * KV)
        dve.wait_ge(s_loaded, t * 48 + 48)
        sums = hv(ag)[:, :, HC]
        y.chain(nc.vector.tensor_scalar(mx[:], sums, 0.0, -BIG, ALU.is_equal, ALU.mult))
        y.chain(nc.vector.tensor_tensor(mx[:], mx[:], ag[:, H * (HC + 1):AGW], ALU.add))
        y.chain(nc.vector.tensor_tensor(ls[:], hv(own)[:, :, HC], ad[:], ALU.add))
        y.chain(nc.vector.scalar_tensor_tensor(ls[:], ls[:], 0.2, ls[:], ALU.mult, ALU.max))
        y.chain(nc.vector.tensor_tensor(m2[:], mx[:], ls[:], ALU.max))
        y.chain(nc.vector.tensor_tensor(e[:, 0, :], mx[:], m2[:], ALU.subtract))
        y.chain(nc.vector.tensor_tensor(e[:, 1, :], ls[:], m2[:], ALU.subtract))
        dve.sem_inc(s_exps, 1)
        dve.wait_ge(s_exp, t + 1)
        y.chain(nc.vector.tensor_tensor(ab[:], sums, e[:, 0, :], ALU.mult))
        y.chain(nc.vector.tensor_tensor(sm[:], ab[:], e[:, 1, :], ALU.add))
        y.chain(nc.vector.tensor_scalar(sm[:], sm[:], 1e-16, None, ALU.add))
        y.chain(nc.vector.reciprocal(rs[:], sm[:]))
        y.chain(nc.vector.tensor_tensor(e[:], e[:], rs[:].unsqueeze(1).broadcast_to([P, 2, H]), ALU.mult))
        y.chain(nc.vector.tensor_tensor(wide(v), hv(ag)[:, :, 0:HC], each(e[:, 0, :]), ALU.mult))
        y.chain(nc.vector.tensor_tensor(wide(v2), hv(own)[:, :, 0:HC], each(e[:, 1, :]), ALU.mult))
        y.chain(nc.vector.tensor_tensor(v[:], v[:], v2[:], ALU.add))
        y.chain(nc.vector.tensor_tensor(v[:], v[:], m.row("gat_bias"), ALU.add))
        y.chain(nc.vector.scalar_tensor_tensor(v2[:], v[:], 0.0, m.row("prelu1"), ALU.min, ALU.mult))
        y.chain(nc.vector.scalar_tensor_tensor(t4[:, 0:D], v[:], 0.0, v2[:], ALU.max, ALU.add))
        y.chain(nc.vector.memset(t4[:, D:ROW], 1.0))
        dve.sem_inc(s_ready, 1)
        y.chain(nc.vector.memset(mx[:], 0.0))
        assert y.k == KV, y.k

    def pe_part(pe, t):
        pe.wait_ge(s_ready, t + 1)
        for k in range(2):
            last = nc.tensor.transpose(psT[:, k * P:k * P + P], t4[:, k * P:k * P + P], m.ident[:])
        last.then_inc(s_turned, 1)
        pe.wait_ge(s_copied, t + 1)
        for k in range(2):
            nc.tensor.matmul(psO[:, 0:D + 1], lt[:, k * P:k * P + P], m.wqk[:, k, :], start=(k == 0), stop=False)
        nc.tensor.matmul(psO[:, 0:D + 1], m.ones[0:1, :], m.bqk[:], start=False, stop=True).then_inc(s_product, 1)

    def act_part(act, t):
        act.wait_ge(s_exps, t + 1)
        nc.scalar.activation(e[:], e[:], ACT.Exp).then_inc(s_exp, 1)
        act.wait_ge(s_turned, t + 1)
        nc.scalar.activation(lt[:], psT[:, 0:D], ACT.Copy).then_inc(s_copied, 1)
        act.wait_ge(s_product, t + 1)
        nc.scalar.activation(q[:], psO[:, 0:D + 1], ACT.Copy).then_inc(s_q, 1)

    return dict(sp=sp_part, dve=dve_part, pe=pe_part, act=act_part)


def out_nodes(nc, m, sb, sem, psb):
    ag, t4, xa = sb("ag", [P, D + 1]), sb("t4", [P, ROW]), sb("xa", [P, D])
    an, lt, sa, v, o = sb("an", [P, D + 1]), sb("lt", [P, 4, P]), sb("sa", [1, P]), sb("v", [P, D]), sb("o", [P, D])
    rs = sb("rs", [P, 1])
    psT, psS, psO = psb("psT", [P, 4, P]), psb("psS", [P, 512]), psb("psO", [P, 512])
    s_loaded, s_stored, s_chained, s_ready, s_turned, s_copied, s_product, s_out = (
        sem(n) for n in ("loaded", "stored", "chained", "ready", "turned", "copied", "product", "out"))
    KV = 6

    def sp_part(sp, t):
        for to, fr, n in ((ag, m.agg, D + 1), (t4, m.t4, ROW), (xa, m.xa, D)):
            sp.dma_start(to[:], tile(fr, t, n)).then_inc(s_loaded, 16)
        sp.wait_ge(s_out, t + 1)
        sp.dma_start(tile(m.out, t), o[:]).then_inc(s_stored, 16)
        sp.wait_ge(s_stored, t * 16 + 16)
        hold(m, sp)

    def dve_part(dve, t):
        y = Tally(dve, s_chained)
        y.at(t * KV)
        dve.wait_ge(s_loaded, t * 48 + 48)
        y.chain(nc.vector.tensor_scalar(rs[:], ag[:, D:D + 1], 1e-16, None, ALU.add))
        y.chain(nc.vector.reciprocal(rs[:], rs[:]))
        y.chain(nc.vector.tensor_scalar(an[:], ag[:], rs[:, 0:1], None, ALU.mult))
        dve.sem_inc(s_ready, 1)
        dve.wait_ge(s_product, t + 1)
        y.chain(nc.vector.scalar_tensor_tensor(v[:], psO[:, 0:D], 0.0, m.row("prelu2"), ALU.min, ALU.mult))
        y.chain(nc.vector.scalar_tensor_tensor(o[:], psO[:, 0:D], 0.0, v[:], ALU.max, ALU.add))
        y.chain(nc.vector.tensor_tensor(o[:], o[:], xa[:], ALU.add))
        dve.sem_inc(s_out, 1)
        assert y.k == KV

    def pe_part(pe, t):
        pe.wait_ge(s_ready, t + 1)
        for j, src in enumerate((an, an, t4, t4)):
            nc.tensor.transpose(psT[:, j, :], src[:, (j % 2) * P:(j % 2) * P + P], m.ident[:])
        nc.tensor.transpose(psS[0:1, 0:P], an[:, D:D + 1], m.ident[:]).then_inc(s_turned, 1)
        pe.wait_ge(s_copied, t * 2 + 2)
        for j in range(4):
            nc.tensor.matmul(psO[:, 0:D], lt[:, j, :], (m.wv, m.wsk)[j // 2][:, j % 2, :], start=(j == 0), stop=False)
        nc.tensor.matmul(psO[:, 0:D], sa[:], m.bv[:], start=False, stop=False)
        nc.tensor.matmul(psO[:, 0:D], m.ones[0:1, :], m.bsk[:], start=False, stop=True).then_inc(s_product, 1)

    def act_part(act, t):
        act.wait_ge(s_turned, t + 1)
        nc.scalar.activation(lt[:], psT[:], ACT.Copy).then_inc(s_copied, 1)
        nc.scalar.activation(sa[:], psS[0:1, 0:P], ACT.Copy).then_inc(s_copied, 1)

    return dict(sp=sp_part, dve=dve_part, pe=pe_part, act=act_part)


def build(nc, a, out):
    with ExitStack() as c:
        sb = lambda n, s, d=F32: c.enter_context(nc.sbuf_tensor(n, s, d))
        m = Shared()
        m.ROWS = ("g6", "c6", "b6", "g7", "c7", "b7", "bp", "gat_bias", "prelu1", "prelu2")
        m.ident, m.ones, m.iota = sb("ident", [P, P]), sb("ones", [P, P]), sb("iota", [P, P])
        m.iotap, m.eps, m.t4one = sb("iotap", [P, 1]), sb("eps", [P, 1]), sb("t4one", [1, 1])
        m.srcI = sb("srcI", [P, NC + LEAD * U], I32)
        m.dstF, m.wF, m.lastE, m.hiF, m.loF = (sb(n, [P, NC]) for n in ("dstF", "wF", "lastE", "hiF", "loF"))
        m.d0rep, m.rcol = sb("d0rep", [P, NG]), sb("rcol", [P, NG])
        m.cont, m.runf, m.runb = sb("cont", [1, NC]), sb("runf", [1, NG * H * (U + 1)]), sb("runb", [1, NG * H * U])
        m.ctl = sb("ctl", [1, NG * 3], I32)
        m.dis = sb("dis", [P, NT])
        m.w6, m.w7, m.wp, m.wv, m.wsk = (sb(n, [P, 2, D]) for n in ("w6", "w7", "wp", "wv", "wsk"))
        m.gw, m.wqk = sb("gw", [P, 2, AGW]), sb("wqk", [P, 2, D + 1])
        m.bqk, m.bv, m.bsk = sb("bqk", [1, D + 1]), sb("bvr", [1, D]), sb("bskr", [1, D])
        m.rows = sb("rows", [P, len(m.ROWS), D])
        m.row = lambda n: m.rows[:, m.ROWS.index(n), :]
        dram = lambda n, s: nc.dram_tensor(n, s, F32, kind="Internal").ap()
        m.x, m.out = a["x"], out
        m.h0, m.x1, m.xa, m.t1, m.t2 = (dram(n, (NP, D)) for n in ("h0", "x1", "xa", "t1", "t2"))
        m.t3, m.t4 = dram("t3", (NP, ROW)), dram("t4", (NP, ROW))
        m.ad, m.qk = dram("ad", (NW, H)), dram("qk", (NW, D + 1))
        m.agg = dram("agg", (NW, AGW))
        m.masks, m.dstf = dram("masks", (4, NC * P)), dram("dstf", (NC * P,))
        m.held = {str(e.engine): c.enter_context(nc.semaphore(f"held{k}"))
                  for k, e in enumerate((nc.sync, nc.scalar, nc.vector, nc.tensor, nc.gpsimd))}
        load_all(nc, m, a)
        degrees(nc, m)
        first_rows(nc, m, a["x"])
        gcn_pass(nc, m, "g1_", m.t1)
        node_phase(nc, m, "n1_", gcn_nodes(1))
        gcn_pass(nc, m, "g2_", m.t2)
        node_phase(nc, m, "n2_", gcn_nodes(2))
        softmax_pass(nc, m, "g3_", m.t3, m.ad, True)
        node_phase(nc, m, "n3_", gat_nodes)
        softmax_pass(nc, m, "g4_", m.t4, m.qk, False)
        node_phase(nc, m, "n4_", out_nodes)


def kernel(**inputs):
    import numpy as np
    import concourse.bacc as bacc
    from concourse.bass_utils import run_bass_kernel_spmd as run
    i = {k: np.asarray(v) for k, v in inputs.items()}
    L0 = lambda n: i["L0_gnn_" + n]
    L1 = lambda n: i["L1_gnn_" + n]
    pad = NC * P - E
    dst = np.concatenate([np.full(1, -2, np.int32), i["dst"], np.full(pad + 1, -1, np.int32)])
    src = np.concatenate([i["src"], np.zeros(pad + LEAD * GE, np.int32)])
    w = np.concatenate([i["edge_weight"], np.zeros(pad, np.float32)])
    nxt = dst[2:].copy().reshape(NG, GE)
    nxt[:, -1] = -3
    cols = lambda v: np.ascontiguousarray(v.reshape(-1, P).T)
    att = np.zeros((D, 2 * H), np.float32)
    for h in range(H):
        att[h * HC:(h + 1) * HC, h] = L1("att_src")[h]
        att[h * HC:(h + 1) * HC, H + h] = L1("att_dst")[h]
    arrays = {
        "x": np.concatenate([i["x"], np.zeros((NP - N, D), np.float32)]),
        "dst_flat": dst, "src_cols": cols(src), "dst_cols": cols(dst[1:1 + NC * P]), "next_cols": cols(nxt), "w_cols": cols(w),
        "W6T": L0("W6").T, "W7T": L0("W7").T, "WpT": L0("Wp").T,
        "gat_W": L1("gat_W"), "gat_WT": L1("gat_W").T, "att": att, "WqT": L1("Wq").T,
        "WkTb": np.concatenate([L1("Wk").T, L1("bk")[:, None]], axis=1), "Wv": L1("Wv"), "Wskip": L1("Wskip"),
        "bq": L1("bq"), "bv": L1("bv"), "bskip": L1("bskip"),
        "g6": L0("ln6_g"), "c6": L0("ln6_b"), "b6": L0("b6"), "g7": L0("ln7_g"), "c7": L0("ln7_b"), "b7": L0("b7"),
        "bp": L0("bp"), "gat_bias": L1("gat_bias"), "prelu1": L1("prelu1_a"), "prelu2": L1("prelu2_a"),
    }
    nc = bacc.Bacc("TRN2", target_bir_lowering=False, num_devices=1)
    ins = {k + "_in": np.ascontiguousarray(v) for k, v in arrays.items()}
    aps = {k[:-3]: nc.dram_tensor(k, v.shape, mybir.dt.from_np(v.dtype), kind="ExternalInput").ap() for k, v in ins.items()}
    out = nc.dram_tensor("out", (NP, D), F32, kind="ExternalOutput").ap()
    build(nc, aps, out)
    return run(nc, [ins], core_ids=[0]).results[0]["out"][:N]
```

```python
from contextlib import ExitStack

import concourse.bass as bass
from concourse import mybir

F32 = mybir.dt.float32
I32 = mybir.dt.int32
ALU = mybir.AluOpType
ACT = mybir.ActivationFunctionType
P = 128
N = 6250
E = 106250
D = 256
H = 4
HC = D // H
U = 8
GE = U * P
NG = -(-E // GE)
NC = NG * U
NT = -(-N // P)
NP = NT * P
NW = NP + P
NB = 8
NBG = 4
ROW = 260
AGW = 264
BT = 7
LN_EPS = 1e-5
BIG = 1.0e30
LEAD = 4
IOA = bass.IndirectOffsetOnAxis
WINDOW_FITS = "a group's windows end less than P nodes after the next group's first node"


class Shared:
    pass


class Tally:

    def __init__(self, eng, sem):
        self.eng, self.sem, self.base, self.k = eng, sem, 0, 0

    def at(self, base):
        self.base, self.k = base, 0

    def chain(self, ins):
        self.k += 1
        ins.then_inc(self.sem, 1)
        self.eng.wait_ge(self.sem, self.base + self.k)
        return ins


def semaphores(nc, c, tag):
    sems = []

    def release():
        nc.clear_and_free_semaphores(sems)
        nc.all_engine_barrier()

    def sem(name):
        sems.append(nc.alloc_semaphore(tag + name))
        return sems[-1]

    c.callback(release)
    return sem


def hold(m, eng):
    eng.sem_inc(m.held[str(eng.engine)], 1)


def load_group(nc, m, eng, g, first=False):
    return [eng.value_load(m.ctl[0:1, bass.ds(g * 3 + k, 1)], min_val=lo, max_val=hi)
            for k, lo, hi in ((0, 0, N - 1), (1, 1, NT), (2, 0, NG + NT))[not first:]]


def window_start(nc, d0, i):
    return nc.s_assert_within(d0 + i * P, 0, NP - 1, skip_runtime_bounds_check_because=WINDOW_FITS)


def load_all(nc, m, a):
    with ExitStack() as c:
        sb = lambda n, s, d=F32: c.enter_context(nc.sbuf_tensor("in_" + n, s, d))
        sem = semaphores(nc, c, "in_")
        pt = c.enter_context(nc.psum_tensor("in_ps", [P, 4, 512], F32))
        dstR, nxtR = sb("dstR", [P, NC], I32), sb("nxtR", [P, NC], I32)
        hiI = sb("hiI", [P, NC], I32)
        rowsI = sb("rowsI", [NG, 3, GE], I32)
        rowsF = sb("rowsF", [NG, 3, GE])
        mks = sb("mks", [NG, 4, GE])
        endI, endF = sb("endI", [1, 2, NC + 1], I32), sb("endF", [1, 2, NC + 1])
        con, sgl, rf = sb("con", [1, NC + 1]), sb("sgl", [1, NC]), sb("rf", [1, NC])
        d0i = sb("d0i", [1, NG + 1], I32)
        d0f = sb("d0f", [1, NG + 1])
        spn = sb("spn", [1, NG], I32)
        rem = sb("rem", [1, NG + 1], I32)
        remf = sb("remf", [1, NG + 1])
        nwf, zero, incl, bas = (sb(n, [1, NG]) for n in ("nwf", "zero", "incl", "bas"))
        gw = sb("gw", [P, 2, D])
        zrow = sb("zrow", [P, D + 1])
        gwT, att, wqT, wkb, bqc = (sb("gwT", [P, 2, D]), sb("att", [P, 2, 2 * H]), sb("wqT", [P, 2, D]),
                                   sb("wkb", [P, 2, D + 1]), sb("bqc", [P, 2]))
        s_set, s_ld, s_w, s_v, s_cast, s_pe, s_st, s_seg, s_rd = (
            sem(n) for n in ("set", "ld", "w", "v", "cast", "pe", "st", "seg", "rd"))
        block = c.enter_context(nc.Block())

        @block.gpsimd
        def _(pool):
            nc.gpsimd.memset(m.ident[:], 0.0).then_inc(s_set, 1)
            nc.gpsimd.memset(m.ones[:], 1.0)
            nc.gpsimd.memset(zrow[:], 0.0)
            nc.gpsimd.memset(m.eps[:], LN_EPS)
            nc.gpsimd.iota(m.iota[:], [[1, P]], base=0, channel_multiplier=0,
                           allow_small_or_imprecise_dtypes=True)
            nc.gpsimd.iota(m.iotap[:], [[1, 1]], base=0, channel_multiplier=1,
                           allow_small_or_imprecise_dtypes=True).then_inc(s_set, 1)
            pool.wait_ge(s_set, 2)
            nc.gpsimd.affine_select(out=m.ident[:], in_=m.ident[:], compare_op=ALU.not_equal, fill=1.0,
                                    base=0, pattern=[[-1, P]], channel_multiplier=1).then_inc(s_set, 1)

        @block.sync
        def _(sp):
            sp.dma_start(dstR[:], a["dst_cols"]).then_inc(s_ld, 16)
            sp.dma_start(nxtR[:], a["next_cols"]).then_inc(s_ld, 16)
            for k in range(3):
                sp.dma_start(rowsI[:, k, :], a["dst_flat"][k:k + NC * P].rearrange("(g e) -> g e", e=GE)).then_inc(s_ld, 16)
            with nc.allow_non_contiguous_dma(reason="first destination of each group"):
                sp.dma_start(d0i[0:1, 0:NG], a["dst_flat"][1:1 + NC * P].rearrange("(a g e) -> a g e", a=1, e=GE)[:, :, 0]).then_inc(s_ld, 16)
                sp.dma_start(endI[0:1, 0, 0:NC], a["dst_flat"][1:1 + NC * P].rearrange("(a c e) -> a c e", a=1, e=P)[:, :, 0]).then_inc(s_ld, 16)
                sp.dma_start(endI[0:1, 0, NC:NC + 1], a["dst_flat"][0:1].rearrange("(a c) -> a c", a=1)).then_inc(s_ld, 16)
                sp.dma_start(endI[0:1, 1, 0:NC], a["dst_flat"][0:NC * P].rearrange("(a c e) -> a c e", a=1, e=P)[:, :, 0]).then_inc(s_ld, 16)
                sp.dma_start(endI[0:1, 1, NC:NC + 1], a["dst_flat"][NC * P:NC * P + 1].rearrange("(a c) -> a c", a=1)).then_inc(s_ld, 16)
            sp.dma_start(m.srcI[:], a["src_cols"]).then_inc(s_w, 16)
            sp.dma_start(m.wF[:], a["w_cols"]).then_inc(s_w, 16)
            for t_, n in ((m.w6, "W6T"), (m.w7, "W7T"), (m.wp, "WpT"), (gw, "gat_W"), (gwT, "gat_WT"), (att, "att"),
                          (wqT, "WqT"), (wkb, "WkTb"), (m.wv, "Wv"), (m.wsk, "Wskip")):
                sp.dma_start(t_[:], a[n].rearrange("(k p) n -> p k n", p=P)).then_inc(s_w, 16)
            with nc.allow_non_contiguous_dma(reason="a column of biases"):
                sp.dma_start(bqc[:], a["bq"].rearrange("(k p) -> p k", p=P)).then_inc(s_w, 16)
            for k, n in enumerate(m.ROWS):
                sp.dma_start(m.rows[:, k, :], a[n].partition_broadcast(P)).then_inc(s_w, 16)
            for t_, n in ((m.bv, "bv"), (m.bsk, "bskip")):
                sp.dma_start(t_[:], a[n].rearrange("(a n) -> a n", a=1)).then_inc(s_w, 16)
            sp.wait_ge(s_set, 3)
            sp.dma_start(m.ad[NP:NW, :], zrow[:, 0:H]).then_inc(s_st, 16)
            sp.dma_start(m.qk[NP:NW, :], zrow[:]).then_inc(s_st, 16)
            sp.wait_ge(s_seg, 1)
            sp.dma_start(m.masks.rearrange("k (g e) -> g k e", e=GE), mks[:]).then_inc(s_st, 16)
            sp.dma_start(m.dstf.rearrange("(g e) -> g e", e=GE), rowsF[:, 1, :]).then_inc(s_st, 16)
            sp.wait_ge(s_st, 64)
        NWL = 2 + 10 + 1 + len(m.ROWS) + 2

        @block.vector
        def _(dve):
            y = Tally(dve, s_v)
            dve.wait_ge(s_ld, 16 * 10)
            y.chain(nc.vector.tensor_copy(m.dstF[:], dstR[:]))
            nc.vector.tensor_copy(rowsF[:], rowsI[:])
            y.chain(nc.vector.tensor_tensor(m.lastE[:], dstR[:], nxtR[:], ALU.not_equal))
            y.chain(nc.vector.tensor_scalar(hiI[:], dstR[:], 7, None, ALU.arith_shift_right))
            y.chain(nc.vector.tensor_copy(m.hiF[:], hiI[:]))
            y.chain(nc.vector.scalar_tensor_tensor(m.loF[:], m.hiF[:], -float(P), m.dstF[:], ALU.mult, ALU.add))
            for k in (0, 1):
                y.chain(nc.vector.tensor_tensor(mks[:, k, :], rowsF[:, 1, :], rowsF[:, 2 * k, :], ALU.not_equal))
            rows = rowsF[:, 1, :].rearrange("g (u e) -> g u e", e=P)
            for k, e in ((2, 0), (3, P - 1)):
                y.chain(nc.vector.tensor_tensor(mks[:, k, :].rearrange("g (u e) -> g u e", e=P), rows,
                                                rows[:, :, e:e + 1].broadcast_to([NG, U, P]), ALU.not_equal))
            y.chain(nc.vector.tensor_scalar(mks[:], mks[:], -BIG, None, ALU.mult))
            nc.vector.memset(m.ctl[0:1, 0:1], 0).then_inc(s_seg, 1)
            y.chain(nc.vector.memset(d0i[0:1, 0:1], 0))
            y.chain(nc.vector.memset(d0i[0:1, NG:NG + 1], NP - 1))
            y.chain(nc.vector.tensor_tensor(spn[:], d0i[0:1, 1:NG + 1], d0i[0:1, 0:NG], ALU.subtract))
            y.chain(nc.vector.tensor_scalar(rem[0:1, 1:NG + 1], spn[:], P - 1, None, ALU.bitwise_and))
            y.chain(nc.vector.memset(rem[0:1, 0:1], -1))
            y.chain(nc.vector.tensor_copy(remf[:], rem[:]))
            y.chain(nc.vector.tensor_scalar(spn[:], spn[:], 7, None, ALU.arith_shift_right))
            y.chain(nc.vector.tensor_scalar(nwf[:], spn[:], 1.0, None, ALU.add))
            y.chain(nc.vector.memset(zero[:], 0.0))
            y.chain(nc.vector.tensor_tensor_scan(incl[:], nwf[:], zero[:], 0.0, ALU.add, ALU.add))
            y.chain(nc.vector.tensor_tensor(bas[:], incl[:], nwf[:], ALU.subtract))
            y.chain(nc.vector.tensor_copy(d0f[:], d0i[:]))
            y.chain(nc.vector.tensor_copy(endF[:], endI[:]))
            y.chain(nc.vector.memset(con[:], 0.0))
            y.chain(nc.vector.tensor_tensor(con[0:1, 0:NC], endF[0:1, 0, 0:NC], endF[0:1, 1, 0:NC], ALU.is_equal))
            y.chain(nc.vector.tensor_tensor(sgl[:], endF[0:1, 0, 0:NC], endF[0:1, 1, 1:NC + 1], ALU.is_equal))
            y.chain(nc.vector.tensor_scalar(m.cont[:], con[0:1, 0:NC], -1.0, BIG, ALU.add, ALU.mult))
            y.chain(nc.vector.memset(m.runf[:], -BIG))
            y.chain(nc.vector.memset(m.runb[:], -BIG))
            of = lambda t_: t_[0:1, 0:NC].rearrange("a (g u) -> a g u", u=U)
            fv = m.runf[:].rearrange("a (g h v) -> a g h v", h=H, v=U + 1)
            bv = m.runb[:].rearrange("a (g h u) -> a g h u", h=H, u=U)
            y.chain(nc.vector.tensor_tensor(rf[:], con[0:1, 0:NC], sgl[:], ALU.mult))
            y.chain(nc.vector.tensor_scalar(rf[:], rf[:], -1.0, BIG, ALU.add, ALU.mult))
            for h in range(H):
                y.chain(nc.vector.tensor_copy(fv[:, :, h, 1:U + 1], of(rf)))
            y.chain(nc.vector.tensor_tensor(rf[:], con[0:1, 1:NC + 1], sgl[:], ALU.mult))
            y.chain(nc.vector.tensor_scalar(rf[:], rf[:], -1.0, BIG, ALU.add, ALU.mult))
            for h in range(H):
                y.chain(nc.vector.tensor_copy(bv[:, :, h, 1:U], of(rf)[:, :, 0:U - 1][:, :, ::-1]))
            cv = m.ctl[0:1, :].rearrange("a (g k) -> a g k", k=3)
            y.chain(nc.vector.tensor_copy(cv[:, :, 0], d0i[0:1, 0:NG]))
            y.chain(nc.vector.tensor_copy(cv[:, :, 1], nwf[:]))
            y.chain(nc.vector.tensor_copy(cv[:, :, 2], bas[:]))
            dve.sem_inc(s_cast, 1)
            dve.wait_ge(s_pe, 1)
            nc.vector.tensor_copy(m.d0rep[:], pt[:, 0, 0:NG])
            nc.vector.tensor_scalar(m.rcol[:], pt[:, 1, 0:NG], m.iotap[:, 0:1], None, ALU.is_equal).then_inc(s_rd, 1)
            dve.wait_ge(s_w, 16 * NWL)
            dve.wait_ge(s_pe, 2)
            gv = m.gw[:, :, 0:H * (HC + 1)].rearrange("p k (h c) -> p k h c", h=H)
            for k in range(2):
                nc.vector.tensor_copy(gv[:, k, :, 0:HC], gw[:, k, :].rearrange("p (h c) -> p h c", h=H))
                nc.vector.tensor_copy(gv[:, k, :, HC], pt[:, 0, 16 * k:16 * k + H])
                nc.vector.tensor_copy(m.gw[:, k, H * (HC + 1):AGW], pt[:, 0, 16 * k + H:16 * k + 2 * H])
            dve.wait_ge(s_pe, 3)
            for k in range(2):
                nc.vector.tensor_scalar(m.wqk[:, k, :], pt[:, 2 + k, 0:D + 1], float(D) ** -0.5, None, ALU.mult)
            dve.wait_ge(s_pe, 4)
            y.chain(nc.vector.tensor_scalar(m.bqk[:], pt[0:1, 1, 0:D + 1], float(D) ** -0.5, None, ALU.mult))

        @block.tensor
        def _(pe):
            pe.wait_ge(s_set, 3)
            pe.wait_ge(s_cast, 1)
            nc.tensor.matmul(pt[:, 0, 0:NG], m.ones[0:1, :], d0f[0:1, 0:NG], start=True, stop=True)
            nc.tensor.matmul(pt[:, 1, 0:NG], m.ones[0:1, :], remf[0:1, 0:NG], start=True, stop=True).then_inc(s_pe, 1)
            pe.wait_ge(s_w, 16 * NWL)
            pe.wait_ge(s_rd, 1)
            for k in range(2):
                for j in range(2):
                    last = nc.tensor.matmul(pt[:, 0, 16 * k:16 * k + 2 * H], gwT[:, j, k * P:k * P + P], att[:, j, :],
                                            start=(j == 0), stop=(j == 1))
            last.then_inc(s_pe, 1)
            for k in range(2):
                for j in range(2):
                    last = nc.tensor.matmul(pt[:, 2 + k, 0:D + 1], wqT[:, j, k * P:k * P + P], wkb[:, j, :],
                                            start=(j == 0), stop=(j == 1))
            last.then_inc(s_pe, 1)
            for j in range(2):
                last = nc.tensor.matmul(pt[0:1, 1, 0:D + 1], bqc[:, j:j + 1], wkb[:, j, :], start=(j == 0), stop=(j == 1))
            last.then_inc(s_pe, 1)


def degrees(nc, m):
    with ExitStack() as c:
        sb = lambda n, s, d=F32: c.enter_context(nc.sbuf_tensor("dg_" + n, s, d))
        sem = semaphores(nc, c, "dg_")
        lo, hi = sb("lo", [P, 2, U, P]), sb("hi", [P, 2, U, NT])
        deg, sd, pos = sb("deg", [P, NT]), sb("sd", [P, NT]), sb("pos", [P, NT])
        zero = sb("zero", [P, P])
        ps = c.enter_context(nc.psum_tensor("dg_ps", [P, 512], F32))
        s_z, s_lo, s_eq, s_hi, s_mm, s_v, s_sd = (sem(n) for n in ("z", "lo", "eq", "hi", "mm", "v", "sd"))
        block = c.enter_context(nc.Block())

        @block.gpsimd
        def _(pool):
            nc.gpsimd.memset(zero[:], 0.0).then_inc(s_z, 1)

        @block.vector
        def _(dve):
            y = Tally(dve, s_v)
            with dve.Fori(0, NG // 2) as t:
                for b in range(2):
                    g = t * 2 + b
                    dve.wait_ge(s_mm, g + 1)
                    nc.vector.tensor_tensor(hi[:, b], m.iota[:, 0:NT].unsqueeze(1).broadcast_to([P, U, NT]),
                                            m.hiF[:, bass.ds(g * U, U)].unsqueeze(2).broadcast_to([P, U, NT]),
                                            ALU.is_equal).then_inc(s_eq, 1)
                    nc.vector.tensor_tensor(lo[:, b], m.iota[:].unsqueeze(1).broadcast_to([P, U, P]),
                                            m.loF[:, bass.ds(g * U, U)].unsqueeze(2).broadcast_to([P, U, P]),
                                            ALU.is_equal).then_inc(s_lo, 1)
                    dve.wait_ge(s_eq, g + 1)
                    nc.vector.tensor_tensor(hi[:, b], hi[:, b],
                                            m.wF[:, bass.ds(g * U, U)].unsqueeze(2).broadcast_to([P, U, NT]),
                                            ALU.mult).then_inc(s_hi, 1)
            dve.wait_ge(s_mm, NG + 2 + 1)
            y.chain(nc.vector.tensor_scalar(deg[:], ps[:, 0:NT], 1.0, None, ALU.add))
            y.chain(nc.vector.tensor_scalar(pos[:], deg[:], 0.0, None, ALU.is_gt))
            y.chain(nc.vector.tensor_scalar(deg[:], deg[:], 1e-30, None, ALU.max))
            dve.wait_ge(s_sd, 1)
            y.chain(nc.vector.reciprocal(sd[:], sd[:]))
            y.chain(nc.vector.tensor_tensor(m.dis[:], sd[:], pos[:], ALU.mult))

        @block.scalar
        def _(act):
            act.wait_ge(s_v, 3)
            nc.scalar.activation(sd[:], deg[:], ACT.Sqrt).then_inc(s_sd, 1)

        @block.tensor
        def _(pe):
            pe.wait_ge(s_z, 1)
            pe.sem_inc(s_mm, 2)
            nc.tensor.matmul(ps[:, 0:NT], zero[:], zero[:, 0:NT], start=True, stop=False)
            with pe.Fori(0, NG // 2) as t:
                for b in range(2):
                    pe.wait_ge(s_lo, t * 2 + b + 1)
                    pe.wait_ge(s_hi, t * 2 + b + 1)
                    hold(m, pe)
                    for u in range(U):
                        last = nc.tensor.matmul(ps[:, 0:NT], lo[:, b, u, :], hi[:, b, u, :], start=False, stop=False)
                    last.then_inc(s_mm, 1)
            nc.tensor.matmul(ps[:, 0:NT], zero[:], zero[:, 0:NT], start=False, stop=True).then_inc(s_mm, 1)


def first_rows(nc, m, x):
    B = 7
    assert NT % B == 0
    with ExitStack() as c:
        sb = lambda n, s, d=F32: c.enter_context(nc.sbuf_tensor("fr_" + n, s, d))
        sem = semaphores(nc, c, "fr_")
        xb, hb, nb = sb("x", [P, B, D]), sb("h", [P, B, D]), sb("n", [P, B, D])
        st, mv, sd, r = sb("st", [P, B, 6]), sb("mv", [P, B, 2]), sb("sd", [P, B]), sb("r", [P, B])
        s_ld, s_v, s_a, s_st, s_go = (sem(n) for n in ("ld", "v", "a", "st", "go"))
        block = c.enter_context(nc.Block())
        rows = lambda t_: t_[0:NP, 0:D].rearrange("(t p) n -> p t n", p=P)
        K = 11

        @block.sync
        def _(sp):
            with sp.Fori(0, NT // B) as t:
                sp.dma_start(xb[:], rows(x)[:, bass.ds(t * B, B), :]).then_inc(s_ld, 16)
                sp.wait_ge(s_v, t * K + K)
                sp.dma_start(rows(m.h0)[:, bass.ds(t * B, B), :], hb[:]).then_inc(s_st, 16)
                sp.dma_start(rows(m.t1)[:, bass.ds(t * B, B), :], nb[:]).then_inc(s_st, 16)
                sp.wait_ge(s_st, t * 32 + 32)
                hold(m, sp)

        @block.scalar
        def _(act):
            with act.Fori(0, NT // B) as t:
                act.wait_ge(s_v, t * K + 2)
                nc.scalar.activation(sd[:], mv[:, :, 1], ACT.Sqrt, bias=m.eps[:, 0:1]).then_inc(s_a, 1)
                act.wait_ge(s_v, t * K + 4)
                nc.scalar.activation(hb[:], hb[:], ACT.Relu).then_inc(s_a, 1)
                act.wait_ge(s_v, t * K + 6)
                nc.scalar.activation(sd[:], mv[:, :, 1], ACT.Sqrt, bias=m.eps[:, 0:1]).then_inc(s_a, 1)

        @block.vector
        def _(dve):
            y = Tally(dve, s_v)
            with dve.Fori(0, NT // B) as t:
                y.at(t * K)
                dve.wait_ge(s_ld, t * 16 + 16)
                for part in (0, 1):
                    src = (xb, hb)[part]
                    for j in range(B):
                        last = nc.vector.bn_stats(st[:, j, :], src[:, j, :])
                    y.chain(last)
                    hold(m, dve)
                    for j in range(B):
                        last = nc.vector.bn_aggr(mv[:, j, :], st[:, j, :])
                    y.chain(last)
                    dve.wait_ge(s_a, t * 3 + (1, 3)[part])
                    y.chain(nc.vector.reciprocal(r[:], sd[:]))
                    if part == 1:
                        y.chain(nc.vector.tensor_tensor(r[:], r[:], m.dis[:, bass.ds(t * B, B)], ALU.mult))
                    for j in range(B):
                        last = nc.vector.tensor_scalar((hb, nb)[part][:, j, :], src[:, j, :], mv[:, j, 0:1], r[:, j:j + 1],
                                                       ALU.subtract, ALU.mult)
                    y.chain(last)
                    if part == 0:
                        dve.wait_ge(s_a, t * 3 + 2)
                y.chain(nc.vector.tensor_tensor(nb[:], nb[:], m.row("g6").unsqueeze(1).broadcast_to([P, B, D]), ALU.mult))
                for j in range(B):
                    last = nc.vector.scalar_tensor_tensor(nb[:, j, :], m.row("c6"), m.dis[:, bass.ds(t * B + j, 1)], nb[:, j, :],
                                                          ALU.mult, ALU.add)
                y.k += 1
                assert y.k == K, y.k
                last.then_inc(s_v, 1)
                dve.wait_ge(s_v, t * K + K)
                dve.wait_ge(s_st, t * 32 + 32)


def feed_indices(nc, m, sp, g, b, cur, s_cur, s_done):
    sp.wait_ge(s_done, g + 1)
    sp.dma_start(cur[:, b, :], m.srcI[:, bass.ds(g * U, U)]).then_inc(s_cur[b], 16)


def gather_rows(nc, m, pool, cur, G, width, table, s_cur, s_g, nb):
    with pool.Fori(0, NG // nb) as t:
        for b in range(nb):
            pool.wait_ge(s_cur[b], 16 * t + 16)
            hold(m, pool)
            for u in range(U):
                pool.indirect_dma_start(G[:, b, u, 0:width], None, table,
                                        IOA(ap=cur[:, b, u:u + 1], axis=0)).then_inc(s_g[b], 16)


def store_windows(nc, m, act, d0, nwin, base, width, ps, stage, s_ohu, s_st, s_ev):
    with act.Fori(0, nwin) as i:
        act.wait_ge(s_ohu, (base + i + 2) * U)
        act.wait_ge(s_st, (base + i) * 16 + 16)
        nc.scalar.activation(stage[:, 0:width], ps[:, 0:width], ACT.Copy).then_inc(s_ev, 1)
        act.wait_ge(s_ev, base + i + 2)
        act.dma_start(m.agg[bass.ds(window_start(nc, d0, i), P), 0:width], stage[:, 0:width]).then_inc(s_st, 16)


def gcn_pass(nc, m, tag, table):
    with ExitStack() as c:
        sb = lambda n, s, d=F32: c.enter_context(nc.sbuf_tensor(tag + n, s, d))
        sem = semaphores(nc, c, tag)
        G, cur = sb("G", [P, NBG, U, D]), sb("cur", [P, NBG, U], I32)
        rel, oh = sb("rel", [P, U]), sb("oh", [P, U, P])
        S, scol, stage = sb("S", [P, P]), sb("scol", [P, 1]), sb("stage", [P, D])
        ps = c.enter_context(nc.psum_tensor(tag + "ps", [P, 512], F32))
        s_cur = [sem(f"cur{b}") for b in range(NBG)]
        s_g = [sem(f"gath{b}") for b in range(NBG)]
        s_zero, s_rel, s_oh, s_ohu, s_S, s_y, s_ev, s_st, s_done = (
            sem(n) for n in ("zero", "rel", "oh", "ohu", "S", "y", "ev", "st", "done"))
        block = c.enter_context(nc.Block())

        @block.sync
        def _(sp):
            with sp.Fori(0, NG // NBG) as t:
                for b in range(NBG):
                    feed_indices(nc, m, sp, t * NBG + b, b, cur, s_cur, s_done)

        @block.gpsimd
        def _(pool):
            nc.gpsimd.memset(S[:], 0.0)
            nc.gpsimd.memset(stage[:], 0.0).then_inc(s_zero, 1)
            gather_rows(nc, m, pool, cur, G, D, table, s_cur, s_g, NBG)

        @block.vector
        def _(dve):
            dve.wait_ge(s_zero, 1)
            dve.sem_inc(s_rel, 1)
            dve.sem_inc(s_y, 1)
            with dve.Fori(0, NG) as g:
                nwin, base = load_group(nc, m, dve, g)
                dve.wait_ge(s_rel, g + base + 1)
                nc.vector.tensor_scalar(rel[:], m.dstF[:, bass.ds(g * U, U)], m.d0rep[:, bass.ds(g, 1)],
                                        None, ALU.subtract).then_inc(s_rel, 1)
                dve.wait_ge(s_y, g + base + 1)
                nc.vector.tensor_copy(scol[:], m.rcol[:, bass.ds(g, 1)]).then_inc(s_y, 1)
                hold(m, dve)
                with dve.Fori(0, nwin) as i:
                    dve.wait_ge(s_rel, g + base + i + 2)
                    for u in range(U):
                        dve.wait_ge(s_ohu, (base + i) * U + u + 1)
                        nc.vector.tensor_scalar(oh[:, u, :], m.iota[:], rel[:, u:u + 1],
                                                m.wF[:, bass.ds(g * U + u, 1)],
                                                ALU.is_equal, ALU.mult).then_inc(s_oh, 1)
                    dve.wait_ge(s_ohu, (base + i + 1) * U)
                    dve.wait_ge(s_y, g + base + i + 2)
                    nc.vector.tensor_copy(S[:, 0:1], scol[:]).then_inc(s_S, 1)
                    dve.wait_ge(s_S, base + i + 1)
                    nc.vector.memset(scol[:], 0.0).then_inc(s_y, 1)
                    dve.wait_ge(s_oh, (base + i + 1) * U)
                    nc.vector.tensor_scalar(rel[:], rel[:], float(P), None, ALU.subtract).then_inc(s_rel, 1)

        @block.tensor
        def _(pe):
            pe.sem_inc(s_ohu, U)
            with pe.Fori(0, NG // NBG) as t:
                for b in range(NBG):
                    nwin, base = load_group(nc, m, pe, t * NBG + b)
                    pe.wait_ge(s_g[b], 16 * U * t + 16 * U)
                    hold(m, pe)
                    with pe.Fori(0, nwin) as i:
                        pe.wait_ge(s_ev, base + i + 1)
                        for u in range(U):
                            if u == U - 1:
                                pe.wait_ge(s_S, base + i + 1)
                                nc.tensor.matmul(ps[:, 0:D], S[:], stage[:], start=False, stop=False)
                            pe.wait_ge(s_oh, (base + i) * U + u + 1)
                            nc.tensor.matmul(ps[:, 0:D], oh[:, u, :], G[:, b, u, :],
                                             start=(u == 0), stop=(u == U - 1)).then_inc(s_ohu, 1)

        @block.scalar
        def _(act):
            act.sem_inc(s_ev, 1)
            act.sem_inc(s_done, NBG)
            act.sem_inc(s_st, 16)
            with act.Fori(0, NG) as g:
                d0, nwin, base = load_group(nc, m, act, g, True)
                store_windows(nc, m, act, d0, nwin, base, D, ps, stage, s_ohu, s_st, s_ev)
                act.wait_ge(s_ohu, (base + nwin + 1) * U)
                act.sem_inc(s_done, 1)
            nwin, base = load_group(nc, m, act, NG - 1)
            act.wait_ge(s_st, (base + nwin) * 16 + 16)
            hold(m, act)


def skewed(eng, body):
    for k in range(NB):
        body(k, k)
    with eng.Fori(1, NG // NB) as t:
        for b in range(NB):
            body(t * NB + b, b)
    for k in (NG, NG + 1):
        body(k, k % NB)


def softmax_pass(nc, m, tag, table, win_table, gat):
    HH = H if gat else 1
    HU = HH * U
    WW = H if gat else D + 1
    AW = AGW if gat else D + 1
    SW = HC + 1 if gat else D + 1
    MA = 1 if gat else U
    NA = 1 if gat else 2
    KA, KW = (3 if gat else 2), 3
    KC, KX = (4 if gat else 2), 3
    K1, K2, K3 = 2, 10, 2
    with ExitStack() as c:
        sb = lambda n, s, d=F32: c.enter_context(nc.sbuf_tensor(tag + n, s, d))
        sem = semaphores(nc, c, tag)
        psb = lambda n, s: c.enter_context(nc.psum_tensor(tag + n, s, F32))
        G, cur = sb("G", [P, NB, U, ROW]), sb("cur", [P, NB, U], I32)
        Gp = sb("Gp", [P, U, AGW])
        dB, ohT = sb("dB", [P, 2, GE]), sb("ohT", [P, GE])
        win = sb("win", [P, WW])
        wpos = sb("wpos", [P, 1])
        mk = sb("mk", [HU, 2, 4, P])
        L = sb("L", [P, NB, HH, U])
        Lp, p, z = (sb(n, [P, HH, U]) for n in ("Lp", "p", "z"))
        F, M = sb("F", [HU, P]), sb("M", [HU, 2, P])
        ends = sb("ends", [1, HH, U + 1])
        run = sb("run", [1, HH, U + 1])
        nf, Tf, Tl, Tm = (sb(n, [1, HH, U]) for n in ("nf", "Tf", "Tl", "Tm"))
        dif, fac = sb("dif", [1, HH]), sb("fac", [1, HH])
        junk = sb("junk", [P, D + 1])
        rel, oh = sb("rel", [P, U]), sb("oh", [P, U, P])
        S, scol, stage = sb("S", [P, HH, P]), sb("scol", [P, HH]), sb("stage", [P, AW])
        psA = psb("psA", [P, NA, 512])
        psL, psE, psM, ps = psb("psL", [HU, 512]), psb("psE", [P, 512]), psb("psM", [P, 2, 512]), psb("ps", [P, 512])
        psX = psE[0:1, 0:2 * HU]
        psY = psE[0:HU, 128:130]
        psF = lambda g: psM[:, g % 2, HU:HU + HH]
        s_cur = [sem(f"cur{b}") for b in range(NB)]
        s_g = [sem(f"gath{b}") for b in range(NB)]
        s_mk = [sem(f"mk{b}") for b in range(2)]
        s_db = [sem(f"db{b}") for b in range(2)]
        (s_zero, s_win, s_free, s_ya, s_y1, s_y2, s_y3, s_yc, s_oht, s_pa, s_pu, s_L, s_lt, s_s1, s_fl, s_s2, s_tt,
         s_s3, s_mb, s_z, s_p, s_fac, s_gp, s_oh, s_ohu, s_S, s_ev, s_st, s_done) = (sem(n) for n in (
             "zero", "win", "free", "ya", "y1", "y2", "y3", "yc", "oht", "pa", "pu", "L", "lt", "s1", "fl", "s2",
             "tt", "s3", "mb", "z", "p", "fac", "gp", "oh", "ohu", "S", "ev", "st", "done"))
        block = c.enter_context(nc.Block())
        heads = lambda t_: t_.rearrange("p u (h c) -> p u h c", h=H)
        flat = lambda t_: t_.rearrange("a h u -> a (h u)")
        uh = lambda t_: t_.rearrange("p h u -> p u h")
        mxs = lambda g: psM[:, g % 2, 0:HU].rearrange("p (h u) -> p h u", h=HH)

        @block.sync
        def _(sp):
            for b in range(LEAD):
                feed_indices(nc, m, sp, b, b, cur, s_cur, s_done)
            with sp.Fori(0, NG // NB) as t:
                for b in range(NB):
                    g = t * NB + b
                    feed_indices(nc, m, sp, g + LEAD, (b + LEAD) % NB, cur, s_cur, s_done)
                    d0, nwin, base = load_group(nc, m, sp, g, True)
                    sp.wait_ge(s_free, g + 1)
                    sp.dma_start(dB[:, b % 2, :], m.dstf[bass.ds(g * GE, GE)].partition_broadcast(P)).then_inc(s_db[b % 2], 16)
                    with sp.Fori(0, nwin) as i:
                        sp.wait_ge(s_pa, (base + i) * MA + 1)
                        hold(m, sp)
                        sp.dma_start(win[:], win_table[bass.ds(window_start(nc, d0, i), P), 0:WW]).then_inc(s_win, 16)
                    sp.wait_ge(s_s3, g + 1)
                    for h in range(HH):
                        sp.dma_start(mk[h * U:h * U + U, b % 2, :, :],
                                     m.masks[:, bass.ds(g * GE, GE)].rearrange("k (u e) -> u k e", e=P)).then_inc(s_mk[b % 2], 16)
            for b in range(LEAD):
                sp.wait_ge(s_cur[b], 16 * (NG // NB + 1))

        @block.gpsimd
        def _(pool):
            nc.gpsimd.memset(ends[:], -BIG)
            nc.gpsimd.memset(Tl[:], -BIG)
            nc.gpsimd.memset(S[:], 0.0)
            nc.gpsimd.memset(stage[:], 0.0).then_inc(s_zero, 1)
            gather_rows(nc, m, pool, cur, G, ROW, table, s_cur, s_g, NB)

        @block.vector
        def _(dve):
            ya, y1, y2, y3, yc = (Tally(dve, s_) for s_ in (s_ya, s_y1, s_y2, s_y3, s_yc))
            dve.wait_ge(s_zero, 1)
            dve.sem_inc(s_free, 2)
            dve.sem_inc(s_pu, NA)
            dve.sem_inc(s_s3, 2)

            kept = {}

            def spread(g, n, b):
                ya.at(g * KA + 2 + n * KW)
                dve.wait_ge(s_pa, n * MA + 1)
                ya.chain(nc.vector.tensor_scalar(ohT[:], dB[:, b % 2, :], wpos[:, 0:1], None, ALU.is_equal))
                dve.sem_inc(s_oht, 1)
                ya.chain(nc.vector.tensor_scalar(wpos[:], wpos[:], float(P), None, ALU.add))

            def logits(g, n, b):
                ya.at(g * KA + 4 + n * KW)
                if gat:
                    dve.wait_ge(s_pa, n + 2)
                    ya.chain(nc.vector.tensor_tensor(uh(L[:, b]), uh(L[:, b]), psA[:, 0, 0:HU].rearrange("p (u h) -> p u h", h=H), ALU.add))
                else:
                    for u in range(U):
                        dve.wait_ge(s_pa, n * U + u + 2)
                        if u:
                            dve.wait_ge(s_pu, n * U + u + NA)
                        nc.vector.tensor_tensor_reduce(out=junk[:], in0=G[:, b, u, 0:D + 1], in1=psA[:, u % NA, 0:D + 1],
                                                       scale=1.0, scalar=0.0, op0=ALU.mult, op1=ALU.add,
                                                       accum_out=Lp[:, 0, u:u + 1]).then_inc(s_pu, 1)
                    dve.wait_ge(s_pu, n * U + U + NA)
                    ya.chain(nc.vector.tensor_tensor(L[:, b], L[:, b], Lp[:], ALU.add))

            def body(k, b):
                fixed = isinstance(k, int)
                if not fixed or k < NG:
                    nwin, base = kept[b] = load_group(nc, m, dve, k)
                    dve.wait_ge(s_g[b], (k - b) * (16 * U // NB) + 16 * U)
                    ya.at(k * KA + base * KW)
                    if gat:
                        ya.chain(nc.vector.tensor_copy(uh(L[:, b]), heads(G[:, b, :, :])[:, :, :, HC]))
                    else:
                        ya.chain(nc.vector.memset(L[:, b], 0.0))
                    ya.chain(nc.vector.tensor_tensor(wpos[:], m.iotap[:], m.d0rep[:, bass.ds(k, 1)], ALU.add))
                    dve.wait_ge(s_db[b % 2], (k - b % 2) * 8 + 16)
                    spread(k, base, b)
                if not fixed or k >= 2:
                    dve.wait_ge(s_mb, k - 1)
                    nc.vector.tensor_tensor(z[:], L[:, (b - 2) % NB], mxs(b), ALU.subtract).then_inc(s_z, 1)
                if not fixed or 1 <= k <= NG:
                    g = k - 1
                    y2.at(g * K2)
                    dve.wait_ge(s_fl, g + 1)
                    dve.wait_ge(s_fac, g + 1)
                    first, last = (psX[:, j * HU:j * HU + HU].rearrange("a (h u) -> a h u", h=HH) for j in (0, 1))
                    cont = m.cont[0:1, bass.ds(g * U, U)].unsqueeze(1).broadcast_to([1, HH, U])
                    y2.chain(nc.vector.tensor_copy(ends[:, :, 1:U + 1], last))
                    y2.chain(nc.vector.tensor_tensor_scan(flat(run[:]), m.runf[0:1, bass.ds(g * H * (U + 1), HH * (U + 1))],
                                                          flat(ends[:]), -BIG, ALU.add, ALU.max))
                    y2.chain(nc.vector.tensor_tensor(nf[:], run[:, :, 0:U], cont, ALU.add))
                    y2.chain(nc.vector.tensor_tensor(nf[:], nf[:], first, ALU.max))
                    back = m.runb[0:1, bass.ds(g * H * U, HH * U)]
                    y2.chain(nc.vector.tensor_tensor_scan(flat(Tf[:])[:, ::-1], back, flat(nf[:])[:, ::-1], -BIG, ALU.add, ALU.max))
                    y2.chain(nc.vector.tensor_tensor(Tl[:, :, 0:U - 1], Tf[:, :, 1:U], cont[:, :, 1:U], ALU.add))
                    y2.chain(nc.vector.tensor_tensor(Tm[:], Tl[:], run[:, :, 1:U + 1], ALU.max))
                    y2.chain(nc.vector.tensor_tensor(dif[:], ends[:, :, 0], Tf[:, :, 0], ALU.subtract))
                    y2.chain(nc.vector.tensor_scalar(dif[:], dif[:], 0.0, None, ALU.min))
                    y2.chain(nc.vector.tensor_copy(ends[:, :, 0], run[:, :, U]))
                    dve.sem_inc(s_s2, 1)
                    assert y2.k == K2
                if not fixed or k < NG:
                    logits(k, base, b)
                    hold(m, dve)
                    with dve.If(nwin > 1):
                        with dve.Fori(1, nwin) as i:
                            spread(k, base + i, b)
                            logits(k, base + i, b)
                    ya.at(k * KA + 2 + (base + nwin) * KW)
                    if gat:
                        ya.chain(nc.vector.scalar_tensor_tensor(L[:, b], L[:, b], 0.2, L[:, b], ALU.mult, ALU.max))
                    dve.sem_inc(s_L, 1)
                    dve.sem_inc(s_free, 1)
                if not fixed or 1 <= k <= NG:
                    g, q = k - 1, (b - 1) % 2
                    y3.at(g * K3)
                    dve.wait_ge(s_tt, g + 1)
                    for j in (0, 1):
                        y3.chain(nc.vector.scalar_tensor_tensor(M[:, q, :], mk[:, q, 2 + j, :], psY[:, j:j + 1], M[:, q, :], ALU.add, ALU.max))
                    dve.sem_inc(s_s3, 1)
                if not fixed or k < NG:
                    y1.at(k * K1)
                    dve.wait_ge(s_lt, k + 1)
                    dve.wait_ge(s_mk[b % 2], (k - b % 2) * (8 * HH) + 16 * HH)
                    y1.chain(nc.vector.tensor_tensor_scan(F[:], mk[:, b % 2, 0, :], psL[:, 0:P], -BIG, ALU.add, ALU.max))
                    y1.chain(nc.vector.tensor_tensor_scan(M[:, b % 2, ::-1], mk[:, b % 2, 1, ::-1], F[:, ::-1], -BIG, ALU.add, ALU.max))
                    dve.sem_inc(s_s1, 1)
                if not fixed or k >= 2:
                    weigh(k - 2, (b - 2) % NB)

            def weigh(g, b):
                nwin, base = kept[b] if b < NB - 2 else load_group(nc, m, dve, g)
                yc.at(g * KC + base * KX)
                dve.wait_ge(s_ohu, (base + 1) * U)
                if gat:
                    yc.chain(nc.vector.tensor_tensor(Gp[:, :, H * SW:AW], uh(mxs(b)),
                                                     m.lastE[:, bass.ds(g * U, U)].unsqueeze(2).broadcast_to([P, U, H]), ALU.mult))
                    dve.wait_ge(s_p, g + 1)
                    pw = heads(Gp[:, :, 0:H * SW])
                    nc.vector.tensor_copy(pw[:, :, :, HC], uh(p[:]))
                    yc.chain(nc.vector.tensor_tensor(pw[:, :, :, 0:HC], heads(G[:, b, :, :])[:, :, :, 0:HC],
                                                     uh(p[:]).unsqueeze(3).broadcast_to([P, U, H, HC]), ALU.mult))
                    dve.sem_inc(s_gp, 1)
                yc.chain(nc.vector.tensor_scalar(scol[:], psF(b), m.rcol[:, bass.ds(g, 1)], None, ALU.mult))
                yc.chain(nc.vector.tensor_scalar(rel[:], m.dstF[:, bass.ds(g * U, U)], m.d0rep[:, bass.ds(g, 1)],
                                                 None, ALU.subtract))
                k0 = yc.k
                assert k0 == KC, k0
                if not gat:
                    dve.wait_ge(s_p, g + 1)
                hold(m, dve)
                with dve.Fori(0, nwin) as i:
                    yc.at(g * KC + k0 + (base + i) * KX)
                    for u in range(U):
                        dve.wait_ge(s_ohu, (base + i) * U + u + 1)
                        if gat:
                            nc.vector.tensor_scalar(oh[:, u, :], m.iota[:], rel[:, u:u + 1], None, ALU.is_equal).then_inc(s_oh, 1)
                        else:
                            nc.vector.tensor_scalar(oh[:, u, :], m.iota[:], rel[:, u:u + 1], p[:, 0, u:u + 1],
                                                    ALU.is_equal, ALU.mult).then_inc(s_oh, 1)
                        if u == U - 2:
                            dve.wait_ge(s_ohu, (base + i + 1) * U)
                            yc.chain(nc.vector.tensor_copy(S[:, :, 0], scol[:]))
                            dve.sem_inc(s_S, 1)
                    yc.chain(nc.vector.memset(scol[:], 0.0))
                    dve.wait_ge(s_oh, (base + i + 1) * U)
                    yc.chain(nc.vector.tensor_scalar(rel[:], rel[:], float(P), None, ALU.subtract))
                    assert yc.k == KX

            skewed(dve, body)

        @block.tensor
        def _(pe):
            pe.sem_inc(s_pa, 1)
            pe.sem_inc(s_ohu, U)

            kept = {}

            def body(k, b):
                fixed = isinstance(k, int)
                if not fixed or k < NG:
                    nwin, base = kept[b] = load_group(nc, m, pe, k)
                    with pe.Fori(0, nwin) as i:
                        pe.wait_ge(s_win, (base + i) * 16 + 16)
                        pe.wait_ge(s_oht, base + i + 1)
                        for u in range(U):
                            if gat:
                                last = nc.tensor.matmul(psA[:, 0, u * H:u * H + H], ohT[:, u * P:u * P + P], win[:], start=True, stop=True)
                            else:
                                pe.wait_ge(s_pu, (base + i) * U + u + 1)
                                nc.tensor.matmul(psA[:, u % NA, 0:WW], ohT[:, u * P:u * P + P], win[:],
                                                 start=True, stop=True).then_inc(s_pa, 1)
                        if gat:
                            last.then_inc(s_pa, 1)
                if not fixed or 1 <= k <= NG:
                    pe.wait_ge(s_s2, k)
                    hold(m, pe)
                    nc.tensor.matmul(psY[:, 0:1], flat(Tf[:]), m.ones[0:1, 0:1], start=True, stop=True)
                    nc.tensor.matmul(psY[:, 1:2], flat(Tm[:]), m.ones[0:1, 0:1], start=True, stop=True).then_inc(s_tt, 1)
                if not fixed or k < NG:
                    pe.wait_ge(s_L, k + 1)
                    hold(m, pe)
                    nc.tensor.transpose(psL[:, 0:P], L[:, b].rearrange("p h u -> p (h u)"), m.ident[:]).then_inc(s_lt, 1)
                if not fixed or 1 <= k <= NG:
                    pe.wait_ge(s_fac, k + 1)
                    nc.tensor.matmul(psF(b - 1), m.ones[0:1, :], fac[:], start=True, stop=True)
                    pe.wait_ge(s_s3, k + 2)
                    hold(m, pe)
                    q = (b - 1) % 2
                    nc.tensor.transpose(psM[:, q, 0:HU], M[:, q, :], m.ident[0:HU, 0:HU]).then_inc(s_mb, 1)
                if not fixed or k < NG:
                    pe.wait_ge(s_s1, k + 1)
                    hold(m, pe)
                    nc.tensor.matmul(psX[:, 0:HU], M[:, b % 2, 0:1], m.ident[0:HU, 0:HU], start=True, stop=True)
                    nc.tensor.matmul(psX[:, HU:2 * HU], M[:, b % 2, P - 1:P], m.ident[0:HU, 0:HU], start=True, stop=True).then_inc(s_fl, 1)
                if not fixed or k >= 2:
                    g, bc = k - 2, (b - 2) % NB
                    nwin2, base2 = kept[bc] if bc < NB - 2 else load_group(nc, m, pe, g)
                    if gat:
                        pe.wait_ge(s_gp, g + 1)
                    hold(m, pe)
                    with pe.Fori(0, nwin2) as i:
                        pe.wait_ge(s_ev, base2 + i + 1)
                        for u in range(U):
                            if u == U - 1:
                                pe.wait_ge(s_S, base2 + i + 1)
                                for h in range(HH):
                                    nc.tensor.matmul(ps[:, h * SW:h * SW + SW], S[:, h, :], stage[:, h * SW:h * SW + SW],
                                                     start=False, stop=False)
                            pe.wait_ge(s_oh, (base2 + i) * U + u + 1)
                            rhs = Gp[:, u, :] if gat else G[:, bc, u, 0:AW]
                            nc.tensor.matmul(ps[:, 0:AW], oh[:, u, :], rhs, start=(u == 0), stop=(u == U - 1)).then_inc(s_ohu, 1)

            skewed(pe, body)

        @block.scalar
        def _(act):
            act.sem_inc(s_ev, 1)
            act.sem_inc(s_done, NB)
            act.sem_inc(s_st, 16)
            act.sem_inc(s_fac, 1)

            def body(k, factors=True, sums=True):
                if factors:
                    act.wait_ge(s_s2, k)
                    nc.scalar.activation(fac[:], dif[:], ACT.Exp).then_inc(s_fac, 1)
                if sums:
                    act.wait_ge(s_z, k - 1)
                    nc.scalar.activation(p[:], z[:], ACT.Exp).then_inc(s_p, 1)
                    d0, nwin, base = load_group(nc, m, act, k - 2, True)
                    store_windows(nc, m, act, d0, nwin, base, AW, ps, stage, s_ohu, s_st, s_ev)
                    act.wait_ge(s_ohu, (base + nwin + 1) * U)
                    act.sem_inc(s_done, 1)

            body(1, sums=False)
            with act.Fori(2, NG + 1) as k:
                body(k)
            body(NG + 1, factors=False)
            nwin, base = load_group(nc, m, act, NG - 1)
            act.wait_ge(s_st, (base + nwin) * 16 + 16)
            hold(m, act)


def node_phase(nc, m, tag, body):
    with ExitStack() as c:
        sb = lambda n, s, d=F32: c.enter_context(nc.sbuf_tensor(tag + n, s, d))
        sem = semaphores(nc, c, tag)
        psb = lambda n, s: c.enter_context(nc.psum_tensor(tag + n, s, F32))
        parts = body(nc, m, sb, sem, psb)
        s = parts["s"]
        block = c.enter_context(nc.Block())

        @block.sync
        def _(sp):
            with sp.Fori(0, NT // BT) as t:
                parts["sp"](sp, t)

        @block.scalar
        def _(act):
            act.sem_inc(s.stored, parts["stores"] * 16)
            with act.Fori(0, NT // BT) as t:
                parts["act"](act, t)
            act.wait_ge(s.stored, (NT // BT + 1) * parts["stores"] * 16)

        @block.vector
        def _(dve):
            for used in s.used:
                dve.sem_inc(used, 1)
            with dve.Fori(0, NT // BT) as t:
                parts["dve"](dve, t)

        @block.tensor
        def _(pe):
            pe.sem_inc(s.out[-1], BT)
            with pe.Fori(0, NT // BT) as t:
                products(pe, t, s, parts["turn"], parts["multiply"])


def tiles(table, t, width=D):
    return table[bass.ds(t * (BT * P), BT * P), 0:width].rearrange("(b p) n -> p b n", p=P)


def products(pe, t, s, turn, multiply):
    R = len(s.out)
    for r in range(R):
        pe.wait_ge(s.ready, t * R + r + 1)
        for j in range(BT + 1):
            if j < BT:
                turn(r, j).then_inc(s.turned, 1)
            if j > 0:
                i = j - 1
                pe.wait_ge(s.copied, (t * R + r) * BT + i + 1)
                if i >= 2:
                    pe.wait_ge(s.out[r], t * BT + (BT if r == R - 1 else 0) + i - 1)
                elif i == 0 and r == 0:
                    pe.wait_ge(s.out[R - 1], t * BT + BT)
                multiply(r, i).then_inc(s.product, 1)


def node_sems(sem, rounds, loads):
    s = Shared()
    s.stored, s.chained, s.ready, s.turned, s.copied, s.product, s.result = (
        sem(n) for n in ("stored", "chained", "ready", "turned", "copied", "product", "result"))
    s.out = [sem(f"out{r}") for r in range(rounds)]
    s.loaded = [sem(f"loaded{k}") for k in range(loads)]
    s.used = [sem(f"used{k}") for k in range(loads)]
    return s


def gcn_nodes(layer):
    def body(nc, m, sb, sem, psb):
        ag, tt_, res, a, o1, o2, nb, lt = (sb(n, [P, BT, D]) for n in ("ag", "tt", "res", "a", "o1", "o2", "nb", "lt"))
        if layer == 2:
            xin, t3 = sb("xin", [P, BT, D]), sb("t3", [P, BT, AGW])
        st, mv, sd, rd = sb("st", [P, BT, 6]), sb("mv", [P, BT, 2]), sb("sd", [P, BT]), sb("rd", [P, BT])
        psT, psO = psb("psT", [P, 2, 512]), psb("psO", [P, 2, 512])
        w = m.w6 if layer == 1 else m.w7
        table, resid = (m.t1, m.h0) if layer == 1 else (m.t2, m.x1)
        bias = m.row("b6" if layer == 1 else "b7")
        rounds = [(a, w, D)] if layer == 1 else [(a, w, D), (o1, m.wp, D), (nb, m.gw, AGW)]
        R = len(rounds)
        s = node_sems(sem, R, 2)
        s.variance, s.deviation = sem("variance"), sem("deviation")
        NS = 2 if layer == 1 else 3
        KV = 10
        every = lambda row: row.unsqueeze(1).broadcast_to([P, BT, D])

        def sp_part(sp, t):
            sp.wait_ge(s.used[0], t + 1)
            hold(m, sp)
            for to, fr in ((ag, m.agg), (tt_, table)):
                sp.dma_start(to[:], tiles(fr, t)).then_inc(s.loaded[0], 16)
            sp.wait_ge(s.used[1], t + 1)
            hold(m, sp)
            for to, fr in ((res, resid),) + (((xin, m.x),) if layer == 2 else ()):
                sp.dma_start(to[:], tiles(fr, t)).then_inc(s.loaded[1], 16)

        def dve_part(dve, t):
            y = Tally(dve, s.chained)
            y.at(t * KV)
            dve.wait_ge(s.loaded[0], t * 32 + 32)
            y.chain(nc.vector.tensor_tensor(a[:], ag[:], tt_[:], ALU.add))
            dve.sem_inc(s.ready, 1)
            dve.sem_inc(s.used[0], 1)
            dve.wait_ge(s.stored, (t + 1) * (NS * 16))
            for j in range(BT):
                dve.wait_ge(s.product, t * R * BT + j + 1)
                nc.vector.scalar_tensor_tensor(o1[:, j, :], psO[:, j % 2, 0:D], m.dis[:, bass.ds(t * BT + j, 1)], bias,
                                               ALU.mult, ALU.add).then_inc(s.out[0], 1)
            dve.wait_ge(s.out[0], t * BT + BT + (BT if R == 1 else 0))
            dve.wait_ge(s.loaded[1], (t + 1) * (16 if layer == 1 else 32))
            y.chain(nc.vector.scalar_tensor_tensor(o1[:], o1[:], 0.0, res[:], ALU.max, ALU.add))
            src = o1
            if layer == 2:
                dve.sem_inc(s.ready, 1)
                for j in range(BT):
                    dve.wait_ge(s.product, t * R * BT + BT + j + 1)
                    nc.vector.tensor_tensor(o2[:, j, :], psO[:, j % 2, 0:D], m.row("bp"), ALU.add).then_inc(s.out[1], 1)
                dve.wait_ge(s.out[1], t * BT + BT)
                y.chain(nc.vector.tensor_tensor(o2[:], o2[:], xin[:], ALU.add))
                src = o2
            dve.sem_inc(s.used[1], 1)
            for j in range(BT):
                last = nc.vector.bn_stats(st[:, j, :], src[:, j, :])
            y.chain(last)
            hold(m, dve)
            for j in range(BT):
                last = nc.vector.bn_aggr(mv[:, j, :], st[:, j, :])
            y.chain(last)
            dve.sem_inc(s.variance, 1)
            dve.wait_ge(s.deviation, t + 1)
            y.chain(nc.vector.reciprocal(rd[:], sd[:]))
            if layer == 1:
                y.chain(nc.vector.tensor_tensor(rd[:], rd[:], m.dis[:, bass.ds(t * BT, BT)], ALU.mult))
            for j in range(BT):
                last = nc.vector.tensor_scalar(nb[:, j, :], src[:, j, :], mv[:, j, 0:1], rd[:, j:j + 1], ALU.subtract, ALU.mult)
            y.chain(last)
            if layer == 1:
                y.chain(nc.vector.tensor_tensor(nb[:], nb[:], every(m.row("g7")), ALU.mult))
                for j in range(BT):
                    last = nc.vector.scalar_tensor_tensor(o2[:, j, :], m.row("c7"), m.dis[:, bass.ds(t * BT + j, 1)], nb[:, j, :],
                                                          ALU.mult, ALU.add)
                y.chain(last)
                dve.sem_inc(s.result, 1)
                y.k += 1
                dve.sem_inc(s.chained, 1)
            else:
                y.chain(nc.vector.tensor_scalar(nb[:], nb[:], 0.0, None, ALU.max))
                dve.sem_inc(s.ready, 1)
                y.k += 2
                dve.sem_inc(s.chained, 2)
            assert y.k == KV, y.k

        def turn(r, j):
            for k in range(2):
                last = nc.tensor.transpose(psT[:, j % 2, k * P:k * P + P], rounds[r][0][:, j, k * P:k * P + P], m.ident[:])
            return last

        def multiply(r, j):
            _, rhs, n = rounds[r]
            for k in range(2):
                last = nc.tensor.matmul(psO[:, j % 2, 0:n], lt[:, j, k * P:k * P + P], rhs[:, k, 0:n], start=(k == 0), stop=(k == 1))
            return last

        def act_part(act, t):
            for r in range(R):
                if r == 2:
                    act.wait_ge(s.stored, (t + 1) * (NS * 16))
                    hold(m, act)
                for j in range(BT + 1):
                    if j < BT:
                        act.wait_ge(s.turned, (t * R + r) * BT + j + 1)
                        nc.scalar.activation(lt[:, j, :], psT[:, j % 2, 0:D], ACT.Copy).then_inc(s.copied, 1)
                    if r == 2 and j > 0:
                        act.wait_ge(s.product, (t * R + r) * BT + j)
                        nc.scalar.activation(t3[:, j - 1, :], psO[:, (j - 1) % 2, 0:AGW], ACT.Copy).then_inc(s.out[2], 1)
                if r == min(1, R - 1):
                    act.wait_ge(s.variance, t + 1)
                    nc.scalar.activation(sd[:], mv[:, :, 1], ACT.Sqrt, bias=m.eps[:, 0:1]).then_inc(s.deviation, 1)
            if layer == 1:
                act.wait_ge(s.result, t + 1)
                hold(m, act)
                act.dma_start(tiles(m.x1, t), o1[:]).then_inc(s.stored, 16)
                act.dma_start(tiles(m.t2, t), o2[:]).then_inc(s.stored, 16)
            else:
                act.wait_ge(s.out[2], (t + 2) * BT)
                hold(m, act)
                act.dma_start(tiles(m.xa, t), o2[:]).then_inc(s.stored, 16)
                act.dma_start(tiles(m.t3, t, ROW), t3[:, :, 0:ROW]).then_inc(s.stored, 16)
                act.dma_start(tiles(m.ad, t, H), t3[:, :, ROW:AGW]).then_inc(s.stored, 16)

        return dict(s=s, stores=NS, sp=sp_part, dve=dve_part, turn=turn, multiply=multiply, act=act_part)
    return body


def gat_nodes(nc, m, sb, sem, psb):
    ag, own, ad = sb("ag", [P, BT, AGW]), sb("own", [P, BT, ROW]), sb("ad", [P, BT, H])
    v, v2 = sb("v", [P, BT, D]), sb("v2", [P, BT, D])
    t4, lt, q = sb("t4", [P, BT, ROW]), sb("lt", [P, BT, D]), sb("q", [P, BT, D + 1])
    mx, ls, m2, ab, sm, rs = (sb(n, [P, BT, H]) for n in ("mx", "ls", "m2", "ab", "sm", "rs"))
    e = sb("e", [P, 2, BT, H])
    psT, psO = psb("psT", [P, 2, 512]), psb("psO", [P, 2, 512])
    s = node_sems(sem, 1, 1)
    s_exps, s_exp = sem("exps"), sem("exp")
    KV = 19
    hv = lambda t_: t_[:, :, 0:H * (HC + 1)].rearrange("p b (h c) -> p b h c", h=H)
    wide = lambda t_: t_[:].rearrange("p b (h c) -> p b h c", h=H)
    each = lambda t_: t_.unsqueeze(3).broadcast_to([P, BT, H, HC])
    every = lambda row: row.unsqueeze(1).broadcast_to([P, BT, D])

    def sp_part(sp, t):
        sp.wait_ge(s.used[0], t + 1)
        hold(m, sp)
        for to, fr, n in ((ag, m.agg, AGW), (own, m.t3, ROW), (ad, m.ad, H)):
            sp.dma_start(to[:], tiles(fr, t, n)).then_inc(s.loaded[0], 16)

    def dve_part(dve, t):
        y = Tally(dve, s.chained)
        y.at(t * KV)
        dve.wait_ge(s.loaded[0], t * 48 + 48)
        sums = hv(ag)[:, :, :, HC]
        y.chain(nc.vector.tensor_scalar(mx[:], sums, 0.0, -BIG, ALU.is_equal, ALU.mult))
        y.chain(nc.vector.tensor_tensor(mx[:], mx[:], ag[:, :, H * (HC + 1):AGW], ALU.add))
        y.chain(nc.vector.tensor_tensor(ls[:], hv(own)[:, :, :, HC], ad[:], ALU.add))
        y.chain(nc.vector.scalar_tensor_tensor(ls[:], ls[:], 0.2, ls[:], ALU.mult, ALU.max))
        y.chain(nc.vector.tensor_tensor(m2[:], mx[:], ls[:], ALU.max))
        y.chain(nc.vector.tensor_tensor(e[:, 0], mx[:], m2[:], ALU.subtract))
        y.chain(nc.vector.tensor_tensor(e[:, 1], ls[:], m2[:], ALU.subtract))
        dve.sem_inc(s_exps, 1)
        dve.wait_ge(s_exp, t + 1)
        y.chain(nc.vector.tensor_tensor(ab[:], sums, e[:, 0], ALU.mult))
        y.chain(nc.vector.tensor_tensor(sm[:], ab[:], e[:, 1], ALU.add))
        y.chain(nc.vector.tensor_scalar(sm[:], sm[:], 1e-16, None, ALU.add))
        y.chain(nc.vector.reciprocal(rs[:], sm[:]))
        y.chain(nc.vector.tensor_tensor(e[:], e[:], rs[:].unsqueeze(1).broadcast_to([P, 2, BT, H]), ALU.mult))
        y.chain(nc.vector.tensor_tensor(wide(v), hv(ag)[:, :, :, 0:HC], each(e[:, 0]), ALU.mult))
        y.chain(nc.vector.tensor_tensor(wide(v2), hv(own)[:, :, :, 0:HC], each(e[:, 1]), ALU.mult))
        dve.sem_inc(s.used[0], 1)
        y.chain(nc.vector.tensor_tensor(v[:], v[:], v2[:], ALU.add))
        y.chain(nc.vector.tensor_tensor(v[:], v[:], every(m.row("gat_bias")), ALU.add))
        y.chain(nc.vector.scalar_tensor_tensor(v2[:], v[:], 0.0, every(m.row("prelu1")), ALU.min, ALU.mult))
        dve.wait_ge(s.stored, (t + 1) * 32)
        y.chain(nc.vector.scalar_tensor_tensor(t4[:, :, 0:D], v[:], 0.0, v2[:], ALU.max, ALU.add))
        y.chain(nc.vector.memset(t4[:, :, D:ROW], 1.0))
        dve.sem_inc(s.ready, 1)
        assert y.k == KV, y.k

    def turn(r, j):
        for k in range(2):
            last = nc.tensor.transpose(psT[:, j % 2, k * P:k * P + P], t4[:, j, k * P:k * P + P], m.ident[:])
        return last

    def multiply(r, j):
        for k in range(2):
            nc.tensor.matmul(psO[:, j % 2, 0:D + 1], lt[:, j, k * P:k * P + P], m.wqk[:, k, :], start=(k == 0), stop=False)
        return nc.tensor.matmul(psO[:, j % 2, 0:D + 1], m.ones[0:1, :], m.bqk[:], start=False, stop=True)

    def act_part(act, t):
        act.wait_ge(s_exps, t + 1)
        nc.scalar.activation(e[:], e[:], ACT.Exp).then_inc(s_exp, 1)
        act.wait_ge(s.stored, (t + 1) * 32)
        hold(m, act)
        for j in range(BT + 1):
            if j < BT:
                act.wait_ge(s.turned, t * BT + j + 1)
                nc.scalar.activation(lt[:, j, :], psT[:, j % 2, 0:D], ACT.Copy).then_inc(s.copied, 1)
            if j > 0:
                act.wait_ge(s.product, t * BT + j)
                nc.scalar.activation(q[:, j - 1, :], psO[:, (j - 1) % 2, 0:D + 1], ACT.Copy).then_inc(s.out[0], 1)
        act.wait_ge(s.out[0], (t + 2) * BT)
        hold(m, act)
        act.dma_start(tiles(m.t4, t, ROW), t4[:]).then_inc(s.stored, 16)
        act.dma_start(tiles(m.qk, t, D + 1), q[:]).then_inc(s.stored, 16)

    return dict(s=s, stores=2, sp=sp_part, dve=dve_part, turn=turn, multiply=multiply, act=act_part)


def out_nodes(nc, m, sb, sem, psb):
    ag, t4, xa = sb("ag", [P, BT, D + 1]), sb("t4", [P, BT, ROW]), sb("xa", [P, BT, D])
    an, lt, sa, v, o = sb("an", [P, BT, D + 1]), sb("lt", [P, BT, 4, P]), sb("sa", [1, BT, P]), sb("v", [P, BT, D]), sb("o", [P, BT, D])
    rs = sb("rs", [P, BT])
    psT, psS, psO = psb("psT", [P, 2, 4, P]), psb("psS", [P, 2, 512]), psb("psO", [P, 2, 512])
    s = node_sems(sem, 1, 1)
    KV = 5

    def sp_part(sp, t):
        sp.wait_ge(s.used[0], t + 1)
        hold(m, sp)
        for to, fr, n in ((ag, m.agg, D + 1), (t4, m.t4, ROW), (xa, m.xa, D)):
            sp.dma_start(to[:], tiles(fr, t, n)).then_inc(s.loaded[0], 16)

    def dve_part(dve, t):
        y = Tally(dve, s.chained)
        y.at(t * KV)
        dve.wait_ge(s.loaded[0], t * 48 + 48)
        y.chain(nc.vector.tensor_scalar(rs[:], ag[:, :, D], 1e-16, None, ALU.add))
        y.chain(nc.vector.reciprocal(rs[:], rs[:]))
        for j in range(BT):
            last = nc.vector.tensor_scalar(an[:, j, :], ag[:, j, :], rs[:, j:j + 1], None, ALU.mult)
        y.chain(last)
        dve.sem_inc(s.ready, 1)
        dve.wait_ge(s.stored, (t + 1) * 16)
        for j in range(BT):
            dve.wait_ge(s.product, t * BT + j + 1)
            nc.vector.tensor_scalar(v[:, j, :], psO[:, j % 2, 0:D], 0.0, None, ALU.min)
            nc.vector.tensor_scalar(o[:, j, :], psO[:, j % 2, 0:D], 0.0, None, ALU.max).then_inc(s.out[0], 1)
        dve.wait_ge(s.out[0], (t + 2) * BT)
        y.chain(nc.vector.tensor_tensor(o[:], o[:], xa[:], ALU.add))
        dve.sem_inc(s.used[0], 1)
        nc.vector.tensor_tensor(v[:], v[:], m.row("prelu2").unsqueeze(1).broadcast_to([P, BT, D]), ALU.mult).then_inc(s.mult, 1)
        dve.wait_ge(s.mult, t + 1)
        y.chain(nc.vector.tensor_tensor(o[:], o[:], v[:], ALU.add))
        dve.sem_inc(s.result, 1)
        assert y.k == KV

    s.mult = sem("mult")

    def turn(r, j):
        for k, src in enumerate((an, an, t4, t4)):
            nc.tensor.transpose(psT[:, j % 2, k, :], src[:, j, (k % 2) * P:(k % 2) * P + P], m.ident[:])
        return nc.tensor.transpose(psS[0:1, j % 2, 0:P], an[:, j, D:D + 1], m.ident[:])

    def multiply(r, j):
        for k in range(4):
            nc.tensor.matmul(psO[:, j % 2, 0:D], lt[:, j, k, :], (m.wv, m.wsk)[k // 2][:, k % 2, :], start=(k == 0), stop=False)
        nc.tensor.matmul(psO[:, j % 2, 0:D], sa[:, j, :], m.bv[:], start=False, stop=False)
        return nc.tensor.matmul(psO[:, j % 2, 0:D], m.ones[0:1, :], m.bsk[:], start=False, stop=True)

    def act_part(act, t):
        for j in range(BT):
            act.wait_ge(s.turned, t * BT + j + 1)
            nc.scalar.activation(lt[:, j], psT[:, j % 2], ACT.Copy)
            nc.scalar.activation(sa[:, j, :], psS[0:1, j % 2, 0:P], ACT.Copy).then_inc(s.copied, 1)
        act.wait_ge(s.result, t + 1)
        hold(m, act)
        act.dma_start(tiles(m.out, t), o[:]).then_inc(s.stored, 16)

    return dict(s=s, stores=1, sp=sp_part, dve=dve_part, turn=turn, multiply=multiply, act=act_part)


def build(nc, a, out):
    with ExitStack() as c:
        sb = lambda n, s, d=F32: c.enter_context(nc.sbuf_tensor(n, s, d))
        m = Shared()
        m.ROWS = ("g6", "c6", "b6", "g7", "c7", "b7", "bp", "gat_bias", "prelu1", "prelu2")
        m.ident, m.ones, m.iota = sb("ident", [P, P]), sb("ones", [P, P]), sb("iota", [P, P])
        m.iotap, m.eps = sb("iotap", [P, 1]), sb("eps", [P, 1])
        m.srcI = sb("srcI", [P, NC + LEAD * U], I32)
        m.dstF, m.wF, m.lastE, m.hiF, m.loF = (sb(n, [P, NC]) for n in ("dstF", "wF", "lastE", "hiF", "loF"))
        m.d0rep, m.rcol = sb("d0rep", [P, NG]), sb("rcol", [P, NG])
        m.cont, m.runf, m.runb = sb("cont", [1, NC]), sb("runf", [1, NG * H * (U + 1)]), sb("runb", [1, NG * H * U])
        m.ctl = sb("ctl", [1, NG * 3], I32)
        m.dis = sb("dis", [P, NT])
        m.w6, m.w7, m.wp, m.wv, m.wsk = (sb(n, [P, 2, D]) for n in ("w6", "w7", "wp", "wv", "wsk"))
        m.gw, m.wqk = sb("gw", [P, 2, AGW]), sb("wqk", [P, 2, D + 1])
        m.bqk, m.bv, m.bsk = sb("bqk", [1, D + 1]), sb("bvr", [1, D]), sb("bskr", [1, D])
        m.rows = sb("rows", [P, len(m.ROWS), D])
        m.row = lambda n: m.rows[:, m.ROWS.index(n), :]
        dram = lambda n, s: nc.dram_tensor(n, s, F32, kind="Internal").ap()
        m.x, m.out = a["x"], out
        m.h0, m.x1, m.xa, m.t1, m.t2 = (dram(n, (NP, D)) for n in ("h0", "x1", "xa", "t1", "t2"))
        m.t3, m.t4 = dram("t3", (NP, ROW)), dram("t4", (NP, ROW))
        m.ad, m.qk = dram("ad", (NW, H)), dram("qk", (NW, D + 1))
        m.agg = dram("agg", (NW, AGW))
        m.masks, m.dstf = dram("masks", (4, NC * P)), dram("dstf", (NC * P,))
        m.held = {str(e.engine): c.enter_context(nc.semaphore(f"held{k}"))
                  for k, e in enumerate((nc.sync, nc.scalar, nc.vector, nc.tensor, nc.gpsimd))}
        load_all(nc, m, a)
        degrees(nc, m)
        first_rows(nc, m, a["x"])
        gcn_pass(nc, m, "g1_", m.t1)
        node_phase(nc, m, "n1_", gcn_nodes(1))
        gcn_pass(nc, m, "g2_", m.t2)
        node_phase(nc, m, "n2_", gcn_nodes(2))
        softmax_pass(nc, m, "g3_", m.t3, m.ad, True)
        node_phase(nc, m, "n3_", gat_nodes)
        softmax_pass(nc, m, "g4_", m.t4, m.qk, False)
        node_phase(nc, m, "n4_", out_nodes)


def kernel(**inputs):
    import numpy as np
    import concourse.bacc as bacc
    from concourse.bass_utils import run_bass_kernel_spmd as run
    i = {k: np.asarray(v) for k, v in inputs.items()}
    L0 = lambda n: i["L0_gnn_" + n]
    L1 = lambda n: i["L1_gnn_" + n]
    pad = NC * P - E
    dst = np.concatenate([np.full(1, -2, np.int32), i["dst"], np.full(pad + 1, -1, np.int32)])
    src = np.concatenate([i["src"], np.zeros(pad + LEAD * GE, np.int32)])
    w = np.concatenate([i["edge_weight"], np.zeros(pad, np.float32)])
    nxt = dst[2:].copy().reshape(NG, GE)
    nxt[:, -1] = -3
    cols = lambda v: np.ascontiguousarray(v.reshape(-1, P).T)
    att = np.zeros((D, 2 * H), np.float32)
    for h in range(H):
        att[h * HC:(h + 1) * HC, h] = L1("att_src")[h]
        att[h * HC:(h + 1) * HC, H + h] = L1("att_dst")[h]
    arrays = {
        "x": np.concatenate([i["x"], np.zeros((NP - N, D), np.float32)]),
        "dst_flat": dst, "src_cols": cols(src), "dst_cols": cols(dst[1:1 + NC * P]), "next_cols": cols(nxt), "w_cols": cols(w),
        "W6T": L0("W6").T, "W7T": L0("W7").T, "WpT": L0("Wp").T,
        "gat_W": L1("gat_W"), "gat_WT": L1("gat_W").T, "att": att, "WqT": L1("Wq").T,
        "WkTb": np.concatenate([L1("Wk").T, L1("bk")[:, None]], axis=1), "Wv": L1("Wv"), "Wskip": L1("Wskip"),
        "bq": L1("bq"), "bv": L1("bv"), "bskip": L1("bskip"),
        "g6": L0("ln6_g"), "c6": L0("ln6_b"), "b6": L0("b6"), "g7": L0("ln7_g"), "c7": L0("ln7_b"), "b7": L0("b7"),
        "bp": L0("bp"), "gat_bias": L1("gat_bias"), "prelu1": L1("prelu1_a"), "prelu2": L1("prelu2_a"),
    }
    nc = bacc.Bacc("TRN2", target_bir_lowering=False, num_devices=1)
    ins = {k + "_in": np.ascontiguousarray(v) for k, v in arrays.items()}
    aps = {k[:-3]: nc.dram_tensor(k, v.shape, mybir.dt.from_np(v.dtype), kind="ExternalInput").ap() for k, v in ins.items()}
    out = nc.dram_tensor("out", (NP, D), F32, kind="ExternalOutput").ap()
    build(nc, aps, out)
    return run(nc, [ins], core_ids=[0]).results[0]["out"][:N]
```
